# Optimizing a Trainium2 kernel written in Bass

```python
import numpy as np
import jax
import jax.numpy as jnp

def _softmax(x, axis=-1):
    return jax.nn.softmax(x, axis=axis)

def _gelu(x):
    return jax.nn.gelu(x, approximate=True)

def _silu(x):
    return jax.nn.silu(x)

def _sigmoid(x):
    return jax.nn.sigmoid(x)

def _layernorm(x, axis=-1, eps=1e-05):
    m = jnp.mean(x, axis=axis, keepdims=True)
    v = jnp.var(x, axis=axis, keepdims=True)
    return (x - m) / jnp.sqrt(v + eps)

def _scatter_add(tgt, idx, src, axis=0):
    return tgt.at[idx].add(src)

def _segment_sum(src, seg, n):
    return jax.ops.segment_sum(src, seg, n)
kernel_name = 'mk_xattn_ffn_d1_seqx_r4_0d354f'

def setup_inputs(seed: int=0):
    np.random.seed(seed)
    _w = jnp.asarray

    def _rec_inputs():
        import jax
        import jax.numpy as jnp
        _rk = jax.random.key(seed)
        x = -0.0002928 + 1 * jax.random.normal(jax.random.fold_in(_rk, 1), (4, 512, 256), jnp.float32)
        _lenS = 512 - jax.random.randint(jax.random.fold_in(_rk, 7), (4,), 0, max(1, 512 // 4) + 1, jnp.int32)
        _lenS2 = 512 - jax.random.randint(jax.random.fold_in(_rk, 8), (4,), 0, max(1, 512 // 4) + 1, jnp.int32)
        _ctx_1024P = jax.random.normal(jax.random.fold_in(_rk, 11), (4, 16, 256), jnp.float32)
        _ctx_1024c = jax.random.dirichlet(jax.random.fold_in(_rk, 511), 0.3 * jnp.ones((16,), jnp.float32), (4, 512))
        _ctx_1024t = jnp.einsum('bsk,bkd->bsd', _ctx_1024c, _ctx_1024P)
        _ctx_1024t = _ctx_1024t * jax.lax.rsqrt(jnp.mean(jnp.square(_ctx_1024t)) + 1e-12) * 0.953939
        ctx_1024 = -1.39393e-06 + 0.999914 * (_ctx_1024t + 0.3 * jax.random.normal(jax.random.fold_in(_rk, 611), (4, 512, 256), jnp.float32))
        _validS = jnp.arange(512)[None, :] < _lenS[:, None]
        _validS2 = jnp.arange(512)[None, :] < _lenS2[:, None]
        _causal = jnp.tril(jnp.ones((512, 512), dtype=bool))
        mask_Bx1x1xS2_ff0 = jnp.where(jnp.ones((4, 1, 1, 512), dtype=bool), 0.0, -1000000000.0).astype(jnp.float32)
        return (x, ctx_1024, mask_Bx1x1xS2_ff0)
    x, ctx_1024, mask_Bx1x1xS2_ff0 = _rec_inputs()

    def _L0_xattn_setup():
        import jax, jax.numpy as jnp
        import numpy as np
        N_HEADS, D_MODEL, D_HEAD, N_CTX = (16, 256, 64, 512)
        IGNORE = -100000.0
        key = jax.random.key(seed)
        ks = jax.random.split(key, 8)
        B, S = (2, 512)
        return {'query_input': jax.random.normal(ks[0], (B, S, D_MODEL), jnp.float32), 'key_input': jax.random.normal(ks[1], (B, S, D_MODEL), jnp.float32), 'value_input': jax.random.normal(ks[2], (B, S, D_MODEL), jnp.float32), 'additive_attention_mask': jnp.zeros((B, 1, 1, S), jnp.float32), 'W_Q': jax.random.normal(ks[3], (N_HEADS, D_MODEL, D_HEAD), jnp.float32) * 0.02, 'W_K': jax.random.normal(ks[4], (N_HEADS, D_MODEL, D_HEAD), jnp.float32) * 0.02, 'W_V': jax.random.normal(ks[5], (N_HEADS, D_MODEL, D_HEAD), jnp.float32) * 0.02, 'W_O': jax.random.normal(ks[6], (N_HEADS, D_HEAD, D_MODEL), jnp.float32) * 0.02, 'b_Q': jnp.zeros((N_HEADS, D_HEAD), jnp.float32), 'b_K': jnp.zeros((N_HEADS, D_HEAD), jnp.float32), 'b_V': jnp.zeros((N_HEADS, D_HEAD), jnp.float32), 'b_O': jnp.zeros((D_MODEL,), jnp.float32)}
    _L0_xattn_all = _L0_xattn_setup()
    _L0_xattn_in = {k: v for k, v in _L0_xattn_all.items() if k in ('W_Q', 'W_K', 'W_V', 'W_O', 'b_Q', 'b_K', 'b_V', 'b_O')}
    del _L0_xattn_all

    def _L0_ffn_setup():
        import jax, jax.numpy as jnp
        import numpy as np
        D_MODEL = 256
        EXPERT_DIM = 512
        N_EXPERTS = 8
        LN_EPS = 1e-05

        def _bit_quant(W):
            scale = jnp.clip(jnp.mean(jnp.abs(W), axis=-1, keepdims=True), 1e-05, None)
            w_q = jnp.clip(jnp.round(W / scale), -1.0, 1.0) * scale
            return W + jax.lax.stop_gradient(w_q - W)
        key = jax.random.key(seed)
        ks = jax.random.split(key, 7)
        x = jax.random.normal(ks[0], (4, 512, D_MODEL), dtype=jnp.float32)
        shared_w1 = jax.random.normal(ks[1], (EXPERT_DIM, D_MODEL), dtype=jnp.float32) / np.sqrt(EXPERT_DIM)
        shared_w2 = jax.random.normal(ks[2], (D_MODEL, EXPERT_DIM), dtype=jnp.float32) / np.sqrt(D_MODEL)
        expert_w1 = jax.random.normal(ks[3], (N_EXPERTS, EXPERT_DIM, D_MODEL), dtype=jnp.float32) / np.sqrt(EXPERT_DIM)
        expert_w2 = jax.random.normal(ks[4], (N_EXPERTS, D_MODEL, EXPERT_DIM), dtype=jnp.float32) / np.sqrt(D_MODEL)
        router_w = 0.02 * jax.random.normal(ks[5], (N_EXPERTS, D_MODEL), dtype=jnp.float32)
        ln_gamma = jnp.ones((D_MODEL,), dtype=jnp.float32)
        ln_beta = jnp.zeros((D_MODEL,), dtype=jnp.float32)
        return {'x': x, 'shared_w1': shared_w1, 'shared_w2': shared_w2, 'expert_w1': expert_w1, 'expert_w2': expert_w2, 'router_w': router_w, 'ln_gamma': ln_gamma, 'ln_beta': ln_beta}
    _L0_ffn_all = _L0_ffn_setup()
    _L0_ffn_in = {k: v for k, v in _L0_ffn_all.items() if k in ('shared_w1', 'shared_w2', 'expert_w1', 'expert_w2', 'router_w', 'ln_gamma', 'ln_beta')}
    del _L0_ffn_all
    return {'x': x, 'ctx_1024': ctx_1024, 'mask_Bx1x1xS2_ff0': mask_Bx1x1xS2_ff0, 'L0_xattn_W_Q': _L0_xattn_in['W_Q'], 'L0_xattn_W_K': _L0_xattn_in['W_K'], 'L0_xattn_W_V': _L0_xattn_in['W_V'], 'L0_xattn_W_O': _L0_xattn_in['W_O'], 'L0_xattn_b_Q': _L0_xattn_in['b_Q'], 'L0_xattn_b_K': _L0_xattn_in['b_K'], 'L0_xattn_b_V': _L0_xattn_in['b_V'], 'L0_xattn_b_O': _L0_xattn_in['b_O'], 'L0_ffn_shared_w1': _L0_ffn_in['shared_w1'], 'L0_ffn_shared_w2': _L0_ffn_in['shared_w2'], 'L0_ffn_expert_w1': _L0_ffn_in['expert_w1'], 'L0_ffn_expert_w2': _L0_ffn_in['expert_w2'], 'L0_ffn_router_w': _L0_ffn_in['router_w'], 'L0_ffn_ln_gamma': _L0_ffn_in['ln_gamma'], 'L0_ffn_ln_beta': _L0_ffn_in['ln_beta']}

def reference(x, ctx_1024, mask_Bx1x1xS2_ff0, L0_xattn_W_Q, L0_xattn_W_K, L0_xattn_W_V, L0_xattn_W_O, L0_xattn_b_Q, L0_xattn_b_K, L0_xattn_b_V, L0_xattn_b_O, L0_ffn_shared_w1, L0_ffn_shared_w2, L0_ffn_expert_w1, L0_ffn_expert_w2, L0_ffn_router_w, L0_ffn_ln_gamma, L0_ffn_ln_beta):
    import jax
    import jax.numpy as jnp

    def _L0_xattn_ref(query_input, key_input, value_input, additive_attention_mask, W_Q, W_K, W_V, W_O, b_Q, b_K, b_V, b_O):
        import jax, jax.numpy as jnp
        import numpy as np
        N_HEADS, D_MODEL, D_HEAD, N_CTX = (16, 256, 64, 512)
        IGNORE = -100000.0
        attn_scale = jnp.float32(np.sqrt(D_HEAD))
        q = jnp.einsum('bpm,hmd->bphd', query_input, W_Q) + b_Q
        k = jnp.einsum('bpm,hmd->bphd', key_input, W_K) + b_K
        v = jnp.einsum('bpm,hmd->bphd', value_input, W_V) + b_V
        attn_scores = jnp.einsum('bqhd,bkhd->bhqk', q, k) / attn_scale
        S_q, S_k = (attn_scores.shape[-2], attn_scores.shape[-1])
        causal = jnp.tril(jnp.ones((N_CTX, N_CTX), bool))[:S_q, :S_k]
        attn_scores = jnp.where(causal, attn_scores, jnp.float32(IGNORE))
        attn_scores = attn_scores + additive_attention_mask
        pattern = jax.nn.softmax(attn_scores, axis=-1)
        z = jnp.einsum('bkhd,bhqk->bqhd', v, pattern)
        out = jnp.einsum('bqhd,hdm->bqm', z, W_O) + b_O
        return out

    def _L0_ffn_ref(x, shared_w1, shared_w2, expert_w1, expert_w2, router_w, ln_gamma, ln_beta):
        import jax, jax.numpy as jnp
        import numpy as np
        D_MODEL = 256
        EXPERT_DIM = 512
        N_EXPERTS = 8
        LN_EPS = 1e-05

        def _bit_quant(W):
            scale = jnp.clip(jnp.mean(jnp.abs(W), axis=-1, keepdims=True), 1e-05, None)
            w_q = jnp.clip(jnp.round(W / scale), -1.0, 1.0) * scale
            return W + jax.lax.stop_gradient(w_q - W)
        mu = jnp.mean(x, axis=-1, keepdims=True)
        var = jnp.mean(jnp.square(x - mu), axis=-1, keepdims=True)
        h = (x - mu) / jnp.sqrt(var + LN_EPS) * ln_gamma + ln_beta
        sw1, sw2 = (_bit_quant(shared_w1), _bit_quant(shared_w2))
        shared_out = jax.nn.silu(jnp.einsum('btd,fd->btf', h, sw1)) @ sw2.T
        probs = jax.nn.softmax(h @ router_w.T, axis=-1)
        top_prob = jnp.max(probs, axis=-1)
        top_idx = jnp.argmax(probs, axis=-1)
        ew1, ew2 = (_bit_quant(expert_w1), _bit_quant(expert_w2))
        h1 = jax.nn.silu(jnp.einsum('btd,efd->ebtf', h, ew1))
        eo = jnp.einsum('ebtf,edf->ebtd', h1, ew2)
        gate = jax.nn.one_hot(top_idx, N_EXPERTS, dtype=h.dtype) * top_prob[..., None]
        routed_out = jnp.einsum('ebtd,bte->btd', eo, gate)
        return shared_out + routed_out
    x = x + _L0_xattn_ref(_layernorm(x, axis=-1), ctx_1024, ctx_1024, mask_Bx1x1xS2_ff0, L0_xattn_W_Q, L0_xattn_W_K, L0_xattn_W_V, L0_xattn_W_O, L0_xattn_b_Q, L0_xattn_b_K, L0_xattn_b_V, L0_xattn_b_O)
    x = x + _L0_ffn_ref(_layernorm(x, axis=-1), L0_ffn_shared_w1, L0_ffn_shared_w2, L0_ffn_expert_w1, L0_ffn_expert_w2, L0_ffn_router_w, L0_ffn_ln_gamma, L0_ffn_ln_beta)
    return x

_drawn_inputs = setup_inputs


def setup_inputs(seed=0):
    import zlib

    import numpy as np

    out = dict(_drawn_inputs(seed))
    spreads = {'L0_xattn_b_Q': (0.0, 0.8),
     'L0_xattn_b_K': (0.0, 0.8),
     'L0_xattn_b_V': (0.0, 0.1),
     'L0_xattn_b_O': (0.0, 0.1),
     'L0_ffn_ln_gamma': (1.0, 0.2),
     'L0_ffn_ln_beta': (0.0, 0.293)}
    factors = {'L0_xattn_W_Q': 8.0, 'L0_xattn_W_K': 8.0}
    for name, (base, spread) in spreads.items():
        noise = np.random.default_rng([zlib.crc32(name.encode()), seed]).standard_normal(out[name].shape)
        drawn = base * np.exp(spread * noise) if base else spread * noise
        out[name] = jnp.asarray(drawn.astype(out[name].dtype))
    for name, factor in factors.items():
        out[name] = (out[name] * factor).astype(out[name].dtype)
    return out
```

```python
from contextlib import ExitStack

import concourse.bass as bass
from concourse import mybir

F32 = mybir.dt.float32
F32R = mybir.dt.float32r
ALU = mybir.AluOpType
ACT = mybir.ActivationFunctionType
AX = mybir.AxisListType

P = 128
B, S, D = 4, 512, 256
T = B * S
NT = T // P
KT = D // P
H, DH = 16, 64
HP = H // 2
QT = S // P
F = 512
FT = F // P
NE = 8
EPS = 1e-5
IGNORE = -1e5
SCALE = float(DH) ** -0.5
W8 = 1.0 / SCALE
FAR = -1e30

S_OFF = [P * i * (i + 1) // 2 for i in range(QT)]
S_W = [P * (i + 1) for i in range(QT)]
S_ALL = P * QT * (QT + 1) // 2
T_UNITS = [[0], [1, 3], [2]]
T_W = [S - P * j for j in range(QT)]
T_OFF = {0: 0, 1: T_W[0], 3: T_W[0] + T_W[1], 2: T_W[0] + T_W[1] + T_W[3]}


def wait_alone(eng, s, value, passed):
    eng.wait_ge(s, value)
    eng.sem_inc(passed, 1)


def attention(nc, x, ctx_t, mask, wkqv, bqkv, ident_d, zt):
    ctx = ExitStack()
    with ctx:
        def sb(name, shape, dt=F32):
            return ctx.enter_context(nc.sbuf_tensor(name, shape, dt))

        def sem(name):
            return ctx.enter_context(nc.semaphore(name))

        xh, xl = sb("xh", [P, KT, T], F32R), sb("xl", [P, KT, T], F32R)
        ch, cl = sb("ch", [P, KT, T], F32R), sb("cl", [P, KT, T], F32R)
        xin = sb("xin", [P, 2, QT, D])
        cin = sb("cin", [P, 2, KT, S])
        ident = sb("ident", [P, P])
        maskb = sb("maskb", [P, S])
        seen = sb("seen", [P, P])
        ignore = sb("ignore", [P, P])
        madd = sb("madd", [P, B, S_ALL])
        stats = sb("stats", [P, QT, 6])
        mv = sb("mv", [P, QT, 2])
        var_eps = sb("var_eps", [P, QT])
        neg_half = sb("neg_half", [P, QT])
        rstd = sb("rstd", [P, QT])
        wraw = sb("wraw", [P, 3, KT, P])
        wh, wl = sb("wh", [P, 3, KT, P], F32R), sb("wl", [P, 3, KT, P], F32R)
        bias = sb("bias", [P, 2, 4])
        kh, kl = sb("kh", [P, 2, S], F32R), sb("kl", [P, 2, S], F32R)
        qh, ql = sb("qh", [P, 2, 2, S], F32R), sb("ql", [P, 2, 2, S], F32R)
        vv = sb("vv", [P, 2, QT, 2, 2 * DH], F32R)
        NSB = 4
        sc = sb("sc", [P, NSB, S_ALL])
        mx = sb("mx", [P, NSB, QT])
        nm = sb("nm", [P, NSB, QT])
        rs = sb("rs", [P, NSB, QT])
        rc = sb("rc", [P, NSB, QT])
        ph, pl = sb("ph", [P, 2, S_ALL], F32R), sb("pl", [P, 2, S_ALL], F32R)
        zz = sb("zz", [P, 2, S])

        sps = ctx.enter_context(nc.psum_tensor("sps", [P, 3, 512], F32))
        tps = ctx.enter_context(nc.psum_tensor("tps", [P, 2, 512], F32))
        zps = ctx.enter_context(nc.psum_tensor("zps", [P, 512], F32))
        pps = ctx.enter_context(nc.psum_tensor("pps", [P, 2, 512], F32))
        SB_ = [(0, 0), (0, P), (1, 0), (2, 0)]

        s_const = sem("s_const")
        s_xin = [sem(f"s_xin{k}") for k in range(2)]
        s_cin = [sem(f"s_cin{k}") for k in range(2)]
        s_w, s_bias = sem("s_w"), [sem("s_bias0"), sem("s_bias1")]
        s_zero = sem("s_zero")
        s_gp = sem("s_gp")
        s_bn, s_agg, s_ve, s_rstd, s_xn = (sem(n) for n in ("s_bn", "s_agg", "s_ve", "s_rstd", "s_xn"))
        s_xt, s_xh, s_xl, s_chi, s_clo = (sem(n) for n in ("s_xt", "s_xh", "s_xl", "s_chi", "s_clo"))
        s_tab = sem("s_tab")
        s_wh, s_wl = sem("s_wh"), sem("s_wl")
        s_proj, s_hi, s_lo = sem("s_proj"), sem("s_hi"), sem("s_lo")
        s_sc, s_dg, s_max, s_nm, s_exp, s_rc, s_nrm = (sem(n) for n in ("s_sc", "s_dg", "s_max", "s_nm", "s_exp", "s_rc", "s_nrm"))
        s_t, s_ph, s_pl, s_z, s_zc, s_za = (sem(n) for n in ("s_t", "s_ph", "s_pl", "s_z", "s_zc", "s_za"))
        s_zo = [sem("s_zo0"), sem("s_zo1")]
        passed = sem("passed")

        NH = 2 * B
        C = {s_w: 16, s_bias[0]: 16, s_wh: 1, s_wl: 1,
             s_proj: 3 * B, s_hi: 4 * B, s_lo: 4 * B, s_sc: 3 * NH, s_dg: 2 * NH, s_max: 4 * NH, s_nm: NH,
             s_exp: 4 * NH, s_rc: NH, s_nrm: 4 * NH, s_t: 3 * NH, s_ph: 3 * NH, s_pl: 3 * NH,
             s_z: NH, s_zc: NH, s_za: NH, s_zo[0]: 16 * B // 2, s_zo[1]: 16 * B // 2}

        def at(turn, s, k):
            return turn * C[s] + (C[s] + k)

        steps = range(-4, NH)

        block = ctx.enter_context(nc.Block())

        @block.sync
        def _(sp):
            sp.dma_start(ident[:], ident_d).then_inc(s_const, 16)
            for b in range(B):
                k = b % 2
                if b >= 2:
                    sp.wait_ge(s_xt, b - 1)
                    sp.wait_ge(s_clo, b - 1)
                sp.dma_start(xin[:, k], x[b * S:(b + 1) * S, :].rearrange("(t p) d -> p t d", p=P)).then_inc(s_xin[k], 16)
                sp.dma_start(cin[:, k], ctx_t[:, :, b * S:(b + 1) * S]).then_inc(s_cin[k], 16)
            for b in range(B):
                if b:
                    sp.wait_ge(s_tab, b)
                sp.dma_start(maskb[:], mask[b]).then_inc(s_const, 16)
                sp.wait_ge(s_const, 16 * (b + 2))
            with sp.Fori(0, HP) as hp:
                sp.wait_ge(s_wl, at(hp, s_wl, 0))
                sp.dma_start(wraw[:], wkqv[hp]).then_inc(s_w, 16)
                sp.wait_ge(s_za, at(hp, s_za, 0))
                sp.dma_start(bias[:, 0], bqkv[hp]).then_inc(s_bias[0], 16)
                for u in range(B):
                    sp.wait_ge(s_za, at(hp, s_za, 2 * u + 2))
                    sp.dma_start(zt[hp, :, u * S:(u + 1) * S], zz[:, u % 2]).then_inc(s_zo[u % 2], 16)
            for k in range(2):
                sp.wait_ge(s_zo[k], C[s_zo[k]] * (HP + 1))

        @block.gpsimd
        def _(pool):
            for s, c in C.items():
                pool.sem_inc(s, c)
            pool.memset(seen[:], 1.0).then_inc(s_gp, 1)
            pool.memset(ignore[:], 0.0).then_inc(s_gp, 1)
            pool.memset(neg_half[:], -0.5).then_inc(s_gp, 1)
            pool.wait_ge(s_gp, 3)
            pool.affine_select(out=seen[:], in_=seen[:], compare_op=ALU.is_ge, fill=0.0, base=0,
                               pattern=[[-1, P]], channel_multiplier=1).then_inc(s_gp, 1)
            pool.affine_select(out=ignore[:], in_=ignore[:], compare_op=ALU.is_ge, fill=W8 * IGNORE, base=0,
                               pattern=[[-1, P]], channel_multiplier=1).then_inc(s_gp, 1)
            for b in range(B):
                k = b % 2
                pool.wait_ge(s_ve, b + 1)
                pool.tensor_tensor(rstd[:], var_eps[:], neg_half[:], ALU.pow).then_inc(s_rstd, 1)
                pool.wait_ge(s_chi, b + 1)
                pool.tensor_tensor(cl[:, :, b * S:(b + 1) * S], cin[:, k], ch[:, :, b * S:(b + 1) * S].bitcast(F32),
                                   ALU.subtract).then_inc(s_clo, 1)
            for b in range(B):
                pool.wait_ge(s_const, 16 * (b + 2))
                for i in range(QT):
                    pool.tensor_scalar(madd[:, b, S_OFF[i]:S_OFF[i] + S_W[i]], maskb[:, 0:S_W[i]], W8, None,
                                       ALU.mult).then_inc(s_gp, 1)
                pool.wait_ge(s_gp, 5 + 8 * b + 4)
                for i in range(QT):
                    dg = madd[:, b, S_OFF[i] + P * i:S_OFF[i] + P * (i + 1)]
                    pool.tensor_tensor(dg, dg, ignore[:], ALU.add).then_inc(s_gp, 1)
                pool.wait_ge(s_gp, 5 + 8 * b + 8)
                pool.sem_inc(s_tab, 1)
            with pool.Fori(0, HP) as hp:
                def nrm(n):
                    wait_alone(pool, s_rc, at(hp, s_rc, n + 1), passed)
                    for i in range(QT):
                        e = sc[:, n % NSB, S_OFF[i]:S_OFF[i] + S_W[i]]
                        pool.tensor_scalar(e, e, rc[:, n % NSB, i:i + 1], None, ALU.mult).then_inc(s_nrm, 1)
                pool.wait_ge(s_w, at(hp, s_w, 16))
                wait_alone(pool, s_proj, at(hp, s_proj, 0), passed)
                pool.tensor_copy(wh[:], wraw[:]).then_inc(s_wh, 1)
                pool.wait_ge(s_wh, at(hp, s_wh, 1))
                pool.tensor_tensor(wl[:], wraw[:], wh[:].bitcast(F32), ALU.subtract).then_inc(s_wl, 1)
                for k in steps:
                    if 0 <= k + 1 < NH:
                        nrm(k + 1)

        @block.tensor
        def _(pe):
            pe.wait_ge(s_const, 16)
            for b in range(B):
                pe.wait_ge(s_xn, 4 * (b + 1))
                if b:
                    pe.wait_ge(s_xl, b)
                for kt in range(KT):
                    for t in range(QT):
                        last = pe.transpose(pps[:, kt, t * P:(t + 1) * P], xin[:, b % 2, t, kt * P:(kt + 1) * P], ident[:])
                last.then_inc(s_xt, 1)
            pe.wait_ge(s_xl, B)
            pe.wait_ge(s_clo, B)
            pe.wait_ge(s_zero, 8)
            with pe.Fori(0, HP) as hp:
                def project(u, which):
                    n = 3 * u + which
                    before = n - 2
                    done = {0: 1, 1: 3, 2: 4}
                    if before >= 0:
                        pe.wait_ge(s_lo, at(hp, s_lo, 4 * (before // 3) + done[before % 3]))
                    else:
                        pe.wait_ge(s_lo, at(hp, s_lo, 0))
                    dst = pps[:, n % 2, :]
                    cols = slice(u * S, (u + 1) * S)
                    if which < 2:
                        a, al = (ch, cl) if which == 0 else (xh, xl)
                        g = 0
                        for kt in range(KT):
                            for w_, a_ in ((wh, a), (wh, al), (wl, a)):
                                last = pe.matmul(dst, w_[:, which, kt, :], a_[:, kt, cols], start=(g == 0), stop=(g == 5))
                                g += 1
                    else:
                        for t in range(QT):
                            g = 0
                            tc_ = slice(u * S + t * P, u * S + (t + 1) * P)
                            for kt in range(KT):
                                for w_, a_ in ((wh, ch), (wl, ch), (wh, cl)):
                                    last = pe.matmul(dst[:, t * P:(t + 1) * P], a_[:, kt, tc_], w_[:, 2, kt, :],
                                                     start=(g == 0), stop=(g == 5))
                                    g += 1
                    last.then_inc(s_proj, 1)

                def scores(n):
                    u, s = n // 2, n % 2
                    pe.wait_ge(s_lo, at(hp, s_lo, 4 * u + 3))
                    for i in range(QT):
                        bank, col = SB_[i]
                        if i != 1:
                            left = 4 * (n - 1) + (2, 2, 3, 4)[i]
                            pe.wait_ge(s_max, at(hp, s_max, max(left, 0)))
                        dst = sps[:, bank, col:col + S_W[i]]
                        qs = slice(i * P, (i + 1) * P)
                        for g, (a, k_) in enumerate(((qh, kh), (qh, kl), (ql, kh))):
                            last = pe.matmul(dst, a[:, u % 2, s, qs], k_[:, u % 2, 0:S_W[i]], start=(g == 0), stop=(g == 2))
                        if i != 0:
                            last.then_inc(s_sc, 1)

                def turn_probs(n):
                    pe.wait_ge(s_nrm, at(hp, s_nrm, 4 * n + 4))
                    for m, unit in enumerate(T_UNITS):
                        g = 3 * n + m
                        pe.wait_ge(s_pl, at(hp, s_pl, max(g - 1, 0)))
                        col = 0
                        for j in unit:
                            for i in range(j, QT):
                                last = pe.transpose(tps[:, g % 2, col:col + P],
                                                    sc[:, n % NSB, S_OFF[i] + j * P:S_OFF[i] + (j + 1) * P], ident[:])
                                col += P
                        last.then_inc(s_t, 1)

                def values(n):
                    u, s = n // 2, n % 2
                    pe.wait_ge(s_za, at(hp, s_za, max(n, 0)))
                    if s == 0:
                        pe.wait_ge(s_lo, at(hp, s_lo, 4 * u + 4))
                    pe.wait_ge(s_pl, at(hp, s_pl, 3 * n + 3))
                    for g, (j, p_) in enumerate((j, p_) for j in range(QT) for p_ in (ph, pl)):
                        last = pe.matmul(zps[:, j * P:S], vv[:, u % 2, j, s, :], p_[:, n % 2, T_OFF[j]:T_OFF[j] + T_W[j]],
                                         start=(g == 0), stop=(g == 7))
                    last.then_inc(s_z, 1)

                pe.wait_ge(s_wl, at(hp, s_wl, 1))
                for k in steps:
                    if k >= 0:
                        turn_probs(k)
                    if 0 <= k + 2 < NH:
                        scores(k + 2)
                    if k >= 0:
                        values(k)
                    u, odd = (k + 4) // 2, (k + 4) % 2
                    if u < B:
                        if odd:
                            project(u, 2)
                        else:
                            project(u, 0)
                            project(u, 1)

        @block.scalar
        def _(act):
            for b in range(B):
                cols = slice(b * S, (b + 1) * S)
                act.wait_ge(s_cin[b % 2], 16 * (b // 2 + 1))
                act.activation(ch[:, :, cols], cin[:, b % 2], ACT.Copy).then_inc(s_chi, 1)
                act.wait_ge(s_xt, b + 1)
                act.activation(xh[:, :, cols], pps[:, :, :], ACT.Copy).then_inc(s_xh, 1)
            with act.Fori(0, HP) as hp:
                def high(u, which):
                    n = 3 * u + which
                    act.wait_ge(s_proj, at(hp, s_proj, n + 1))
                    src = pps[:, n % 2, :]
                    if which == 0:
                        act.wait_ge(s_sc, at(hp, s_sc, max(3 * (2 * u - 2), 0)))
                        act.activation(kh[:, u % 2, :], src, ACT.Identity, bias=bias[:, 0, 1:2]).then_inc(s_hi, 1)
                    elif which == 1:
                        for s in range(2):
                            rows = slice(s * DH, (s + 1) * DH)
                            act.activation(qh[rows, u % 2, s, :], src[rows, :], ACT.Identity,
                                           bias=bias[rows, 0, 0:1]).then_inc(s_hi, 1)
                    else:
                        act.wait_ge(s_z, at(hp, s_z, max(2 * u - 2, 0)))
                        act.activation(vv[:, u % 2, :, :, 0:DH], src.rearrange("p (t s d) -> p t s d", t=QT, s=2),
                                       ACT.Copy).then_inc(s_hi, 1)

                def exps(n):
                    act.wait_ge(s_nm, at(hp, s_nm, n + 1))
                    for i in range(QT):
                        e = sc[:, n % NSB, S_OFF[i]:S_OFF[i] + S_W[i]]
                        act.activation(e, e, ACT.Exp, bias=nm[:, n % NSB, i:i + 1], scale=SCALE,
                                       accum_out=rs[:, n % NSB, i:i + 1]).then_inc(s_exp, 1)

                def probs_high(n):
                    act.wait_ge(s_z, at(hp, s_z, max(n - 1, 0)))
                    for m, unit in enumerate(T_UNITS):
                        g = 3 * n + m
                        act.wait_ge(s_t, at(hp, s_t, g + 1))
                        w = sum(T_W[j] for j in unit)
                        o = T_OFF[unit[0]]
                        act.activation(ph[:, n % 2, o:o + w], tps[:, g % 2, 0:w], ACT.Copy).then_inc(s_ph, 1)

                def z_copy(n):
                    u, s = n // 2, n % 2
                    rows = slice(s * DH, (s + 1) * DH)
                    act.wait_ge(s_z, at(hp, s_z, n + 1))
                    if s == 0:
                        act.wait_ge(s_zo[u % 2], at(hp, s_zo[u % 2], max(16 * (u // 2), 0)))
                    act.activation(zz[rows, u % 2, :], zps[0:DH, :], ACT.Identity, bias=bias[rows, 0, 2:3]).then_inc(s_zc, 1)

                act.wait_ge(s_bias[0], at(hp, s_bias[0], 16))
                for k in steps:
                    if k >= 0:
                        probs_high(k)
                    if 0 <= k + 2 < NH:
                        exps(k + 2)
                    if k >= 0:
                        z_copy(k)
                    u, odd = (k + 4) // 2, (k + 4) % 2
                    if u < B:
                        if odd:
                            high(u, 2)
                        else:
                            high(u, 0)
                            high(u, 1)

        @block.vector
        def _(dve):
            for buf in (qh, ql):
                for k in range(2):
                    dve.memset(buf[DH:P, k, 0, :].bitcast(F32), 0.0).then_inc(s_zero, 1)
                    dve.memset(buf[0:DH, k, 1, :].bitcast(F32), 0.0).then_inc(s_zero, 1)
            for b in range(B):
                dve.wait_ge(s_xin[b % 2], 16 * (b // 2 + 1))
                for t in range(QT):
                    dve.bn_stats(stats[:, t, :], xin[:, b % 2, t, :]).then_inc(s_bn, 1)
                dve.wait_ge(s_bn, 4 * (b + 1))
                for t in range(QT):
                    dve.bn_aggr(mv[:, t, :], stats[:, t, :]).then_inc(s_agg, 1)
                dve.wait_ge(s_agg, 4 * (b + 1))
                dve.tensor_scalar(var_eps[:], mv[:, :, 1], EPS, None, ALU.add).then_inc(s_ve, 1)
                dve.wait_ge(s_rstd, b + 1)
                for t in range(QT):
                    dve.tensor_scalar(xin[:, b % 2, t, :], xin[:, b % 2, t, :], mv[:, t, 0:1], rstd[:, t:t + 1],
                                      ALU.subtract, ALU.mult).then_inc(s_xn, 1)
                dve.wait_ge(s_xh, b + 1)
                cols = slice(b * S, (b + 1) * S)
                dve.tensor_tensor(xl[:, :, cols], pps[:, :, :], xh[:, :, cols].bitcast(F32), ALU.subtract).then_inc(s_xl, 1)
            dve.wait_ge(s_tab, B)
            with dve.Fori(0, HP) as hp:
                def low(u, which):
                    n = 3 * u + which
                    src = pps[:, n % 2, :]
                    if which == 0:
                        dve.wait_ge(s_hi, at(hp, s_hi, 4 * u + 1))
                        dve.scalar_tensor_tensor(out=kl[:, u % 2, :], in0=src, scalar=bias[:, 0, 1:2],
                                                 in1=kh[:, u % 2, :].bitcast(F32), op0=ALU.add, op1=ALU.subtract).then_inc(s_lo, 1)
                    elif which == 1:
                        dve.wait_ge(s_hi, at(hp, s_hi, 4 * u + 3))
                        for s in range(2):
                            rows = slice(s * DH, (s + 1) * DH)
                            dve.scalar_tensor_tensor(out=ql[rows, u % 2, s, :], in0=src[rows, :], scalar=bias[rows, 0, 0:1],
                                                     in1=qh[rows, u % 2, s, :].bitcast(F32), op0=ALU.add,
                                                     op1=ALU.subtract).then_inc(s_lo, 1)
                    else:
                        dve.wait_ge(s_hi, at(hp, s_hi, 4 * u + 4))
                        dve.tensor_tensor(vv[:, u % 2, :, :, DH:2 * DH], src.rearrange("p (t s d) -> p t s d", t=QT, s=2),
                                          vv[:, u % 2, :, :, 0:DH].bitcast(F32), ALU.subtract).then_inc(s_lo, 1)

                def masked_max(n):
                    u = n // 2
                    dve.wait_ge(s_t, at(hp, s_t, max(3 * (n - NSB + 1), 0)))
                    dve.wait_ge(s_sc, at(hp, s_sc, 3 * n + 1))
                    dg = sps[:, 0, 0:2 * 256].rearrange("p (a c) -> p a c", a=2)[:, :, 0:P]
                    sb2 = seen[:].rearrange("p (a c) -> p a c", a=1).to_broadcast([P, 2, P])
                    dve.tensor_tensor(dg, dg, sb2, ALU.mult).then_inc(s_dg, 1)
                    wait_alone(dve, s_dg, at(hp, s_dg, 2 * n + 1), passed)
                    for i in range(QT):
                        if i == 2:
                            dve.wait_ge(s_sc, at(hp, s_sc, 3 * n + 3))
                            dg = sps[:, 1:3, :].rearrange("p a c -> p (a c)")[:, 256:256 + 640 + P]
                            dg = bass.AP(dg.tensor, dg.offset, [list(dg.ap[0]), [640, 2], [1, P]])
                            dve.tensor_tensor(dg, dg, sb2, ALU.mult).then_inc(s_dg, 1)
                            wait_alone(dve, s_dg, at(hp, s_dg, 2 * n + 2), passed)
                        bank, col = SB_[i]
                        dve.tensor_tensor_reduce(out=sc[:, n % NSB, S_OFF[i]:S_OFF[i] + S_W[i]],
                                                 in0=sps[:, bank, col:col + S_W[i]],
                                                 in1=madd[:, u, S_OFF[i]:S_OFF[i] + S_W[i]],
                                                 scale=1.0, scalar=-3.0e38, op0=ALU.add, op1=ALU.max,
                                                 accum_out=mx[:, n % NSB, i:i + 1]).then_inc(s_max, 1)
                    dve.wait_ge(s_max, at(hp, s_max, 4 * n + 4))
                    dve.tensor_scalar(nm[:, n % NSB, :], mx[:, n % NSB, :], -SCALE, None, ALU.mult).then_inc(s_nm, 1)

                def recip(n):
                    dve.wait_ge(s_exp, at(hp, s_exp, 4 * n + 4))
                    dve.reciprocal(rc[:, n % NSB, :], rs[:, n % NSB, :]).then_inc(s_rc, 1)

                def probs_low(n):
                    for m, unit in enumerate(T_UNITS):
                        g = 3 * n + m
                        dve.wait_ge(s_ph, at(hp, s_ph, g + 1))
                        w = sum(T_W[j] for j in unit)
                        o = T_OFF[unit[0]]
                        dve.tensor_tensor(pl[:, n % 2, o:o + w], tps[:, g % 2, 0:w], ph[:, n % 2, o:o + w].bitcast(F32),
                                          ALU.subtract).then_inc(s_pl, 1)

                def z_add(n):
                    u, s = n // 2, n % 2
                    rows = slice(s * DH, (s + 1) * DH)
                    dve.wait_ge(s_zc, at(hp, s_zc, n + 1))
                    dve.tensor_tensor(zz[rows, u % 2, :], zps[DH:P, :], zz[rows, u % 2, :], ALU.add).then_inc(s_za, 1)

                for k in steps:
                    if 0 <= k + 1 < NH:
                        recip(k + 1)
                    if k >= 0:
                        probs_low(k)
                    if 0 <= k + 2 < NH:
                        masked_max(k + 2)
                    if k >= 0:
                        z_add(k)
                    u, odd = (k + 4) // 2, (k + 4) % 2
                    if u < B:
                        if odd:
                            low(u, 2)
                        else:
                            low(u, 0)
                            low(u, 1)


def experts(nc, ap, zt, out):
    with ExitStack() as ctx:
        x2 = ctx.enter_context(nc.sbuf_tensor("x2", [P, B, QT, D], F32))
        ht = ctx.enter_context(nc.sbuf_tensor("ht", [P, KT, T], F32))
        gate = ctx.enter_context(nc.sbuf_tensor("gate", [P, B, QT, NE + 1], F32))
        router(nc, ap, zt, x2, ht, gate)
        expert_loop(nc, ap, x2, ht, gate, out)


def router(nc, ap, zt, x2, ht, gate):
    ctx = ExitStack()
    with ctx:
        def sb(name, shape, dt=F32):
            return ctx.enter_context(nc.sbuf_tensor(name, shape, dt))

        def sem(name):
            return ctx.enter_context(nc.semaphore(name))

        ident = sb("ident2", [P, P])
        wo = sb("wo", [P, HP, D])
        rows = sb("rows", [P, 3, D])
        wr = sb("wr", [P, KT, NE])
        zs = sb("zs", [P, 2, HP, P])
        xg = sb("xg", [P, QT, D])
        hg = sb("hg", [P, QT, D])
        hs = sb("hs", [P, KT, S])
        stats = sb("stats2", [P, QT, 6])
        mv = sb("mv2", [P, QT, 2])
        ve = sb("ve2", [P, QT])
        rstd = sb("rstd2", [P, QT])
        neg_half = sb("neg_half2", [P, QT])
        iota = sb("iota", [P, QT, NE])
        small = sb("small", [P, 6, QT, NE])
        tiny = sb("tiny", [P, 6, QT])
        ops = ctx.enter_context(nc.psum_tensor("ops", [P, 2, 512], F32))
        hps = ctx.enter_context(nc.psum_tensor("hps", [P, 2, 512], F32))
        rps = ctx.enter_context(nc.psum_tensor("rps", [P, QT, NE], F32))

        r_in, r_gp, r_x = sem("r_in"), sem("r_gp"), sem("r_x")
        r_z = [sem("r_z0"), sem("r_z1")]
        r_o, r_dve, r_ve, r_pow, r_ht, r_hc, r_hd, r_log, r_e, r_ez = (sem(n) for n in (
            "r_o", "r_dve", "r_ve", "r_pow", "r_ht", "r_hc", "r_hd", "r_log", "r_e", "r_ez"))
        r_res, r_h, r_passed = sem("r_res"), sem("r_h"), sem("r_passed")
        NLINK = 38
        C = {r_x: 16, r_z[0]: 32, r_z[1]: 32, r_o: 4, r_dve: NLINK, r_ve: 2, r_pow: 2, r_ht: 1, r_hc: 1, r_hd: 1,
             r_log: 1, r_e: 1, r_ez: 1, r_res: 4, r_h: 1}

        def at(turn, s, k):
            return turn * C[s] + (C[s] + k)

        block = ctx.enter_context(nc.Block())

        @block.sync
        def _(sp):
            for d, s in ((ident, "ident"), (wo, "wo"), (rows, "rows"), (wr, "wr")):
                sp.dma_start(d[:], ap[s]).then_inc(r_in, 16)
            with sp.Fori(0, B) as b:
                sp.wait_ge(r_h, at(b, r_h, 0))
                sp.dma_start(xg[:], ap["x"].rearrange("(b t p) d -> b p t d", b=B, p=P)[b]).then_inc(r_x, 16)
                zv = zt.rearrange("h p (b t q) -> b t p h q", b=B, q=P)
                for t in range(QT):
                    sp.wait_ge(r_o, at(b, r_o, max(t - 1, 0)))
                    sp.dma_start(zs[:, t % 2], zv[b, t]).then_inc(r_z[t % 2], 16)

        @block.gpsimd
        def _(pool):
            for s, c in C.items():
                pool.sem_inc(s, c)
            pool.memset(neg_half[:], -0.5).then_inc(r_gp, 1)
            for e in range(NE):
                pool.memset(iota[:, :, e:e + 1], float(e)).then_inc(r_gp, 1)
            for b in range(B):
                pool.memset(gate[:, b, :, 0:1], 1.0).then_inc(r_gp, 1)
            with pool.Fori(0, B) as b:
                for k in range(2):
                    pool.wait_ge(r_ve, at(b, r_ve, k + 1))
                    pool.tensor_tensor(rstd[:], ve[:], neg_half[:], ALU.pow).then_inc(r_pow, 1)

        @block.tensor
        def _(pe):
            pe.wait_ge(r_in, 64)
            with pe.Fori(0, B) as b:
                for t in range(QT):
                    pe.wait_ge(r_z[t % 2], at(b, r_z[t % 2], 16 * (t // 2 + 1)))
                    pe.wait_ge(r_res, at(b, r_res, max(t - 1, 0)))
                    for h in range(HP):
                        last = pe.matmul(ops[:, t % 2, 0:D], zs[:, t % 2, h, :], wo[:, h, :], start=(h == 0), stop=(h == HP - 1))
                    last.then_inc(r_o, 1)
                pe.wait_ge(r_h, at(b, r_h, 1))
                pe.wait_ge(r_hc, at(b, r_hc, 0))
                for kt in range(KT):
                    for t in range(QT):
                        last = pe.transpose(hps[:, kt, t * P:(t + 1) * P], hg[:, t, kt * P:(kt + 1) * P], ident[:])
                last.then_inc(r_ht, 1)
                pe.wait_ge(r_hc, at(b, r_hc, 1))
                pe.wait_ge(r_ez, at(b, r_ez, 0))
                for t in range(QT):
                    for kt in range(KT):
                        last = pe.matmul(rps[:, t, :], hs[:, kt, t * P:(t + 1) * P], wr[:, kt, :], start=(kt == 0), stop=(kt == 1))
                last.then_inc(r_log, 1)

        @block.scalar
        def _(act):
            with act.Fori(0, B) as b:
                act.wait_ge(r_ht, at(b, r_ht, 1))
                act.wait_ge(r_log, at(b, r_log, 0))
                act.activation(hs[:], hps[:], ACT.Copy).then_inc(r_hc, 1)
                act.wait_ge(r_hc, at(b, r_hc, 1))
                act.activation(ht[:].rearrange("p k (b n) -> p k b n", b=B)[:, :, b, :], hs[:], ACT.Copy).then_inc(r_hd, 1)
                act.wait_ge(r_e, at(b, r_e, 1))
                act.activation(small[:, 1], small[:, 0], ACT.Exp).then_inc(r_ez, 1)

        @block.vector
        def _(dve):
            dve.wait_ge(r_in, 64)
            dve.wait_ge(r_gp, 1 + NE + B)
            with dve.Fori(0, B) as b:
                count = [0]

                def link(ins):
                    count[0] += 1
                    ins.then_inc(r_dve, 1)
                    dve.wait_ge(r_dve, at(b, r_dve, count[0]))

                def row(k):
                    return rows[:, k:k + 1, :].to_broadcast([P, QT, D])

                def norm(src, dst, k):
                    for t in range(QT):
                        link(dve.bn_stats(stats[:, t, :], src[:, t, :]))
                    dve.sem_inc(r_passed, 1)
                    for t in range(QT):
                        link(dve.bn_aggr(mv[:, t, :], stats[:, t, :]))
                        dve.sem_inc(r_passed, 1)
                    dve.tensor_scalar(ve[:], mv[:, :, 1], EPS, None, ALU.add).then_inc(r_ve, 1)
                    dve.wait_ge(r_pow, at(b, r_pow, k + 1))
                    for t in range(QT):
                        link(dve.tensor_scalar(dst[:, t, :], src[:, t, :], mv[:, t, 0:1], rstd[:, t:t + 1],
                                               ALU.subtract, ALU.mult))

                dve.wait_ge(r_x, at(b, r_x, 16))
                for t in range(QT):
                    dve.wait_ge(r_o, at(b, r_o, t + 1))
                    dve.tensor_tensor(xg[:, t, :], ops[:, t % 2, 0:D], xg[:, t, :], ALU.add).then_inc(r_res, 1)
                dve.wait_ge(r_res, at(b, r_res, QT))
                link(dve.tensor_tensor(xg[:], xg[:], row(0), ALU.add))
                link(dve.tensor_copy(x2[:, b], xg[:]))
                norm(xg, hg, 0)
                norm(hg, hg, 1)
                link(dve.tensor_tensor(hg[:], hg[:], row(1), ALU.mult))
                dve.tensor_tensor(hg[:], hg[:], row(2), ALU.add).then_inc(r_h, 1)
                m, e, eq, cand, hot = (small[:, n] for n in range(5))
                mx, em, es, ix, pr = (tiny[:, n] for n in range(5))

                def wide(v):
                    return v.rearrange("p (t o) -> p t o", o=1).to_broadcast([P, QT, NE])
                dve.wait_ge(r_log, at(b, r_log, 1))
                link(dve.tensor_reduce(mx, rps[:], AX.X, ALU.max))
                dve.tensor_tensor(m, rps[:], wide(mx), ALU.subtract).then_inc(r_e, 1)
                dve.wait_ge(r_ez, at(b, r_ez, 1))
                link(dve.tensor_reduce(em, e, AX.X, ALU.max))
                link(dve.tensor_reduce(es, e, AX.X, ALU.add))
                link(dve.reciprocal(pr, es))
                link(dve.tensor_tensor(pr, pr, em, ALU.mult))
                link(dve.tensor_tensor(eq, e, wide(em), ALU.is_lt))
                link(dve.tensor_scalar(eq, eq, float(NE), None, ALU.mult))
                link(dve.tensor_tensor(cand, iota[:], eq, ALU.add))
                link(dve.tensor_reduce(ix, cand, AX.X, ALU.min))
                link(dve.tensor_tensor(hot, iota[:], wide(ix), ALU.is_equal))
                link(dve.tensor_tensor(gate[:, b, :, 1:NE + 1], hot, wide(pr), ALU.mult))
                pad = NLINK - count[0]
                assert pad == 0, (count[0])


def expert_loop(nc, ap, x2, ht, gate, out):
    ctx = ExitStack()
    with ctx:
        def sb(name, shape, dt=F32):
            return ctx.enter_context(nc.sbuf_tensor(name, shape, dt))

        def sem(name):
            return ctx.enter_context(nc.semaphore(name))

        w1, w2 = sb("w1r", [P, KT, F]), sb("w2r", [P, FT, D])
        a1, a2 = sb("a1", [P, KT, F]), sb("a2", [P, FT, D])
        t1, t2 = sb("t1", [P, KT, F]), sb("t2", [P, FT, D])
        half = sb("half", [P, 2, F])
        s2b = sb("s2b", [P, D])
        s1c = sb("s1c", [P, FT])
        ones = sb("ones", [P, P])
        g = sb("g", [P, 2, FT, S])
        y = sb("y", [P, 2, D])
        sps = ctx.enter_context(nc.psum_tensor("sps3", [P, 2, 512], F32))
        fps = ctx.enter_context(nc.psum_tensor("fps", [P, 4, 512], F32))
        yps = ctx.enter_context(nc.psum_tensor("yps", [P, 2, 512], F32))
        e_w, e_one, e_dve, e_abs, e_sum, e_t, e_f, e_g, e_y, e_acc, e_out = (sem(n) for n in (
            "e_w", "e_one", "e_dve", "e_abs", "e_sum", "e_t", "e_f", "e_g", "e_y", "e_acc", "e_out"))
        e_ym = sem("e_ym")
        C = {e_w: 32, e_dve: 9, e_abs: 2, e_sum: 1, e_t: 1, e_f: 16, e_g: 16, e_y: 16, e_ym: 16, e_acc: 16}

        def at(turn, s, k):
            return turn * C[s] + (C[s] + k)

        block = ctx.enter_context(nc.Block())

        @block.sync
        def _(sp):
            with sp.Fori(0, NE + 1) as e:
                sp.wait_ge(e_t, at(e, e_t, 0))
                sp.dma_start(w1[:], ap["w1"][e]).then_inc(e_w, 16)
                sp.dma_start(w2[:], ap["w2"][e]).then_inc(e_w, 16)
            sp.wait_ge(e_acc, 16 * (NE + 2))
            sp.dma_start(out.rearrange("(b t p) d -> p b t d", b=B, p=P), x2[:]).then_inc(e_out, 16)
            sp.wait_ge(e_out, 16)

        @block.gpsimd
        def _(pool):
            for s, c in C.items():
                pool.sem_inc(s, c)
            pool.memset(ones[:], 1.0).then_inc(e_one, 1)

        @block.tensor
        def _(pe):
            pe.wait_ge(e_one, 1)
            with pe.Fori(0, NE + 1) as e:
                pe.wait_ge(e_abs, at(e, e_abs, 2))
                for kt in range(KT):
                    pe.matmul(sps[:, 0, :], ones[:], a1[:, kt, :], start=(kt == 0), stop=(kt == KT - 1))
                for j in range(FT):
                    pe.matmul(sps[:, 1, 0:D], ones[:], a2[:, j, :], start=(j == 0), stop=(j == FT - 1))
                for j in range(FT):
                    for kt in range(KT):
                        last = pe.matmul(sps[:, 1, D + j:D + j + 1], a1[:, kt, j * P:(j + 1) * P], ones[:, 0:1],
                                         start=(kt == 0), stop=(kt == KT - 1))
                last.then_inc(e_sum, 1)
                pe.wait_ge(e_t, at(e, e_t, 1))
                for c in range(B):
                    for j in range(FT):
                        pe.wait_ge(e_g, at(e, e_g, max(4 * c + j - 3, 0)))
                        for kt in range(KT):
                            last = pe.matmul(fps[:, j, :], t1[:, kt, j * P:(j + 1) * P], ht[:, kt, c * S:(c + 1) * S],
                                             start=(kt == 0), stop=(kt == KT - 1))
                        last.then_inc(e_f, 1)
                    pe.wait_ge(e_g, at(e, e_g, 4 * c + 4))
                    for t in range(QT):
                        n = 4 * c + t
                        pe.wait_ge(e_ym, at(e, e_ym, max(n - 1, 0)))
                        for j in range(FT):
                            last = pe.matmul(yps[:, n % 2, 0:D], g[:, c % 2, j, t * P:(t + 1) * P], t2[:, j, :],
                                             start=(j == 0), stop=(j == FT - 1))
                        last.then_inc(e_y, 1)

        @block.scalar
        def _(act):
            with act.Fori(0, NE + 1) as e:
                for c in range(B):
                    act.wait_ge(e_y, at(e, e_y, max(4 * (c - 1), 0)))
                    for j in range(FT):
                        act.wait_ge(e_f, at(e, e_f, 4 * c + j + 1))
                        act.activation(g[:, c % 2, j, :], fps[:, j, :], ACT.Silu, scale=s1c[:, j:j + 1]).then_inc(e_g, 1)

        @block.vector
        def _(dve):
            with dve.Fori(0, NE + 1) as e:
                count = [0]

                def link(ins):
                    count[0] += 1
                    ins.then_inc(e_dve, 1)
                    dve.wait_ge(e_dve, at(e, e_dve, count[0]))

                dve.wait_ge(e_w, at(e, e_w, 32))
                dve.wait_ge(e_acc, at(e, e_acc, 0))
                dve.scalar_tensor_tensor(out=a1[:], in0=w1[:], scalar=-1.0, in1=w1[:], op0=ALU.mult, op1=ALU.max).then_inc(e_abs, 1)
                dve.scalar_tensor_tensor(out=a2[:], in0=w2[:], scalar=-1.0, in1=w2[:], op0=ALU.mult, op1=ALU.max).then_inc(e_abs, 1)
                dve.wait_ge(e_sum, at(e, e_sum, 1))
                link(dve.tensor_scalar(half[:, 0, :], sps[:, 0, :], 0.5 / D, 0.5e-5, ALU.mult, ALU.max))
                link(dve.tensor_scalar(half[:, 1, 0:D], sps[:, 1, 0:D], 0.5 / F, 0.5e-5, ALU.mult, ALU.max))
                link(dve.tensor_scalar(s2b[:], sps[:, 1, 0:D], 1.0 / F, 1e-5, ALU.mult, ALU.max))
                link(dve.tensor_scalar(s1c[:], sps[:, 1, D:D + FT], 1.0 / D, 1e-5, ALU.mult, ALU.max))
                hb1 = half[:, 0:1, :].to_broadcast([P, KT, F])
                hb2 = half[:, 1:2, 0:D].to_broadcast([P, FT, D])
                link(dve.tensor_tensor(t1[:], w1[:], hb1, ALU.is_gt))
                link(dve.scalar_tensor_tensor(out=a1[:], in0=w1[:], scalar=-1.0, in1=hb1, op0=ALU.mult, op1=ALU.is_gt))
                link(dve.tensor_tensor(t1[:], t1[:], a1[:], ALU.subtract))
                link(dve.tensor_tensor(t2[:], w2[:], hb2, ALU.is_gt))
                link(dve.scalar_tensor_tensor(out=a2[:], in0=w2[:], scalar=-1.0, in1=hb2, op0=ALU.mult, op1=ALU.is_gt))
                dve.tensor_tensor(t2[:], t2[:], a2[:], ALU.subtract).then_inc(e_t, 1)
                for n in range(NT):
                    c, t = n // QT, n % QT
                    dve.wait_ge(e_y, at(e, e_y, n + 1))
                    if n >= 2:
                        dve.wait_ge(e_acc, at(e, e_acc, n - 1))
                    dve.scalar_tensor_tensor(out=y[:, n % 2, :], in0=yps[:, n % 2, 0:D], scalar=gate[:, c, t, bass.ds(e, 1)],
                                             in1=s2b[:], op0=ALU.mult, op1=ALU.mult).then_inc(e_ym, 1)
                    dve.wait_ge(e_ym, at(e, e_ym, n + 1))
                    dve.tensor_tensor(x2[:, c, t, :], x2[:, c, t, :], y[:, n % 2, :], ALU.add).then_inc(e_acc, 1)


def kernel(**inputs):
    import numpy as _np
    import concourse.bacc as _bacc
    from concourse import mybir as _mybir
    from concourse.bass_utils import run_bass_kernel_spmd as _run

    a = {k: _np.asarray(v) for k, v in inputs.items()}
    c = _np.ascontiguousarray
    wkqv = _np.stack([a[f"L0_xattn_W_{n}"] for n in "KQV"])
    wkqv = wkqv.reshape(3, HP, 2, KT, P, DH).transpose(1, 4, 0, 3, 2, 5)
    bqkv = _np.stack([a[f"L0_xattn_b_{n}"] for n in "QKVV"]).reshape(4, HP, P).transpose(1, 2, 0)
    ffn = "L0_ffn_"
    arrays = {
        "x": c(a["x"].reshape(T, D)),
        "ctx_t": c(a["ctx_1024"].reshape(T, KT, P).transpose(2, 1, 0)),
        "mask": c(_np.broadcast_to(a["mask_Bx1x1xS2_ff0"].reshape(B, 1, S), (B, P, S))),
        "wkqv": c(wkqv.reshape(HP, P, 3, KT, P)),
        "bqkv": c(bqkv),
        "ident": _np.eye(P, dtype=_np.float32),
        "wo": c(a["L0_xattn_W_O"].reshape(HP, P, D).transpose(1, 0, 2)),
        "rows": c(_np.broadcast_to(_np.stack([a["L0_xattn_b_O"], a[ffn + "ln_gamma"], a[ffn + "ln_beta"]]), (P, 3, D))),
        "w1": c(_np.concatenate([a[ffn + "shared_w1"][None], a[ffn + "expert_w1"]]).reshape(NE + 1, F, KT, P).transpose(0, 3, 2, 1)),
        "w2": c(_np.concatenate([a[ffn + "shared_w2"][None], a[ffn + "expert_w2"]]).reshape(NE + 1, D, FT, P).transpose(0, 3, 2, 1)),
        "wr": c(a[ffn + "router_w"].reshape(NE, KT, P).transpose(2, 1, 0)),
    }
    nc = _bacc.Bacc("TRN2", target_bir_lowering=False, num_devices=1)
    ap = {n: nc.dram_tensor(f"in_{n}", v.shape, _mybir.dt.from_np(v.dtype), kind="ExternalInput").ap() for n, v in arrays.items()}
    out = nc.dram_tensor("out", (T, D), _mybir.dt.float32, kind="ExternalOutput").ap()
    zt = nc.dram_tensor("zt", (HP, P, T), _mybir.dt.float32, kind="Internal").ap()
    attention(nc, ap["x"], ap["ctx_t"], ap["mask"], ap["wkqv"], ap["bqkv"], ap["ident"], zt)
    experts(nc, ap, zt, out)
    r = _run(nc, [{f"in_{n}": v for n, v in arrays.items()}], core_ids=[0])
    return _np.asarray(r.results[0]["out"]).reshape(B, S, D)
```

```python
from contextlib import ExitStack

import concourse.bass as bass
from concourse import mybir

F32 = mybir.dt.float32
F32R = mybir.dt.float32r
U32 = mybir.dt.uint32
I32 = mybir.dt.int32
ALU = mybir.AluOpType
ACT = mybir.ActivationFunctionType
AX = mybir.AxisListType

P = 128
B, S, D = 4, 512, 256
T = B * S
NT = T // P
KT = D // P
H, DH = 16, 64
HP = H // 2
QT = S // P
F = 512
FT = F // P
NE = 8
EPS = 1e-5
IGNORE = -1e5
SCALE = float(DH) ** -0.5
W8 = 1.0 / SCALE
FAR = -1e30

S_OFF = [P * i * (i + 1) // 2 for i in range(QT)]
S_W = [P * (i + 1) for i in range(QT)]
S_ALL = P * QT * (QT + 1) // 2
T_UNITS = [[0], [1, 3], [2]]
T_W = [S - P * j for j in range(QT)]
T_OFF = {0: 0, 1: T_W[0], 3: T_W[0] + T_W[1], 2: T_W[0] + T_W[1] + T_W[3]}


def wait_alone(eng, s, value, passed):
    eng.wait_ge(s, value)
    eng.sem_inc(passed, 1)


def attention(nc, x, ctx_t, mask, wkqv, bkq_d, ident_d, zt):
    ctx = ExitStack()
    with ctx:
        def sb(name, shape, dt=F32):
            return ctx.enter_context(nc.sbuf_tensor(name, shape, dt))

        def sem(name):
            return ctx.enter_context(nc.semaphore(name))

        xh, xl = sb("xh", [P, KT, T], F32R), sb("xl", [P, KT, T], F32R)
        ch, cl = sb("ch", [P, KT, T], F32R), sb("cl", [P, KT, T], F32R)
        xin = sb("xin", [P, 2, QT, D])
        cin = sb("cin", [P, 2, KT, S])
        ident = sb("ident", [P, P])
        maskb = sb("maskb", [P, S])
        seen = sb("seen", [P, P])
        ignore = sb("ignore", [P, P])
        madd = sb("madd", [P, B, S_ALL])
        stats = sb("stats", [P, QT, 6])
        mv = sb("mv", [P, QT, 2])
        var_eps = sb("var_eps", [P, QT])
        neg_half = sb("neg_half", [P, QT])
        rstd = sb("rstd", [P, QT])
        wraw = sb("wraw", [P, 3, KT, P])
        wh, wl = sb("wh", [P, 3, KT, P], F32R), sb("wl", [P, 3, KT, P], F32R)
        bias = sb("bias", [P, HP, 2])
        bkq = sb("bkq", [P, 2])
        kh, kl = sb("kh", [P, 2, S], F32R), sb("kl", [P, 2, S], F32R)
        qh, ql = sb("qh", [P, 2, 2, S], F32R), sb("ql", [P, 2, 2, S], F32R)
        vv = sb("vv", [P, 2, QT, 2, 2 * DH], F32R)
        NSB = 4
        sc = sb("sc", [P, NSB, S_ALL])
        mx = sb("mx", [P, NSB, QT])
        nm = sb("nm", [P, NSB, QT])
        rs = sb("rs", [P, NSB, QT])
        rc = sb("rc", [P, NSB, QT])
        ph, pl = sb("ph", [P, 2, S_ALL], F32R), sb("pl", [P, 2, S_ALL], F32R)
        zz = sb("zz", [P, 2, S])

        sps = ctx.enter_context(nc.psum_tensor("sps", [P, 3, 512], F32))
        tps = ctx.enter_context(nc.psum_tensor("tps", [P, 2, 512], F32))
        zps = ctx.enter_context(nc.psum_tensor("zps", [P, 512], F32))
        pps = ctx.enter_context(nc.psum_tensor("pps", [P, 2, 512], F32))
        SB_ = [(0, 0), (0, P), (1, 0), (2, 0)]

        s_const = sem("s_const")
        s_xin = [sem(f"s_xin{k}") for k in range(2)]
        s_cin = [sem(f"s_cin{k}") for k in range(2)]
        s_zero, s_gp, s_tab, passed = sem("s_zero"), sem("s_gp"), sem("s_tab"), sem("passed")
        s_bn, s_agg, s_ve, s_rstd, s_xn = (sem(n) for n in ("s_bn", "s_agg", "s_ve", "s_rstd", "s_xn"))
        s_xt, s_xh, s_xl, s_chi, s_clo = (sem(n) for n in ("s_xt", "s_xh", "s_xl", "s_chi", "s_clo"))
        s_wkq, s_wv, s_skq, s_sv = (sem(n) for n in ("s_wkq", "s_wv", "s_skq", "s_sv"))
        s_proj, s_hi, s_lo = sem("s_proj"), sem("s_hi"), sem("s_lo")
        s_sc, s_dg, s_max, s_nm, s_exp, s_rc, s_nrm = (sem(n) for n in ("s_sc", "s_dg", "s_max", "s_nm", "s_exp", "s_rc", "s_nrm"))
        s_t, s_ph, s_pl, s_z, s_zc, s_za = (sem(n) for n in ("s_t", "s_ph", "s_pl", "s_z", "s_zc", "s_za"))
        s_zo = [sem("s_zo0"), sem("s_zo1")]

        NH = 2 * B
        C = {s_wkq: 16, s_wv: 16, s_skq: 3, s_sv: 2, s_proj: 3 * B, s_hi: 4 * B, s_lo: 4 * B,
             s_sc: 3 * NH, s_dg: 2 * NH, s_max: 4 * NH, s_nm: NH, s_exp: 4 * NH, s_rc: NH, s_nrm: 4 * NH,
             s_t: 3 * NH, s_ph: 3 * NH, s_pl: 3 * NH, s_z: NH, s_zc: NH, s_za: NH,
             s_zo[0]: 16 * B // 2, s_zo[1]: 16 * B // 2}

        def at(turn, s, k):
            return turn * C[s] + (C[s] + k)

        K_, Q_, V_ = 0, 1, 2
        AHEAD = 4

        def unit(which, u):
            return 3 * (u - 1) if which == V_ else 3 * (u - 3) + 1 + which

        def split(index, last=False):
            if last and index > unit(V_, 2):
                return split(unit(V_, 2)) + (index >= unit(V_, 3))
            return 4 * (index // 3) + (1, 2, 4)[index % 3] + (index < unit(V_, -1))

        def projected(index, last=False):
            if last and index > unit(V_, 2):
                return projected(unit(V_, 2)) + (index >= unit(V_, 3))
            return index + 1 + (index < unit(V_, -1))

        START = dict(C)
        START[s_proj] += unit(K_, 0) + 1
        START[s_hi] += 4 * (unit(K_, 0) // 3) + 1 + 1
        START[s_lo] = START[s_hi]

        def step_projections(k, last):
            found = [(K_, (k + 5) // 2), (Q_, (k + 5) // 2)] if k % 2 else [(V_, (k + 2) // 2)]
            return [(w, u) for w, u in found if 0 <= u < (B if last else B + 3)]

        def schedule(eng, step):
            for k in range(-5, 0):
                step(0, k, False)
            with eng.Fori(0, HP - 1) as hp:
                for k in range(NH):
                    step(hp, k, False)
            for k in range(NH):
                step(HP - 1, k, True)

        def head(n, last):
            return 0 <= n < (NH if last else NH + AHEAD)

        block = ctx.enter_context(nc.Block())

        @block.sync
        def _(sp):
            sp.dma_start(ident[:], ident_d).then_inc(s_const, 16)
            sp.dma_start(bias[:], bkq_d).then_inc(s_const, 16)
            for b in range(B):
                k = b % 2
                if b >= 2:
                    sp.wait_ge(s_xt, b - 1)
                    sp.wait_ge(s_clo, b - 1)
                sp.dma_start(xin[:, k], x[b * S:(b + 1) * S, :].rearrange("(t p) d -> p t d", p=P)).then_inc(s_xin[k], 16)
                sp.dma_start(cin[:, k], ctx_t[:, :, b * S:(b + 1) * S]).then_inc(s_cin[k], 16)
                if b == 0:
                    sp.dma_start(wraw[:, 0:2], wkqv[0, :, 0:2]).then_inc(s_wkq, 16)
                    sp.dma_start(wraw[:, 2], wkqv[0, :, 2]).then_inc(s_wv, 16)
            for b in range(B):
                if b:
                    sp.wait_ge(s_tab, b)
                sp.dma_start(maskb[:], mask[b]).then_inc(s_const, 16)
                sp.wait_ge(s_const, 16 * (b + 3))

            def turn(hp, last):
                if not last:
                    sp.wait_ge(s_skq, at(hp, s_skq, C[s_skq]))
                    sp.dma_start(wraw[:, 0:2], wkqv[hp + 1, :, 0:2]).then_inc(s_wkq, 16)
                    sp.wait_ge(s_sv, at(hp, s_sv, C[s_sv]))
                    sp.dma_start(wraw[:, 2], wkqv[hp + 1, :, 2]).then_inc(s_wv, 16)
                for u in range(B):
                    sp.wait_ge(s_za, at(hp, s_za, 2 * u + 2))
                    sp.dma_start(zt[hp, :, u * S:(u + 1) * S], zz[:, u % 2]).then_inc(s_zo[u % 2], 16)

            with sp.Fori(0, HP - 1) as hp:
                turn(hp, False)
            turn(HP - 1, True)
            for k in range(2):
                sp.wait_ge(s_zo[k], C[s_zo[k]] * (HP + 1))

        @block.gpsimd
        def _(pool):
            for s in C:
                pool.sem_inc(s, START[s])
            pool.memset(seen[:], 1.0).then_inc(s_gp, 1)
            pool.memset(ignore[:], 0.0).then_inc(s_gp, 1)
            pool.memset(neg_half[:], -0.5).then_inc(s_gp, 1)
            pool.wait_ge(s_gp, 3)
            pool.affine_select(out=seen[:], in_=seen[:], compare_op=ALU.is_ge, fill=0.0, base=0,
                               pattern=[[-1, P]], channel_multiplier=1).then_inc(s_gp, 1)
            pool.affine_select(out=ignore[:], in_=ignore[:], compare_op=ALU.is_ge, fill=W8 * IGNORE, base=0,
                               pattern=[[-1, P]], channel_multiplier=1).then_inc(s_gp, 1)
            for b in range(B):
                k = b % 2
                pool.wait_ge(s_ve, b + 1)
                pool.tensor_tensor(rstd[:], var_eps[:], neg_half[:], ALU.pow).then_inc(s_rstd, 1)
                pool.wait_ge(s_chi, b + 1)
                pool.tensor_tensor(cl[:, :, b * S:(b + 1) * S], cin[:, k], ch[:, :, b * S:(b + 1) * S].bitcast(F32),
                                   ALU.subtract).then_inc(s_clo, 1)

            def split_kq(turn, version):
                wait_alone(pool, s_wkq, at(turn, s_wkq, 16 * (version + 1)), passed)
                if version:
                    wait_alone(pool, s_lo, at(turn, s_lo, split(unit(Q_, B - 1))), passed)
                pool.tensor_copy(bkq[:], bias[:, turn + version, 0:2]).then_inc(s_skq, 1)
                pool.tensor_copy(wh[:, 0:2], wraw[:, 0:2]).then_inc(s_skq, 1)
                pool.wait_ge(s_skq, at(turn, s_skq, C[s_skq] * version + 2))
                pool.tensor_tensor(wl[:, 0:2], wraw[:, 0:2], wh[:, 0:2].bitcast(F32), ALU.subtract).then_inc(s_skq, 1)

            def split_v(turn, version):
                wait_alone(pool, s_wv, at(turn, s_wv, 16 * (version + 1)), passed)
                if version:
                    wait_alone(pool, s_proj, at(turn, s_proj, projected(unit(V_, B - 1))), passed)
                pool.tensor_copy(wh[:, 2], wraw[:, 2]).then_inc(s_sv, 1)
                pool.wait_ge(s_sv, at(turn, s_sv, C[s_sv] * version + 1))
                pool.tensor_tensor(wl[:, 2], wraw[:, 2], wh[:, 2].bitcast(F32), ALU.subtract).then_inc(s_sv, 1)

            pool.wait_ge(s_const, 32)
            split_kq(0, 0)
            split_v(0, 0)
            for b in range(B):
                pool.wait_ge(s_const, 16 * (b + 3))
                for i in range(QT):
                    pool.tensor_scalar(madd[:, b, S_OFF[i]:S_OFF[i] + S_W[i]], maskb[:, 0:S_W[i]], W8, None,
                                       ALU.mult).then_inc(s_gp, 1)
                pool.wait_ge(s_gp, 5 + 8 * b + 4)
                for i in range(QT):
                    dg = madd[:, b, S_OFF[i] + P * i:S_OFF[i] + P * (i + 1)]
                    pool.tensor_tensor(dg, dg, ignore[:], ALU.add).then_inc(s_gp, 1)
                pool.wait_ge(s_gp, 5 + 8 * b + 8)
                pool.sem_inc(s_tab, 1)

            def step(turn, k, last_turn):
                if head(k + 2, last_turn):
                    n = k + 2
                    wait_alone(pool, s_rc, at(turn, s_rc, n + 1), passed)
                    for i in range(QT):
                        e = sc[:, n % NSB, S_OFF[i]:S_OFF[i] + S_W[i]]
                        pool.tensor_tensor(e, e, rc[:, n % NSB, i:i + 1].to_broadcast([P, S_W[i]]), ALU.mult).then_inc(s_nrm, 1)
                if not last_turn:
                    if k == 1:
                        split_kq(turn, 1)
                    if k == 4:
                        split_v(turn, 1)

            schedule(pool, step)

        @block.tensor
        def _(pe):
            pe.wait_ge(s_const, 32)
            for b in range(B):
                pe.wait_ge(s_xn, 4 * (b + 1))
                if b:
                    pe.wait_ge(s_xl, b)
                for kt in range(KT):
                    for t in range(QT):
                        last = pe.transpose(pps[:, kt, t * P:(t + 1) * P], xin[:, b % 2, t, kt * P:(kt + 1) * P], ident[:])
                last.then_inc(s_xt, 1)
            pe.wait_ge(s_xl, B)
            pe.wait_ge(s_clo, B)
            pe.wait_ge(s_zero, 8)

            def project(turn, which, u, last_turn, between=None):
                n = unit(which, u)
                if which == K_ and u in (0, B):
                    pe.wait_ge(s_skq, at(turn, s_skq, C[s_skq] * (u // B + 1)))
                if which == V_ and u in (0, B):
                    pe.wait_ge(s_sv, at(turn, s_sv, C[s_sv] * (u // B + 1)))
                if n >= unit(K_, 1):
                    pe.wait_ge(s_lo, at(turn, s_lo, split(n - 2, last_turn)))
                dst = pps[:, n % 2, :]
                u %= B
                if which == V_:
                    for t in range(QT):
                        if t == QT // 2 and between:
                            between()
                        tokens = slice(u * S + t * P, u * S + (t + 1) * P)
                        terms = [(a_[:, kt, tokens], w_[:, V_, kt, :]) for kt in range(KT)
                                 for a_, w_ in ((ch, wh), (ch, wl), (cl, wh))]
                        for g, (a_, w_) in enumerate(terms):
                            last = pe.matmul(dst[:, t * P:(t + 1) * P], a_, w_, start=(g == 0), stop=(g == len(terms) - 1))
                else:
                    high_in, low_in = (ch, cl) if which == K_ else (xh, xl)
                    tokens = slice(u * S, (u + 1) * S)
                    terms = [(w_[:, which, kt, :], a_[:, kt, tokens]) for kt in range(KT)
                             for w_, a_ in ((wh, high_in), (wh, low_in), (wl, high_in))]
                    for g, (w_, a_) in enumerate(terms):
                        last = pe.matmul(dst, w_, a_, start=(g == 0), stop=(g == len(terms) - 1))
                last.then_inc(s_proj, 1)

            def scores(turn, n):
                u, s = n // 2, n % 2
                if s == 0:
                    pe.wait_ge(s_lo, at(turn, s_lo, split(unit(Q_, u))))
                for i in range(QT):
                    bank, col = SB_[i]
                    if i != 1:
                        pe.wait_ge(s_max, at(turn, s_max, 4 * (n - 1) + (2, 2, 3, 4)[i]))
                    dst = sps[:, bank, col:col + S_W[i]]
                    queries = slice(i * P, (i + 1) * P)
                    terms = ((qh, kh), (qh, kl), (ql, kh))
                    for g, (q_, k_) in enumerate(terms):
                        last = pe.matmul(dst, q_[:, u % 2, s, queries], k_[:, u % 2, 0:S_W[i]],
                                         start=(g == 0), stop=(g == len(terms) - 1))
                    if i != 0:
                        last.then_inc(s_sc, 1)

            def turn_probs(turn, n, units):
                if 0 in units:
                    pe.wait_ge(s_nrm, at(turn, s_nrm, 4 * n + 4))
                for m in units:
                    tiles = T_UNITS[m]
                    g = 3 * n + m
                    pe.wait_ge(s_pl, at(turn, s_pl, g - 1))
                    col = 0
                    for j in tiles:
                        for i in range(j, QT):
                            last = pe.transpose(tps[:, g % 2, col:col + P],
                                                sc[:, n % NSB, S_OFF[i] + j * P:S_OFF[i] + (j + 1) * P], ident[:])
                            col += P
                    last.then_inc(s_t, 1)

            def values(turn, n, last_turn):
                u, s = n // 2, n % 2
                pe.wait_ge(s_za, at(turn, s_za, n))
                if s == 0:
                    pe.wait_ge(s_lo, at(turn, s_lo, split(unit(V_, u), last_turn)))
                pe.wait_ge(s_pl, at(turn, s_pl, 3 * n + 3))
                terms = [(j, p_) for j in range(QT) for p_ in (ph, pl)]
                for g, (j, p_) in enumerate(terms):
                    last = pe.matmul(zps[:, j * P:S], vv[:, u % 2, j, s, :], p_[:, n % 2, T_OFF[j]:T_OFF[j] + T_W[j]],
                                     start=(g == 0), stop=(g == len(terms) - 1))
                last.then_inc(s_z, 1)

            def step(turn, k, last_turn):
                def rest():
                    if k >= 0:
                        turn_probs(turn, k, (2,))

                if k >= 0:
                    turn_probs(turn, k, (0, 1))
                found = step_projections(k, last_turn)
                for which, u in found:
                    if which == Q_:
                        rest()
                    project(turn, which, u, last_turn, rest)
                if not found:
                    rest()
                if k >= 0:
                    values(turn, k, last_turn)
                if head(k + AHEAD, last_turn):
                    scores(turn, k + AHEAD)

            schedule(pe, step)

        @block.scalar
        def _(act):
            for b in range(B):
                cols = slice(b * S, (b + 1) * S)
                act.wait_ge(s_cin[b % 2], 16 * (b // 2 + 1))
                act.activation(ch[:, :, cols], cin[:, b % 2], ACT.Copy).then_inc(s_chi, 1)
                act.wait_ge(s_xt, b + 1)
                act.activation(xh[:, :, cols], pps[:, :, :], ACT.Copy).then_inc(s_xh, 1)

            def high(turn, which, u, last_turn):
                n = unit(which, u)
                act.wait_ge(s_proj, at(turn, s_proj, projected(n, last_turn)))
                src = pps[:, n % 2, :]
                if which == K_:
                    act.wait_ge(s_sc, at(turn, s_sc, 3 * (2 * u - 2)))
                    act.activation(kh[:, u % 2, :], src, ACT.Identity, bias=bkq[:, K_:K_ + 1]).then_inc(s_hi, 1)
                elif which == Q_:
                    for s in range(2):
                        rows = slice(s * DH, (s + 1) * DH)
                        act.activation(qh[rows, u % 2, s, :], src[rows, :], ACT.Identity,
                                       bias=bkq[rows, Q_:Q_ + 1]).then_inc(s_hi, 1)
                else:
                    act.wait_ge(s_z, at(turn, s_z, 2 * u - 2))
                    act.activation(vv[:, u % 2, :, :, 0:DH], src.rearrange("p (t s d) -> p t s d", t=QT, s=2),
                                   ACT.Copy).then_inc(s_hi, 1)

            def exps(turn, n):
                act.wait_ge(s_nm, at(turn, s_nm, n + 1))
                for i in range(QT):
                    e = sc[:, n % NSB, S_OFF[i]:S_OFF[i] + S_W[i]]
                    act.activation(e, e, ACT.Exp, bias=nm[:, n % NSB, i:i + 1], scale=SCALE,
                                   accum_out=rs[:, n % NSB, i:i + 1]).then_inc(s_exp, 1)

            def probs_high(turn, n):
                act.wait_ge(s_z, at(turn, s_z, n - 1))
                for m, tiles in enumerate(T_UNITS):
                    g = 3 * n + m
                    act.wait_ge(s_t, at(turn, s_t, g + 1))
                    w, o = sum(T_W[j] for j in tiles), T_OFF[tiles[0]]
                    act.activation(ph[:, n % 2, o:o + w], tps[:, g % 2, 0:w], ACT.Copy).then_inc(s_ph, 1)

            def z_copy(turn, n):
                u, s = n // 2, n % 2
                rows = slice(s * DH, (s + 1) * DH)
                act.wait_ge(s_z, at(turn, s_z, n + 1))
                if s == 0:
                    act.wait_ge(s_zo[u % 2], at(turn, s_zo[u % 2], 16 * (u // 2)))
                act.activation(zz[rows, u % 2, :], zps[0:DH, :], ACT.Copy).then_inc(s_zc, 1)

            def step(turn, k, last_turn):
                if k >= 0:
                    probs_high(turn, k)
                if head(k + 2, last_turn):
                    exps(turn, k + 2)
                for which, u in step_projections(k, last_turn):
                    high(turn, which, u, last_turn)
                if k >= 0:
                    z_copy(turn, k)

            schedule(act, step)

        @block.vector
        def _(dve):
            for buf in (qh, ql):
                for k in range(2):
                    dve.memset(buf[DH:P, k, 0, :].bitcast(F32), 0.0).then_inc(s_zero, 1)
                    dve.memset(buf[0:DH, k, 1, :].bitcast(F32), 0.0).then_inc(s_zero, 1)
            for b in range(B):
                dve.wait_ge(s_xin[b % 2], 16 * (b // 2 + 1))
                for t in range(QT):
                    dve.bn_stats(stats[:, t, :], xin[:, b % 2, t, :]).then_inc(s_bn, 1)
                dve.wait_ge(s_bn, 4 * (b + 1))
                for t in range(QT):
                    dve.bn_aggr(mv[:, t, :], stats[:, t, :]).then_inc(s_agg, 1)
                dve.wait_ge(s_agg, 4 * (b + 1))
                dve.tensor_scalar(var_eps[:], mv[:, :, 1], EPS, None, ALU.add).then_inc(s_ve, 1)
                dve.wait_ge(s_rstd, b + 1)
                for t in range(QT):
                    dve.tensor_scalar(xin[:, b % 2, t, :], xin[:, b % 2, t, :], mv[:, t, 0:1], rstd[:, t:t + 1],
                                      ALU.subtract, ALU.mult).then_inc(s_xn, 1)
                dve.wait_ge(s_xh, b + 1)
                cols = slice(b * S, (b + 1) * S)
                dve.tensor_tensor(xl[:, :, cols], pps[:, :, :], xh[:, :, cols].bitcast(F32), ALU.subtract).then_inc(s_xl, 1)
            dve.wait_ge(s_tab, B)
            seen2 = seen[:].rearrange("p (a c) -> p a c", a=1).to_broadcast([P, 2, P])

            def low(turn, which, u, last_turn):
                n = unit(which, u)
                src = pps[:, n % 2, :]
                dve.wait_ge(s_hi, at(turn, s_hi, split(n, last_turn)))
                if which == K_:
                    dve.scalar_tensor_tensor(out=kl[:, u % 2, :], in0=src, scalar=bkq[:, K_:K_ + 1],
                                             in1=kh[:, u % 2, :].bitcast(F32), op0=ALU.add, op1=ALU.subtract).then_inc(s_lo, 1)
                elif which == Q_:
                    for s in range(2):
                        rows = slice(s * DH, (s + 1) * DH)
                        dve.scalar_tensor_tensor(out=ql[rows, u % 2, s, :], in0=src[rows, :], scalar=bkq[rows, Q_:Q_ + 1],
                                                 in1=qh[rows, u % 2, s, :].bitcast(F32), op0=ALU.add,
                                                 op1=ALU.subtract).then_inc(s_lo, 1)
                else:
                    dve.tensor_tensor(vv[:, u % 2, :, :, DH:2 * DH], src.rearrange("p (t s d) -> p t s d", t=QT, s=2),
                                      vv[:, u % 2, :, :, 0:DH].bitcast(F32), ALU.subtract).then_inc(s_lo, 1)

            def hide_future(turn, n, part):
                dve.wait_ge(s_sc, at(turn, s_sc, 3 * n + 1 + 2 * part))
                if part == 0:
                    dg = sps[:, 0, 0:2 * 256].rearrange("p (a c) -> p a c", a=2)[:, :, 0:P]
                else:
                    dg = sps[:, 1:3, :].rearrange("p a c -> p (a c)")[:, 256:256 + 640 + P]
                    dg = bass.AP(dg.tensor, dg.offset, [list(dg.ap[0]), [640, 2], [1, P]])
                dve.tensor_tensor(dg, dg, seen2, ALU.mult).then_inc(s_dg, 1)

            def masked_max(turn, n):
                u = (n // 2) % B
                dve.wait_ge(s_t, at(turn, s_t, 3 * (n - NSB + 1)))
                wait_alone(dve, s_dg, at(turn, s_dg, 2 * n + 2), passed)
                for i in range(QT):
                    bank, col = SB_[i]
                    dve.tensor_tensor_reduce(out=sc[:, n % NSB, S_OFF[i]:S_OFF[i] + S_W[i]],
                                             in0=sps[:, bank, col:col + S_W[i]],
                                             in1=madd[:, u, S_OFF[i]:S_OFF[i] + S_W[i]],
                                             scale=1.0, scalar=-3.0e38, op0=ALU.add, op1=ALU.max,
                                             accum_out=mx[:, n % NSB, i:i + 1]).then_inc(s_max, 1)

            def negate_max(turn, n):
                dve.wait_ge(s_max, at(turn, s_max, 4 * n + 4))
                dve.tensor_scalar(nm[:, n % NSB, :], mx[:, n % NSB, :], -SCALE, None, ALU.mult).then_inc(s_nm, 1)

            def reciprocal(turn, n):
                dve.wait_ge(s_exp, at(turn, s_exp, 4 * n + 4))
                dve.reciprocal(rc[:, n % NSB, :], rs[:, n % NSB, :]).then_inc(s_rc, 1)

            def probs_low(turn, n, m):
                g = 3 * n + m
                dve.wait_ge(s_ph, at(turn, s_ph, g + 1))
                w, o = sum(T_W[j] for j in T_UNITS[m]), T_OFF[T_UNITS[m][0]]
                dve.tensor_tensor(pl[:, n % 2, o:o + w], tps[:, g % 2, 0:w], ph[:, n % 2, o:o + w].bitcast(F32),
                                  ALU.subtract).then_inc(s_pl, 1)

            def z_add(turn, n):
                u, s = n // 2, n % 2
                rows = slice(s * DH, (s + 1) * DH)
                dve.wait_ge(s_zc, at(turn, s_zc, n + 1))
                dve.tensor_tensor(zz[rows, u % 2, :], zps[DH:P, :], zz[rows, u % 2, :], ALU.add).then_inc(s_za, 1)

            def step(turn, k, last_turn):
                for part in range(2):
                    if k >= 0:
                        probs_low(turn, k, part)
                    if head(k + 3, last_turn):
                        hide_future(turn, k + 3, part)
                if k >= 0:
                    probs_low(turn, k, 2)
                if head(k + 3, last_turn):
                    masked_max(turn, k + 3)
                projections = step_projections(k, last_turn)
                for which, u in projections[:1]:
                    low(turn, which, u, last_turn)
                if head(k + 3, last_turn):
                    negate_max(turn, k + 3)
                if head(k + 2, last_turn):
                    reciprocal(turn, k + 2)
                for which, u in projections[1:]:
                    low(turn, which, u, last_turn)
                if k >= 0:
                    z_add(turn, k)

            schedule(dve, step)


NB = NT + NE - 1
NA = NT + NB


def feed_forward(nc, ap, zt, rows_in, rows_out, out):
    with ExitStack() as ctx:
        def sb(name, shape, dt=F32):
            return ctx.enter_context(nc.sbuf_tensor(name, shape, dt))

        keep = {
            "x2": sb("x2", [P, NT, D]),
            "h": sb("h", [P, NT, D]),
            "slot": sb("slot", [P, NT], U32),
            "prob": sb("prob", [P, NT]),
            "expert": sb("expert", [P, NA], I32),
            "ident": sb("ident2", [P, P]),
            "t1": sb("t1", [P, NE + 1, KT, F], F32R),
            "t2": sb("t2", [P, NE + 1, FT, D], F32R),
            "s1": sb("s1", [P, NE + 1, F]),
            "s2": sb("s2", [P, NE + 1, D]),
        }
        route(nc, ap, zt, rows_in, **keep)
        run_experts(nc, rows_in, rows_out, out, **keep)


def route(nc, ap, zt, rows_in, x2, h, slot, prob, expert, ident, t1, t2, s1, s2):
    ctx = ExitStack()
    with ctx:
        def sb(name, shape, dt=F32):
            return ctx.enter_context(nc.sbuf_tensor(name, shape, dt))

        def sem(name):
            return ctx.enter_context(nc.semaphore(name))

        wo = sb("wo", [P, HP, D])
        rows = sb("rows", [P, 3, D])
        wr = sb("wr", [P, KT, NE])
        bv = sb("bv", [P, HP])
        bvw = sb("bvw", [P, HP, P])
        zs = sb("zs", [P, 2, HP, P])
        hx = sb("hx", [P, QT, D])
        hs = sb("hs", [P, KT, S])
        ww = sb("ww", [P, 2, KT * F + FT * D])
        wa = sb("wa", [P, 2, KT * F + FT * D])
        wsum = sb("wsum", [P, 2, F + D])
        stats = sb("stats2", [P, QT, 6])
        mv = sb("mv2", [P, QT, 2])
        ve = sb("ve2", [P, QT])
        rstd = sb("rstd2", [P, QT])
        neg_half = sb("neg_half2", [P, QT])
        numbers = sb("numbers", [P, NA])
        before = sb("before", [P, P])
        ones = sb("ones", [P, P])
        small = sb("small", [P, 4, QT, NE])
        tiny = sb("tiny", [P, 5, QT])
        hot = sb("hot", [P, NT, NE])
        count = sb("count", [P, 2, NT, NE])
        filled = sb("filled", [P, NE, NT])
        ends = sb("ends", [P, 2, NE])
        first = sb("first", [P, NE])
        pos = sb("pos", [P, NT, NE])
        fslot = sb("fslot", [P, NT])
        ended = sb("ended", [P, NB, NE])
        fexp = sb("fexp", [P, NB])
        zero = sb("zero", [P, D])
        ops = ctx.enter_context(nc.psum_tensor("ops", [P, 2, 512], F32))
        hps = ctx.enter_context(nc.psum_tensor("hps", [P, 2, 512], F32))
        wps = ctx.enter_context(nc.psum_tensor("wps", [P, 2, 512], F32))
        rps = ctx.enter_context(nc.psum_tensor("rps", [P, QT, NE], F32))
        cps = ctx.enter_context(nc.psum_tensor("cps", [P, 2, NT, NE], F32))

        r_in, r_gp, r_x, r_bv, r_bo, r_xb, passed, r_fill = (sem(n) for n in (
            "r_in", "r_gp", "r_x", "r_bv", "r_bo", "r_xb", "r_passed", "r_fill"))
        r_z = [sem("r_z0"), sem("r_z1")]
        r_w = [sem(f"r_w{k}") for k in range(2)]
        r_abs, r_sgn, r_add, r_sum, r_size, r_big, r_t = (sem(n) for n in (
            "r_abs", "r_sgn", "r_add", "r_sum", "r_size", "r_big", "r_t"))
        r_o, r_res, r_dve, r_link, r_ve, r_pow, r_n2, r_hg, r_h, r_ht, r_hc, r_log, r_e, r_ez = (sem(n) for n in (
            "r_o", "r_res", "r_dve", "r_link", "r_ve", "r_pow", "r_n2", "r_hg", "r_h", "r_ht", "r_hc", "r_log", "r_e", "r_ez"))
        r_hot, r_cnt, r_tail, r_rows, r_sct, r_hx = sem("r_hot"), sem("r_cnt"), sem("r_tail"), sem("r_rows"), sem("r_sct"), sem("r_hx")
        NNORM, NSOFT = 5 * QT, 8
        C = {r_z[0]: 32, r_z[1]: 32, r_o: QT, r_res: QT, r_dve: NNORM, r_link: NSOFT, r_ve: 2, r_pow: 2, r_n2: 1, r_hg: 1,
             r_h: 1, r_ht: 1, r_hc: 1, r_hx: 1, r_log: 1, r_e: 1, r_ez: 1,
             r_w[0]: 32, r_w[1]: 16, r_abs: 3, r_sgn: 3, r_add: 12, r_sum: 3, r_size: 6, r_big: 6, r_t: 6}
        WK = 3
        TURNS = (NE + 1) // WK
        assert TURNS * WK == NE + 1 and TURNS == B - 1
        W1 = KT * F

        def at(turn, s, k):
            return turn * C[s] + (C[s] + k)

        def wait_reuse(eng, turn, k):
            eng.wait_ge(r_t, at(turn, r_t, (0, -2, 2)[k]))

        block = ctx.enter_context(nc.Block())

        @block.sync
        def _(sp):
            for d, s in ((ident, "ident"), (wo, "wo"), (rows, "rows"), (wr, "wr"), (bv, "bv")):
                sp.dma_start(d[:], ap[s]).then_inc(r_in, 16)
            sp.dma_start(x2[:], ap["x"].rearrange("(t p) d -> p t d", p=P)).then_inc(r_x, 16)

            def heads_out(b):
                zv = zt.rearrange("h p (b t q) -> b t p h q", b=B, q=P)
                for t in range(QT):
                    sp.wait_ge(r_o, at(b, r_o, t - 1))
                    sp.dma_start(zs[:, t % 2], zv[b, t]).then_inc(r_z[t % 2], 16)

            heads_out(0)
            sp.wait_ge(r_gp, 1)
            sp.dma_start(rows_in[T:].rearrange("(n p) d -> p n d", p=P),
                         zero[:].rearrange("p (o d) -> p o d", o=1).to_broadcast([P, NB, D])).then_inc(r_fill, 16)
            with sp.Fori(0, B - 1) as b:
                for k in range(WK):
                    wait_reuse(sp, b, k)
                    sp.dma_start(ww[:, k % 2], ap["w"][b * WK + k]).then_inc(r_w[k % 2], 16)
                heads_out(b + 1)

        @block.gpsimd
        def _(pool):
            for s, c in C.items():
                pool.sem_inc(s, c)
            pool.memset(zero[:], 0.0).then_inc(r_gp, 1)
            pool.memset(neg_half[:], -0.5).then_inc(r_gp, 1)
            pool.memset(ones[:], 1.0).then_inc(r_gp, 1)
            pool.iota(numbers[:], pattern=[[1, NA]], base=0, channel_multiplier=0,
                      allow_small_or_imprecise_dtypes=True).then_inc(r_gp, 1)
            pool.wait_ge(r_gp, 4)
            pool.affine_select(out=before[:], in_=ones[:], compare_op=ALU.is_gt, fill=0.0, base=0,
                               pattern=[[1, P]], channel_multiplier=-1).then_inc(r_gp, 1)
            pool.wait_ge(r_x, 16)
            pool.wait_ge(r_bv, 2)
            pool.tensor_tensor(x2[:], x2[:], rows[:, 0:1, :].to_broadcast([P, NT, D]), ALU.add).then_inc(r_xb, 1)

            def powers(b):
                for k in range(2):
                    pool.wait_ge(r_ve, at(b, r_ve, k + 1))
                    pool.tensor_tensor(rstd[:], ve[:], neg_half[:], ALU.pow).then_inc(r_pow, 1)

            def scale_shift(b):
                hb = h[:].rearrange("p (b t) d -> p b t d", b=B)[:, b]
                wait_alone(pool, r_n2, at(b, r_n2, 1), passed)
                pool.tensor_tensor(hb, hb, rows[:, 1:2, :].to_broadcast([P, QT, D]), ALU.mult).then_inc(r_hg, 1)
                pool.wait_ge(r_hx, at(b, r_hx, 0))
                wait_alone(pool, r_hg, at(b, r_hg, 1), passed)
                pool.tensor_tensor(hx[:], hb, rows[:, 2:3, :].to_broadcast([P, QT, D]), ALU.add).then_inc(r_h, 1)

            def size_sums(b, k):
                a1 = wa[:, k % 2, 0:W1].rearrange("p (t n) -> p t n", t=KT)
                a2 = wa[:, k % 2, W1:].rearrange("p (t n) -> p t n", t=FT)
                pool.wait_ge(r_sum, at(b, r_sum, k - 1 if k != 1 else -1))
                wait_alone(pool, r_abs, at(b, r_abs, k + 1), passed)
                pool.tensor_tensor(wsum[:, k % 2, 0:F], a1[:, 0], a1[:, 1], ALU.add).then_inc(r_add, 1)
                pool.tensor_tensor(wsum[:, k % 2, F:], a2[:, 0], a2[:, 1], ALU.add).then_inc(r_add, 1)
                for j in range(2, FT):
                    wait_alone(pool, r_add, at(b, r_add, 4 * k + j), passed)
                    pool.tensor_tensor(wsum[:, k % 2, F:], wsum[:, k % 2, F:], a2[:, j], ALU.add).then_inc(r_add, 1)

            def ternary(b, k):
                pool.wait_ge(r_sgn, at(b, r_sgn, k + 1))
                wait_alone(pool, r_big, at(b, r_big, 2 * k + 2), passed)
                e = b * WK + k
                pool.tensor_tensor(t1[:, bass.ds(e, 1)].rearrange("p o t n -> p (o t n)"), wa[:, k % 2, 0:W1], ww[:, k % 2, 0:W1],
                                   ALU.mult).then_inc(r_t, 1)
                pool.tensor_tensor(t2[:, bass.ds(e, 1)].rearrange("p o t n -> p (o t n)"), wa[:, k % 2, W1:], ww[:, k % 2, W1:],
                                   ALU.mult).then_inc(r_t, 1)

            powers(0)
            scale_shift(0)
            with pool.Fori(0, B - 1) as b:
                size_sums(b, 0)
                size_sums(b, 1)
                ternary(b, 0)
                size_sums(b, 2)
                ternary(b, 1)
                powers(b + 1)
                ternary(b, 2)
                scale_shift(b + 1)
            pool.wait_ge(r_fill, 16)
            pool.wait_ge(r_rows, 16 * B)
            pool.wait_ge(r_hx, at(B - 1, r_hx, 1))
            pool.wait_ge(r_tail, TAIL)
            for t in range(NT):
                pool.indirect_dma_start(rows_in, bass.IndirectOffsetOnAxis(ap=slot[:, t:t + 1], axis=0), h[:, t, :], None).then_inc(r_sct, 16)
            pool.wait_ge(r_sct, 16 * NT)

        @block.tensor
        def _(pe):
            pe.wait_ge(r_in, 80)
            pe.wait_ge(r_bv, 1)
            for g in range(HP):
                last = pe.matmul(wps[:, 1, 0:D], bvw[:, g, :], wo[:, g, :], start=(g == 0), stop=(g == HP - 1))
            last.then_inc(r_bo, 1)

            def project(b):
                for t in range(QT):
                    pe.wait_ge(r_z[t % 2], at(b, r_z[t % 2], 16 * (t // 2 + 1)))
                    pe.wait_ge(r_res, at(b, r_res, t - 1))
                    for g in range(HP):
                        last = pe.matmul(ops[:, t % 2, 0:D], zs[:, t % 2, g, :], wo[:, g, :], start=(g == 0), stop=(g == HP - 1))
                    last.then_inc(r_o, 1)

            def sizes(b, k):
                pe.wait_ge(r_size, at(b, r_size, 2 * k))
                pe.wait_ge(r_add, at(b, r_add, 4 * k + 4))
                pe.matmul(wps[:, 0, :], ones[:], wsum[:, k % 2, 0:F], start=True, stop=True)
                pe.matmul(wps[:, 1, 0:D], ones[:], wsum[:, k % 2, F:], start=True, stop=True).then_inc(r_sum, 1)

            def logits(b):
                pe.wait_ge(r_h, at(b, r_h, 1))
                pe.wait_ge(r_hc, at(b, r_hc, 0))
                for kt in range(KT):
                    for t in range(QT):
                        last = pe.transpose(hps[:, kt, t * P:(t + 1) * P], hx[:, t, kt * P:(kt + 1) * P], ident[:])
                last.then_inc(r_ht, 1)
                pe.wait_ge(r_hc, at(b, r_hc, 1))
                pe.wait_ge(r_e, at(b, r_e, 0))
                for t in range(QT):
                    for kt in range(KT):
                        last = pe.matmul(rps[:, t, :], hs[:, kt, t * P:(t + 1) * P], wr[:, kt, :], start=(kt == 0), stop=(kt == 1))
                last.then_inc(r_log, 1)

            pe.wait_ge(r_gp, 3)
            project(0)
            with pe.Fori(0, B - 1) as b:
                sizes(b, 0)
                sizes(b, 1)
                project(b + 1)
                sizes(b, 2)
                logits(b)
            logits(B - 1)
            pe.wait_ge(r_hot, B)
            pe.wait_ge(r_gp, 5)
            pe.matmul(cps[:, 0], before[:], hot[:], start=True, stop=True)
            pe.matmul(cps[:, 1], ones[:], hot[:], start=True, stop=True).then_inc(r_cnt, 1)

        @block.scalar
        def _(act):
            def weights(b, k):
                act.wait_ge(r_w[k % 2], at(b, r_w[k % 2], 16 * (k // 2 + 1)))
                act.activation(wa[:, k % 2], ww[:, k % 2], ACT.Abs).then_inc(r_abs, 1)
                act.wait_ge(r_abs, at(b, r_abs, k + 1))
                act.activation(ww[:, k % 2], ww[:, k % 2], ACT.Sign).then_inc(r_sgn, 1)

            def router(b):
                act.wait_ge(r_ht, at(b, r_ht, 1))
                act.wait_ge(r_log, at(b, r_log, 0))
                act.activation(hs[:], hps[:], ACT.Copy).then_inc(r_hc, 1)
                act.activation(h[:].rearrange("p (b t) d -> p b t d", b=B)[:, b], hx[:], ACT.Copy).then_inc(r_hx, 1)
                wait_alone(act, r_hx, at(b, r_hx, 1), passed)
                act.dma_start(rows_in[0:T].rearrange("(b t p) d -> b p t d", b=B, p=P)[b],
                              h[:].rearrange("p (b t) d -> p b t d", b=B)[:, b]).then_inc(r_rows, 16)
                act.wait_ge(r_e, at(b, r_e, 1))
                act.activation(small[:, 1], small[:, 0], ACT.Exp).then_inc(r_ez, 1)

            with act.Fori(0, B - 1) as b:
                for k in range(WK):
                    weights(b, k)
                router(b)
            router(B - 1)

        @block.vector
        def _(dve):
            dve.wait_ge(r_in, 80)
            dve.tensor_copy(bvw[:], bv[:].rearrange("p (h o) -> p h o", o=1).to_broadcast([P, HP, P])).then_inc(r_bv, 1)
            dve.wait_ge(r_bo, 1)
            dve.tensor_tensor(rows[:, 0, :], rows[:, 0, :], wps[:, 1, 0:D], ALU.add).then_inc(r_bv, 1)
            dve.wait_ge(r_xb, 1)

            def norms(b):
                done = [0]

                def link(ins):
                    done[0] += 1
                    ins.then_inc(r_dve, 1)
                    dve.wait_ge(r_dve, at(b, r_dve, done[0]))

                def tile(v, t):
                    return v[:, bass.ds(b * QT + t, 1), :].rearrange("p o d -> p (o d)")

                def norm(src, k):
                    for t in range(QT):
                        dve.bn_stats(stats[:, t, :], tile(src, t)).then_inc(r_dve, 1)
                    done[0] += QT
                    wait_alone(dve, r_dve, at(b, r_dve, done[0]), passed)
                    for t in range(QT):
                        dve.bn_aggr(mv[:, t, :], stats[:, t, :]).then_inc(r_dve, 1)
                    done[0] += QT
                    wait_alone(dve, r_dve, at(b, r_dve, done[0]), passed)
                    dve.tensor_scalar(ve[:], mv[:, :, 1], EPS, None, ALU.add).then_inc(r_ve, 1)
                    dve.wait_ge(r_pow, at(b, r_pow, k + 1))
                    for t in range(QT):
                        last = dve.tensor_scalar(tile(h, t), tile(src, t), mv[:, t, 0:1], rstd[:, t:t + 1], ALU.subtract, ALU.mult)
                        if k == 0:
                            last.then_inc(r_dve, 1)
                    if k == 0:
                        done[0] += QT
                        wait_alone(dve, r_dve, at(b, r_dve, done[0]), passed)
                    else:
                        last.then_inc(r_n2, 1)

                for t in range(QT):
                    dve.wait_ge(r_o, at(b, r_o, t + 1))
                    dve.tensor_tensor(tile(x2, t), ops[:, t % 2, 0:D], tile(x2, t), ALU.add).then_inc(r_res, 1)
                wait_alone(dve, r_res, at(b, r_res, QT), passed)
                norm(x2, 0)
                norm(h, 1)
                assert done[0] == C[r_dve], done

            def weights(b, k):
                e = bass.ds(b * WK + k, 1)
                sc1, sc2 = s1[:, e, :].rearrange("p o n -> p (o n)"), s2[:, e, :].rearrange("p o n -> p (o n)")
                dve.wait_ge(r_sum, at(b, r_sum, k + 1))
                dve.tensor_scalar(sc1, wps[:, 0, :], 1.0 / D, 1e-5, ALU.mult, ALU.max).then_inc(r_size, 1)
                dve.tensor_scalar(sc2, wps[:, 1, 0:D], 1.0 / F, 1e-5, ALU.mult, ALU.max).then_inc(r_size, 1)
                dve.wait_ge(r_size, at(b, r_size, 2 * k + 2))
                a1 = wa[:, k % 2, 0:W1].rearrange("p (t n) -> p t n", t=KT)
                a2 = wa[:, k % 2, W1:].rearrange("p (t n) -> p t n", t=FT)
                dve.scalar_tensor_tensor(out=a1, in0=a1, scalar=2.0, in1=s1[:, e, :].to_broadcast([P, KT, F]),
                                         op0=ALU.mult, op1=ALU.is_gt).then_inc(r_big, 1)
                dve.scalar_tensor_tensor(out=a2, in0=a2, scalar=2.0, in1=s2[:, e, :].to_broadcast([P, FT, D]),
                                         op0=ALU.mult, op1=ALU.is_gt).then_inc(r_big, 1)

            def softmax(b):
                done = [0]

                def link(ins):
                    done[0] += 1
                    ins.then_inc(r_link, 1)
                    dve.wait_ge(r_link, at(b, r_link, done[0]))

                def wide(v):
                    return v.rearrange("p (t o) -> p t o", o=1).to_broadcast([P, QT, NE])

                m, e, below, cand = (small[:, n] for n in range(4))
                mx, em, es, ix, pr = (tiny[:, n] for n in range(5))
                iota = numbers[:, 0:NE].rearrange("p (o n) -> p o n", o=1).to_broadcast([P, QT, NE])
                dve.wait_ge(r_log, at(b, r_log, 1))
                link(dve.tensor_reduce(mx, rps[:], AX.X, ALU.max))
                dve.tensor_tensor(m, rps[:], wide(mx), ALU.subtract).then_inc(r_e, 1)
                dve.wait_ge(r_ez, at(b, r_ez, 1))
                link(dve.tensor_reduce(em, e, AX.X, ALU.max))
                link(dve.tensor_reduce(es, e, AX.X, ALU.add))
                link(dve.reciprocal(pr, es))
                link(dve.tensor_tensor(prob[:].rearrange("p (b t) -> p b t", b=B)[:, b], pr, em, ALU.mult))
                link(dve.tensor_tensor(below, e, wide(em), ALU.is_lt))
                link(dve.scalar_tensor_tensor(out=cand, in0=below, scalar=float(NE), in1=iota, op0=ALU.mult, op1=ALU.add))
                link(dve.tensor_reduce(ix, cand, AX.X, ALU.min))
                dve.tensor_tensor(hot[:].rearrange("p (b t) e -> p b t e", b=B)[:, b], iota, wide(ix), ALU.is_equal).then_inc(r_hot, 1)
                assert done[0] == C[r_link], done

            norms(0)
            with dve.Fori(0, B - 1) as b:
                weights(b, 0)
                weights(b, 1)
                norms(b + 1)
                weights(b, 2)
                softmax(b)
            softmax(B - 1)

            dve.wait_ge(r_cnt, 1)
            done = [0]

            def link(ins):
                done[0] += 1
                ins.then_inc(r_tail, 1)
                dve.wait_ge(r_tail, done[0])

            rank, total = cps[:, 0], cps[:, 1]
            link(dve.tensor_copy(count[:, 0], total))
            src, dst = 0, 1
            for k in (1, 2, 4, 8):
                link(dve.tensor_copy(count[:, dst, 0:k], count[:, src, 0:k]))
                link(dve.tensor_tensor(count[:, dst, k:], count[:, src, k:], count[:, src, 0:NT - k], ALU.add))
                src, dst = dst, src
            counts = count[:, src, NT - 1, :]
            link(dve.scalar_tensor_tensor(out=filled[:], in0=numbers[:, 0:NT].rearrange("p (o n) -> p o n", o=1).to_broadcast([P, NE, NT]),
                                          scalar=float(P), in1=counts.rearrange("p (n o) -> p n o", o=1).to_broadcast([P, NE, NT]),
                                          op0=ALU.mult, op1=ALU.is_lt))
            link(dve.tensor_reduce(first[:], filled[:], AX.X, ALU.add))
            link(dve.tensor_copy(ends[:, 0], first[:]))
            a, z = 0, 1
            for k in (1, 2, 4):
                link(dve.tensor_copy(ends[:, z, 0:k], ends[:, a, 0:k]))
                link(dve.tensor_tensor(ends[:, z, k:], ends[:, a, k:], ends[:, a, 0:NE - k], ALU.add))
                a, z = z, a
            end = ends[:, a].rearrange("p (o n) -> p o n", o=1)
            link(dve.tensor_tensor(first[:], ends[:, a], first[:], ALU.subtract))
            link(dve.tensor_tensor(pos[:], count[:, src], total, ALU.subtract))
            link(dve.tensor_tensor(pos[:], pos[:], rank, ALU.add))
            link(dve.scalar_tensor_tensor(out=pos[:], in0=first[:].rearrange("p (o n) -> p o n", o=1).to_broadcast([P, NT, NE]),
                                          scalar=float(P), in1=pos[:], op0=ALU.mult, op1=ALU.add))
            link(dve.tensor_tensor(pos[:], pos[:], hot[:], ALU.mult))
            link(dve.tensor_reduce(fslot[:], pos[:], AX.X, ALU.add))
            link(dve.tensor_scalar(slot[:], fslot[:], float(T), None, ALU.add))
            link(dve.tensor_tensor(ended[:], numbers[:, 0:NB].rearrange("p (n o) -> p n o", o=1).to_broadcast([P, NB, NE]),
                                   end.to_broadcast([P, NB, NE]), ALU.is_ge))
            link(dve.tensor_reduce(fexp[:], ended[:], AX.X, ALU.add))
            link(dve.tensor_scalar(expert[:, NT:NA], fexp[:], 1.0, float(NE), ALU.add, ALU.min))
            link(dve.tensor_scalar(expert[:, 0:NT], numbers[:, 0:NT], 0.0, None, ALU.mult))
            assert done[0] == TAIL, done[0]


TAIL = 29


def run_experts(nc, rows_in, rows_out, out, x2, h, slot, prob, expert, ident, t1, t2, s1, s2):
    ctx = ExitStack()
    with ctx:
        def sb(name, shape, dt=F32):
            return ctx.enter_context(nc.sbuf_tensor(name, shape, dt))

        def ps(name):
            return ctx.enter_context(nc.psum_tensor(name, [P, 2, 512], F32))

        def sem(name):
            return ctx.enter_context(nc.semaphore(name))

        hb = sb("hb", [P, 2, D])
        hh, hl = sb("hh", [P, 2, KT, P], F32R), sb("hl", [P, 2, KT, P], F32R)
        zf = sb("zf", [P, 2, F])
        gf = sb("gf", [P, 2, F])
        gh, gl = sb("gh", [P, 2, FT, P], F32R), sb("gl", [P, 2, FT, P], F32R)
        yb = sb("yb", [P, 2, D])
        GB = 4
        ysh = sb("ysh", [P, GB, D])
        yrt = sb("yrt", [P, GB, D])
        hps, fps, gps, yps = ps("hps3"), ps("fps"), ps("gps"), ps("yps")

        f_ld = [sem("f_ld0"), sem("f_ld1")]
        f_st = [sem("f_st0"), sem("f_st1")]
        f_ht, f_hh, f_hl, f_f, f_z, f_silu, f_gt, f_gh, f_gl, f_y, f_yb, passed = (sem(n) for n in (
            "f_ht", "f_hh", "f_hl", "f_f", "f_z", "f_silu", "f_gt", "f_gh", "f_gl", "f_y", "f_yb", "f_passed"))
        f_sh = [sem(f"f_sh{k}") for k in range(GB)]
        f_rt = [sem(f"f_rt{k}") for k in range(GB)]
        f_mid, f_sum, f_out = sem("f_mid"), sem("f_sum"), sem("f_out")

        LEAD = range(-4, 3)
        BODY = (NA - 5) // 2
        assert LEAD.stop + 2 * BODY == NA - 2

        def after(eng, s, n):
            j, m = n
            if not isinstance(j, int) or 2 * j + m >= 0:
                eng.wait_ge(s, j * 2 + (m + 1))

        def after_dma(eng, s, n):
            j, m = n
            if not isinstance(j, int) or 2 * j + m >= 0:
                eng.wait_ge(s[m % 2], j * 16 + 16 * (m // 2 + 1))

        def there(n):
            j, m = n
            return not isinstance(j, int) or 0 <= 2 * j + m < NA

        def number(n):
            return n[0] * 2 + n[1]

        def schedule(eng, step):
            def at(m):
                return lambda k: (0, m + k)
            for m in LEAD:
                step(at(m))
            with eng.Fori(0, BODY) as j:
                for m in (LEAD.stop, LEAD.stop + 1):
                    step(lambda k, m=m: (j, m + k))
            for m in (NA - 2, NA - 1, NA):
                step(at(m))

        block = ctx.enter_context(nc.Block())

        @block.sync
        def _(sp):
            def step(i):
                n = i(4)
                if there(n):
                    after(sp, f_ht, i(2))
                    sp.dma_start(hb[:, n[1] % 2], rows_in.rearrange("(n p) d -> n p d", p=P)[number(n)]).then_inc(f_ld[n[1] % 2], 16)
            for m in LEAD:
                step(lambda k, m=m: (0, m + k))
            with sp.Fori(0, BODY - 1) as j:
                for m in (LEAD.stop, LEAD.stop + 1):
                    step(lambda k, m=m: (j, m + k))

            sh = rows_out.rearrange("(t p) d -> t p d", p=P)
            for s in range(2):
                sp.wait_ge(f_st[s], 16 * ((NA + 1 - s) // 2))
            for t in range(NT):
                if t >= GB:
                    sp.wait_ge(f_mid, t - GB + 1)
                sp.dma_start(ysh[:, t % GB], sh[t]).then_inc(f_sh[t % GB], 16)
            for t in range(NT):
                sp.wait_ge(f_sum, t + 1)
                sp.dma_start(out.rearrange("(t p) d -> t p d", p=P)[t], x2[:, t, :]).then_inc(f_out, 16)
            sp.wait_ge(f_out, 16 * NT)

        @block.gpsimd
        def _(pool):
            def step(i):
                n = i(-1)
                if there(n):
                    after(pool, f_yb, n)
                    pool.dma_start(rows_out.rearrange("(n p) d -> n p d", p=P)[number(n)], yb[:, n[1] % 2]).then_inc(f_st[n[1] % 2], 16)
            schedule(pool, step)
            for s in range(2):
                pool.wait_ge(f_st[s], 16 * ((NA + 1 - s) // 2))
            for t in range(NT):
                if t >= GB:
                    pool.wait_ge(f_sum, t - GB + 1)
                pool.indirect_dma_start(yrt[:, t % GB, :], None, rows_out, bass.IndirectOffsetOnAxis(ap=slot[:, t:t + 1], axis=0)).then_inc(f_rt[t % GB], 16)

        @block.tensor
        def _(pe):
            def block_expert(n):
                return pe.value_load(expert[0:1, bass.ds(number(n), 1)], min_val=0, max_val=NE)

            def step(i):
                n = i(2)
                if there(n):
                    k = n[1] % 2
                    after_dma(pe, f_ld, n)
                    after(pe, f_hl, i(0))
                    for kt in range(KT):
                        last = pe.transpose(hps[:, k, kt * P:(kt + 1) * P], hb[:, k, kt * P:(kt + 1) * P], ident[:])
                    last.then_inc(f_ht, 1)
                n = i(1)
                if there(n):
                    k = n[1] % 2
                    e = block_expert(n)
                    after(pe, f_hl, n)
                    after(pe, f_z, i(-1))
                    parts = [(v, kt) for kt in range(KT) for v in (hh, hl)]
                    for v, kt in parts:
                        last = pe.matmul(fps[:, k, :], v[:, k, kt, :], t1[:, bass.ds(e, 1), kt, :].rearrange("p o n -> p (o n)"),
                                         start=((v, kt) == parts[0]), stop=((v, kt) == parts[-1]))
                    last.then_inc(f_f, 1)
                n = i(0)
                if there(n):
                    k = n[1] % 2
                    after(pe, f_silu, n)
                    after(pe, f_gl, i(-2))
                    for j in range(FT):
                        last = pe.transpose(gps[:, k, j * P:(j + 1) * P], gf[:, k, j * P:(j + 1) * P], ident[:])
                    last.then_inc(f_gt, 1)
                n = i(-1)
                if there(n):
                    k = n[1] % 2
                    e = block_expert(n)
                    after(pe, f_gl, n)
                    after(pe, f_yb, i(-3))
                    parts = [(v, j) for j in range(FT) for v in (gh, gl)]
                    for v, j in parts:
                        last = pe.matmul(yps[:, k, 0:D], v[:, k, j, :], t2[:, bass.ds(e, 1), j, :].rearrange("p o n -> p (o n)"),
                                         start=((v, j) == parts[0]), stop=((v, j) == parts[-1]))
                    last.then_inc(f_y, 1)
            schedule(pe, step)

        @block.scalar
        def _(act):
            def step(i):
                n = i(2)
                if there(n):
                    k = n[1] % 2
                    after(act, f_ht, n)
                    after(act, f_f, i(0))
                    act.activation(hh[:, k].rearrange("p t n -> p (t n)"), hps[:, k, 0:D], ACT.Copy).then_inc(f_hh, 1)
                n = i(0)
                if there(n):
                    k = n[1] % 2
                    after(act, f_gt, n)
                    after(act, f_y, i(-2))
                    act.activation(gh[:, k].rearrange("p t n -> p (t n)"), gps[:, k, :], ACT.Copy).then_inc(f_gh, 1)
                n = i(1)
                if there(n):
                    k = n[1] % 2
                    after(act, f_z, n)
                    after(act, f_gt, i(-1))
                    act.activation(gf[:, k], zf[:, k], ACT.Silu).then_inc(f_silu, 1)
            schedule(act, step)

        @block.vector
        def _(dve):
            def block_expert(n):
                return dve.value_load(expert[0:1, bass.ds(number(n), 1)], min_val=0, max_val=NE)

            def step(i):
                n = i(2)
                if there(n):
                    k = n[1] % 2
                    after(dve, f_hh, n)
                    dve.tensor_tensor(hl[:, k].rearrange("p t n -> p (t n)"), hps[:, k, 0:D],
                                      hh[:, k].bitcast(F32).rearrange("p t n -> p (t n)"), ALU.subtract).then_inc(f_hl, 1)
                n = i(1)
                if there(n):
                    k = n[1] % 2
                    e = block_expert(n)
                    after(dve, f_f, n)
                    after(dve, f_silu, i(-1))
                    dve.tensor_tensor(zf[:, k], fps[:, k, :], s1[:, bass.ds(e, 1), :].rearrange("p o n -> p (o n)"), ALU.mult).then_inc(f_z, 1)
                n = i(0)
                if there(n):
                    k = n[1] % 2
                    after(dve, f_gh, n)
                    dve.tensor_tensor(gl[:, k].rearrange("p t n -> p (t n)"), gps[:, k, :],
                                      gh[:, k].bitcast(F32).rearrange("p t n -> p (t n)"), ALU.subtract).then_inc(f_gl, 1)
                n = i(-1)
                if there(n):
                    k = n[1] % 2
                    e = block_expert(n)
                    after(dve, f_y, n)
                    after_dma(dve, f_st, i(-3))
                    dve.tensor_tensor(yb[:, k], yps[:, k, 0:D], s2[:, bass.ds(e, 1), :].rearrange("p o n -> p (o n)"), ALU.mult).then_inc(f_yb, 1)
            schedule(dve, step)
            for t in range(NT):
                dve.wait_ge(f_sh[t % GB], 16 * (t // GB + 1))
                dve.tensor_tensor(x2[:, t, :], x2[:, t, :], ysh[:, t % GB], ALU.add).then_inc(f_mid, 1)
                dve.wait_ge(f_mid, t + 1)
                dve.wait_ge(f_rt[t % GB], 16 * (t // GB + 1))
                dve.scalar_tensor_tensor(out=x2[:, t, :], in0=yrt[:, t % GB], scalar=prob[:, t:t + 1], in1=x2[:, t, :],
                                         op0=ALU.mult, op1=ALU.add).then_inc(f_sum, 1)


def kernel(**inputs):
    import numpy as _np
    import concourse.bacc as _bacc
    from concourse import mybir as _mybir
    from concourse.bass_utils import run_bass_kernel_spmd as _run

    a = {k: _np.asarray(v) for k, v in inputs.items()}
    c = _np.ascontiguousarray
    wkqv = _np.stack([a[f"L0_xattn_W_{n}"] for n in "KQV"])
    wkqv = wkqv.reshape(3, HP, 2, KT, P, DH).transpose(1, 4, 0, 3, 2, 5)
    bkq = _np.stack([a[f"L0_xattn_b_{n}"] for n in "KQ"]).reshape(2, HP, P).transpose(2, 1, 0)
    ffn = "L0_ffn_"
    w1 = _np.concatenate([a[ffn + "shared_w1"][None], a[ffn + "expert_w1"]]).reshape(NE + 1, F, KT, P).transpose(0, 3, 2, 1)
    w2 = _np.concatenate([a[ffn + "shared_w2"][None], a[ffn + "expert_w2"]]).reshape(NE + 1, D, FT, P).transpose(0, 3, 2, 1)
    arrays = {
        "x": c(a["x"].reshape(T, D)),
        "ctx_t": c(a["ctx_1024"].reshape(T, KT, P).transpose(2, 1, 0)),
        "mask": c(_np.broadcast_to(a["mask_Bx1x1xS2_ff0"].reshape(B, 1, S), (B, P, S))),
        "wkqv": c(wkqv.reshape(HP, P, 3, KT, P)),
        "bkq": c(bkq),
        "bv": c(a["L0_xattn_b_V"].reshape(HP, P).T),
        "ident": _np.eye(P, dtype=_np.float32),
        "wo": c(a["L0_xattn_W_O"].reshape(HP, P, D).transpose(1, 0, 2)),
        "rows": c(_np.broadcast_to(_np.stack([a["L0_xattn_b_O"], a[ffn + "ln_gamma"], a[ffn + "ln_beta"]]), (P, 3, D))),
        "w": c(_np.concatenate([w1.reshape(NE + 1, P, KT * F), w2.reshape(NE + 1, P, FT * D)], axis=2)),
        "wr": c(a[ffn + "router_w"].reshape(NE, KT, P).transpose(2, 1, 0)),
    }
    nc = _bacc.Bacc("TRN2", target_bir_lowering=False, num_devices=1)
    ap = {n: nc.dram_tensor(f"in_{n}", v.shape, _mybir.dt.from_np(v.dtype), kind="ExternalInput").ap() for n, v in arrays.items()}
    out = nc.dram_tensor("out", (T, D), _mybir.dt.float32, kind="ExternalOutput").ap()
    zt = nc.dram_tensor("zt", (HP, P, T), _mybir.dt.float32, kind="Internal").ap()
    attention(nc, ap["x"], ap["ctx_t"], ap["mask"], ap["wkqv"], ap["bkq"], ap["ident"], zt)
    rows_in, rows_out = (nc.dram_tensor(n, (NA * P, D), _mybir.dt.float32, kind="Internal").ap() for n in ("rows_in", "rows_out"))
    feed_forward(nc, ap, zt, rows_in, rows_out, out)
    r = _run(nc, [{f"in_{n}": v for n, v in arrays.items()}], core_ids=[0])
    return _np.asarray(r.results[0]["out"]).reshape(B, S, D)
```

```python
from contextlib import ExitStack

import concourse.bass as bass
from concourse import mybir

F32 = mybir.dt.float32
F32R = mybir.dt.float32r
U32 = mybir.dt.uint32
I32 = mybir.dt.int32
ALU = mybir.AluOpType
ACT = mybir.ActivationFunctionType
AX = mybir.AxisListType

P = 128
B, S, D = 4, 512, 256
T = B * S
NT = T // P
KT = D // P
H, DH = 16, 64
HP = H // 2
QT = S // P
F = 512
FT = F // P
NE = 8
EPS = 1e-5
IGNORE = -1e5
SCALE = float(DH) ** -0.5
W8 = 1.0 / SCALE
FAR = -1e30
FAR_BELOW = 120.0

S_OFF = [P * i * (i + 1) // 2 for i in range(QT)]
S_W = [P * (i + 1) for i in range(QT)]
S_ALL = P * QT * (QT + 1) // 2
T_UNITS = [[0], [1, 3], [2]]
T_W = [S - P * j for j in range(QT)]
T_OFF = {0: 0, 1: T_W[0], 3: T_W[0] + T_W[1], 2: T_W[0] + T_W[1] + T_W[3]}


def wait_alone(eng, s, value, passed):
    eng.wait_ge(s, value)
    eng.sem_inc(passed, 1)


def attention(nc, ap, zt):
    with ExitStack() as ctx:
        def sb(name, shape, dt=F32):
            return ctx.enter_context(nc.sbuf_tensor(name, shape, dt))

        xh, xl = sb("xh", [P, KT, T], F32R), sb("xl", [P, KT, T], F32R)
        lowest = sb("lowest", [P, B, QT])
        future = sb("future", [P, B, QT])
        attention_seen_keys(nc, ap["x"], ap["ctx_t"], ap["mask"], ap["wkqv"], ap["bkq"], ap["ident"], zt, xh, xl, lowest, future)
        attention_all_keys(nc, ap, zt, xh, xl, lowest, future)


def attention_seen_keys(nc, x, ctx_t, mask, wkqv, bkq_d, ident_d, zt, xh, xl, lowest, future):
    ctx = ExitStack()
    with ctx:
        def sb(name, shape, dt=F32):
            return ctx.enter_context(nc.sbuf_tensor(name, shape, dt))

        def sem(name):
            return ctx.enter_context(nc.semaphore(name))

        ch, cl = sb("ch", [P, KT, T], F32R), sb("cl", [P, KT, T], F32R)
        xin = sb("xin", [P, B, QT, D])
        cin = sb("cin", [P, 2, KT, S])
        ident = sb("ident", [P, P])
        maskb = sb("maskb", [P, B, S])
        tilemax = sb("tilemax", [P, B, QT])
        ignore = sb("ignore", [P, P])
        madd = sb("madd", [P, B, S_ALL])
        stats = sb("stats", [P, 2, QT, 6])
        mv = sb("mv", [P, 2, QT, 2])
        var_eps = sb("var_eps", [P, 2, QT])
        neg_half = sb("neg_half", [P, QT])
        rstd = sb("rstd", [P, 2, QT])
        wraw = sb("wraw", [P, 3, KT, P])
        wh, wl = sb("wh", [P, 3, KT, P], F32R), sb("wl", [P, 3, KT, P], F32R)
        bias = sb("bias", [P, HP, 2])
        bkq = sb("bkq", [P, 2])
        kh, kl = sb("kh", [P, 2, S], F32R), sb("kl", [P, 2, S], F32R)
        qh, ql = sb("qh", [P, 2, 2, S], F32R), sb("ql", [P, 2, 2, S], F32R)
        vv = sb("vv", [P, 2, QT, 2, 2 * DH], F32R)
        NSB = 4
        sc = sb("sc", [P, NSB, S_ALL])
        mx = sb("mx", [P, NSB, QT])
        nm = sb("nm", [P, NSB, QT])
        rs = sb("rs", [P, NSB, QT])
        rc = sb("rc", [P, NSB, QT])
        ph, pl = sb("ph", [P, 2, S_ALL], F32R), sb("pl", [P, 2, S_ALL], F32R)
        zz = sb("zz", [P, 2, S])

        sps = ctx.enter_context(nc.psum_tensor("sps", [P, 3, 512], F32))
        tps = ctx.enter_context(nc.psum_tensor("tps", [P, 2, 512], F32))
        zps = ctx.enter_context(nc.psum_tensor("zps", [P, 512], F32))
        pps = ctx.enter_context(nc.psum_tensor("pps", [P, 2, 512], F32))
        SB_ = [(0, 0), (0, P), (1, 0), (2, 0)]

        s_consts_loaded = sem("s_consts_loaded")
        s_x_loaded = [sem(f"s_x_loaded{b}") for b in range(B)]
        s_mask_loaded, s_future_step, s_lowest, s_mask_scaled = sem("s_mask_loaded"), sem("s_future_step"), sem("s_lowest"), sem("s_mask_scaled")
        s_ctx_loaded = [sem(f"s_ctx_loaded{k}") for k in range(2)]
        s_zeros, s_tables, s_mask_tables, passed = sem("s_zeros"), sem("s_tables"), sem("s_mask_tables"), sem("passed")
        s_stats, s_moments, s_variance, s_rstd, s_normalised = (sem(n) for n in ("s_stats", "s_moments", "s_variance", "s_rstd", "s_normalised"))
        s_x_turned, s_x_high, s_x_low, s_ctx_high, s_ctx_low = (sem(n) for n in ("s_x_turned", "s_x_high", "s_x_low", "s_ctx_high", "s_ctx_low"))
        s_wkq_loaded, s_wv_loaded, s_wkq_split, s_wv_split = (sem(n) for n in ("s_wkq_loaded", "s_wv_loaded", "s_wkq_split", "s_wv_split"))
        s_projected, s_proj_high, s_proj_low = sem("s_projected"), sem("s_proj_high"), sem("s_proj_low")
        s_scores, s_row_max, s_neg_max, s_exps, s_reciprocal, s_probs = (sem(n) for n in ("s_scores", "s_row_max", "s_neg_max", "s_exps", "s_reciprocal", "s_probs"))
        s_probs_turned, s_probs_high, s_probs_low, s_values, s_z_copied, s_z_added = (sem(n) for n in ("s_probs_turned", "s_probs_high", "s_probs_low", "s_values", "s_z_copied", "s_z_added"))
        s_z_stored = [sem("s_z_stored0"), sem("s_z_stored1")]

        NH = 2 * B
        C = {s_wkq_loaded: 16, s_wv_loaded: 16, s_wkq_split: 3, s_wv_split: 2, s_projected: 3 * B, s_proj_high: 4 * B, s_proj_low: 4 * B,
             s_scores: 3 * NH, s_row_max: 4 * NH, s_neg_max: NH, s_exps: 4 * NH, s_reciprocal: NH, s_lowest: NH, s_probs: 4 * NH,
             s_probs_turned: 3 * NH, s_probs_high: 3 * NH, s_probs_low: 3 * NH, s_values: NH, s_z_copied: NH, s_z_added: NH,
             s_z_stored[0]: 16 * B // 2, s_z_stored[1]: 16 * B // 2}

        def at(turn, s, k):
            return turn * C[s] + (C[s] + k)

        K_, Q_, V_ = 0, 1, 2
        AHEAD = 4

        def unit(which, u):
            return 3 * (u - 1) if which == V_ else 3 * (u - 3) + 1 + which

        def split(index, last=False):
            if last and index > unit(V_, 2):
                return split(unit(V_, 2)) + (index >= unit(V_, 3))
            return 4 * (index // 3) + (1, 2, 4)[index % 3] + (index < unit(V_, -1))

        def projected(index, last=False):
            if last and index > unit(V_, 2):
                return projected(unit(V_, 2)) + (index >= unit(V_, 3))
            return index + 1 + (index < unit(V_, -1))

        START = dict(C)
        START[s_projected] += unit(K_, 0) + 1
        START[s_proj_high] += 4 * (unit(K_, 0) // 3) + 1 + 1
        START[s_proj_low] = START[s_proj_high]
        START[s_lowest] -= 1

        def step_projections(k, last):
            found = [(K_, (k + 5) // 2), (Q_, (k + 5) // 2)] if k % 2 else [(V_, (k + 2) // 2)]
            return [(w, u) for w, u in found if 0 <= u < (B if last else B + 3)]

        def schedule(eng, step):
            for k in range(-5, 0):
                step(0, k, False)
            with eng.Fori(0, HP - 1) as hp:
                for k in range(NH):
                    step(hp, k, False)
            for k in range(NH):
                step(HP - 1, k, True)

        def head(n, last):
            return 0 <= n < (NH if last else NH + AHEAD)

        block = ctx.enter_context(nc.Block())

        @block.sync
        def _(sp):
            sp.dma_start(ident[:], ident_d).then_inc(s_consts_loaded, 16)
            sp.dma_start(bias[:], bkq_d).then_inc(s_consts_loaded, 16)
            for b in range(B):
                if b < 2:
                    sp.dma_start(xin[:, b], x[b * S:(b + 1) * S, :].rearrange("(t p) d -> p t d", p=P)).then_inc(s_x_loaded[b], 16)
                    sp.dma_start(cin[:, b], ctx_t[:, :, b * S:(b + 1) * S]).then_inc(s_ctx_loaded[b], 16)
                if b == 0:
                    sp.dma_start(wraw[:, 0:2], wkqv[0, :, 0:2]).then_inc(s_wkq_loaded, 16)
                    sp.dma_start(wraw[:, 2], wkqv[0, :, 2]).then_inc(s_wv_loaded, 16)
            for b in range(2, B):
                sp.dma_start(xin[:, b], x[b * S:(b + 1) * S, :].rearrange("(t p) d -> p t d", p=P)).then_inc(s_x_loaded[b], 16)
            sp.dma_start(maskb[:], mask.rearrange("b p n -> p b n")).then_inc(s_mask_loaded, 16)
            for b in range(2, B):
                sp.wait_ge(s_ctx_low, b - 1)
                sp.dma_start(cin[:, b % 2], ctx_t[:, :, b * S:(b + 1) * S]).then_inc(s_ctx_loaded[b % 2], 16)

            def turn(hp, last):
                if not last:
                    sp.wait_ge(s_wkq_split, at(hp, s_wkq_split, C[s_wkq_split]))
                    sp.dma_start(wraw[:, 0:2], wkqv[hp + 1, :, 0:2]).then_inc(s_wkq_loaded, 16)
                    sp.wait_ge(s_wv_split, at(hp, s_wv_split, C[s_wv_split]))
                    sp.dma_start(wraw[:, 2], wkqv[hp + 1, :, 2]).then_inc(s_wv_loaded, 16)
                for u in range(B):
                    sp.wait_ge(s_z_added, at(hp, s_z_added, 2 * u + 2))
                    sp.dma_start(zt[hp, :, u * S:(u + 1) * S], zz[:, u % 2]).then_inc(s_z_stored[u % 2], 16)

            with sp.Fori(0, HP - 1) as hp:
                turn(hp, False)
            turn(HP - 1, True)
            for k in range(2):
                sp.wait_ge(s_z_stored[k], C[s_z_stored[k]] * (HP + 1))

        @block.gpsimd
        def _(pool):
            for s in C:
                pool.sem_inc(s, START[s])
            pool.memset(ignore[:], 0.0).then_inc(s_tables, 1)
            pool.memset(neg_half[:], -0.5).then_inc(s_tables, 1)
            pool.wait_ge(s_tables, 2)
            pool.affine_select(out=ignore[:], in_=ignore[:], compare_op=ALU.is_ge, fill=FAR, base=0,
                               pattern=[[-1, P]], channel_multiplier=1).then_inc(s_tables, 1)
            pool.memset(lowest[:], 3.0e38).then_inc(s_lowest, 1)

            def power(b):
                pool.wait_ge(s_variance, b + 1)
                pool.tensor_tensor(rstd[:, b % 2], var_eps[:, b % 2], neg_half[:], ALU.pow).then_inc(s_rstd, 1)

            def context_low(b):
                pool.wait_ge(s_ctx_high, b + 1)
                pool.tensor_tensor(cl[:, :, b * S:(b + 1) * S], cin[:, b % 2], ch[:, :, b * S:(b + 1) * S].bitcast(F32),
                                   ALU.subtract).then_inc(s_ctx_low, 1)

            def split_kq(turn, version):
                wait_alone(pool, s_wkq_loaded, at(turn, s_wkq_loaded, 16 * (version + 1)), passed)
                if version:
                    wait_alone(pool, s_proj_low, at(turn, s_proj_low, split(unit(Q_, B - 1))), passed)
                pool.tensor_copy(bkq[:], bias[:, turn + version, 0:2]).then_inc(s_wkq_split, 1)
                pool.tensor_copy(wh[:, 0:2], wraw[:, 0:2]).then_inc(s_wkq_split, 1)
                pool.wait_ge(s_wkq_split, at(turn, s_wkq_split, C[s_wkq_split] * version + 2))
                pool.tensor_tensor(wl[:, 0:2], wraw[:, 0:2], wh[:, 0:2].bitcast(F32), ALU.subtract).then_inc(s_wkq_split, 1)

            def split_v(turn, version):
                wait_alone(pool, s_wv_loaded, at(turn, s_wv_loaded, 16 * (version + 1)), passed)
                if version:
                    wait_alone(pool, s_projected, at(turn, s_projected, projected(unit(V_, B - 1))), passed)
                pool.tensor_copy(wh[:, 2], wraw[:, 2]).then_inc(s_wv_split, 1)
                pool.wait_ge(s_wv_split, at(turn, s_wv_split, C[s_wv_split] * version + 1))
                pool.tensor_tensor(wl[:, 2], wraw[:, 2], wh[:, 2].bitcast(F32), ALU.subtract).then_inc(s_wv_split, 1)

            pool.wait_ge(s_tables, 3)
            pool.wait_ge(s_consts_loaded, 32)
            power(0)
            context_low(0)
            power(1)
            context_low(1)
            split_kq(0, 0)
            power(2)
            power(3)
            split_v(0, 0)
            context_low(2)
            context_low(3)
            for i in range(QT):
                pool.wait_ge(s_mask_scaled, i + 1)
                dg = madd[:, :, S_OFF[i] + P * i:S_OFF[i] + P * (i + 1)]
                pool.tensor_tensor(dg, dg, ignore[:].rearrange("p (o n) -> p o n", o=1).to_broadcast([P, B, P]), ALU.add).then_inc(s_mask_tables, 1)

            def step(turn, k, last_turn):
                if head(k + 2, last_turn):
                    n = k + 2
                    wait_alone(pool, s_reciprocal, at(turn, s_reciprocal, n + 1), passed)
                    for i in range(QT):
                        e = sc[:, n % NSB, S_OFF[i]:S_OFF[i] + S_W[i]]
                        pool.tensor_tensor(e, e, rc[:, n % NSB, i:i + 1].to_broadcast([P, S_W[i]]), ALU.mult).then_inc(s_probs, 1)
                if not last_turn:
                    if k == 1:
                        split_kq(turn, 1)
                    if k == 4:
                        split_v(turn, 1)

            schedule(pool, step)

        @block.tensor
        def _(pe):
            pe.wait_ge(s_consts_loaded, 32)
            for b in range(B):
                pe.wait_ge(s_normalised, 4 * (b + 1))
                if b:
                    pe.wait_ge(s_x_low, b)
                for kt in range(KT):
                    for t in range(QT):
                        last = pe.transpose(pps[:, kt, t * P:(t + 1) * P], xin[:, b, t, kt * P:(kt + 1) * P], ident[:])
                last.then_inc(s_x_turned, 1)
            pe.wait_ge(s_x_low, B)
            pe.wait_ge(s_zeros, 8)
            pe.wait_ge(s_ctx_low, B)

            def project(turn, which, u, last_turn, between=None):
                n = unit(which, u)
                if which == K_ and u in (0, B):
                    pe.wait_ge(s_wkq_split, at(turn, s_wkq_split, C[s_wkq_split] * (u // B + 1)))
                if which == V_ and u in (0, B):
                    pe.wait_ge(s_wv_split, at(turn, s_wv_split, C[s_wv_split] * (u // B + 1)))
                if n >= unit(K_, 1):
                    pe.wait_ge(s_proj_low, at(turn, s_proj_low, split(n - 2, last_turn)))
                dst = pps[:, n % 2, :]
                u %= B
                if which == V_:
                    for t in range(QT):
                        if t == QT // 2 and between:
                            between()
                        tokens = slice(u * S + t * P, u * S + (t + 1) * P)
                        terms = [(a_[:, kt, tokens], w_[:, V_, kt, :]) for kt in range(KT)
                                 for a_, w_ in ((ch, wh), (ch, wl), (cl, wh))]
                        for g, (a_, w_) in enumerate(terms):
                            last = pe.matmul(dst[:, t * P:(t + 1) * P], a_, w_, start=(g == 0), stop=(g == len(terms) - 1))
                else:
                    high_in, low_in = (ch, cl) if which == K_ else (xh, xl)
                    tokens = slice(u * S, (u + 1) * S)
                    terms = [(w_[:, which, kt, :], a_[:, kt, tokens]) for kt in range(KT)
                             for w_, a_ in ((wh, high_in), (wh, low_in), (wl, high_in))]
                    for g, (w_, a_) in enumerate(terms):
                        last = pe.matmul(dst, w_, a_, start=(g == 0), stop=(g == len(terms) - 1))
                last.then_inc(s_projected, 1)

            def scores(turn, n):
                u, s = n // 2, n % 2
                if s == 0:
                    pe.wait_ge(s_proj_low, at(turn, s_proj_low, split(unit(Q_, u))))
                for i in range(QT):
                    bank, col = SB_[i]
                    if i != 1:
                        pe.wait_ge(s_row_max, at(turn, s_row_max, 4 * (n - 1) + (2, 2, 3, 4)[i]))
                    dst = sps[:, bank, col:col + S_W[i]]
                    queries = slice(i * P, (i + 1) * P)
                    terms = ((qh, kh), (qh, kl), (ql, kh))
                    for g, (q_, k_) in enumerate(terms):
                        last = pe.matmul(dst, q_[:, u % 2, s, queries], k_[:, u % 2, 0:S_W[i]],
                                         start=(g == 0), stop=(g == len(terms) - 1))
                    if i != 0:
                        last.then_inc(s_scores, 1)

            def turn_probs(turn, n, units):
                if 0 in units:
                    pe.wait_ge(s_probs, at(turn, s_probs, 4 * n + 4))
                for m in units:
                    tiles = T_UNITS[m]
                    g = 3 * n + m
                    pe.wait_ge(s_probs_low, at(turn, s_probs_low, g - 1))
                    col = 0
                    for j in tiles:
                        for i in range(j, QT):
                            last = pe.transpose(tps[:, g % 2, col:col + P],
                                                sc[:, n % NSB, S_OFF[i] + j * P:S_OFF[i] + (j + 1) * P], ident[:])
                            col += P
                    last.then_inc(s_probs_turned, 1)

            def values(turn, n, last_turn):
                u, s = n // 2, n % 2
                pe.wait_ge(s_z_added, at(turn, s_z_added, n))
                if s == 0:
                    pe.wait_ge(s_proj_low, at(turn, s_proj_low, split(unit(V_, u), last_turn)))
                pe.wait_ge(s_probs_low, at(turn, s_probs_low, 3 * n + 3))
                terms = [(j, p_) for j in range(QT) for p_ in (ph, pl)]
                for g, (j, p_) in enumerate(terms):
                    last = pe.matmul(zps[:, j * P:S], vv[:, u % 2, j, s, :], p_[:, n % 2, T_OFF[j]:T_OFF[j] + T_W[j]],
                                     start=(g == 0), stop=(g == len(terms) - 1))
                last.then_inc(s_values, 1)

            def step(turn, k, last_turn):
                def rest():
                    if k >= 0:
                        turn_probs(turn, k, (2,))

                if k >= 0:
                    turn_probs(turn, k, (0, 1))
                found = step_projections(k, last_turn)
                for which, u in found:
                    if which == Q_:
                        rest()
                    project(turn, which, u, last_turn, rest)
                if not found:
                    rest()
                if k >= 0:
                    values(turn, k, last_turn)
                if head(k + AHEAD, last_turn):
                    scores(turn, k + AHEAD)

            schedule(pe, step)

        @block.scalar
        def _(act):
            def context_high(b):
                act.wait_ge(s_ctx_loaded[b % 2], 16 * (b // 2 + 1))
                act.activation(ch[:, :, b * S:(b + 1) * S], cin[:, b % 2], ACT.Copy).then_inc(s_ctx_high, 1)

            def x_high(b):
                act.wait_ge(s_x_turned, b + 1)
                act.activation(xh[:, :, b * S:(b + 1) * S], pps[:, :, :], ACT.Copy).then_inc(s_x_high, 1)

            context_high(0)
            context_high(1)
            for b in range(B):
                x_high(b)
                if b < 2:
                    context_high(b + 2)
            act.wait_ge(s_mask_loaded, 16)
            for i in range(QT):
                act.activation(madd[:, :, S_OFF[i]:S_OFF[i] + S_W[i]], maskb[:, :, 0:S_W[i]], ACT.Copy, scale=W8).then_inc(s_mask_scaled, 1)

            def high(turn, which, u, last_turn):
                n = unit(which, u)
                act.wait_ge(s_projected, at(turn, s_projected, projected(n, last_turn)))
                src = pps[:, n % 2, :]
                if which == K_:
                    act.wait_ge(s_scores, at(turn, s_scores, 3 * (2 * u - 2)))
                    act.activation(kh[:, u % 2, :], src, ACT.Identity, bias=bkq[:, K_:K_ + 1]).then_inc(s_proj_high, 1)
                elif which == Q_:
                    for s in range(2):
                        rows = slice(s * DH, (s + 1) * DH)
                        act.activation(qh[rows, u % 2, s, :], src[rows, :], ACT.Identity,
                                       bias=bkq[rows, Q_:Q_ + 1]).then_inc(s_proj_high, 1)
                else:
                    act.wait_ge(s_values, at(turn, s_values, 2 * u - 2))
                    act.activation(vv[:, u % 2, :, :, 0:DH], src.rearrange("p (t s d) -> p t s d", t=QT, s=2),
                                   ACT.Copy).then_inc(s_proj_high, 1)

            def exps(turn, n, tiles):
                act.wait_ge(s_neg_max, at(turn, s_neg_max, n + 1))
                for i in tiles:
                    e = sc[:, n % NSB, S_OFF[i]:S_OFF[i] + S_W[i]]
                    act.activation(e, e, ACT.Exp, bias=nm[:, n % NSB, i:i + 1], scale=SCALE,
                                   accum_out=rs[:, n % NSB, i:i + 1]).then_inc(s_exps, 1)

            def probs_high(turn, n):
                act.wait_ge(s_values, at(turn, s_values, n - 1))
                for m, tiles in enumerate(T_UNITS):
                    g = 3 * n + m
                    act.wait_ge(s_probs_turned, at(turn, s_probs_turned, g + 1))
                    w, o = sum(T_W[j] for j in tiles), T_OFF[tiles[0]]
                    act.activation(ph[:, n % 2, o:o + w], tps[:, g % 2, 0:w], ACT.Copy).then_inc(s_probs_high, 1)

            def z_copy(turn, n):
                u, s = n // 2, n % 2
                rows = slice(s * DH, (s + 1) * DH)
                act.wait_ge(s_values, at(turn, s_values, n + 1))
                if s == 0:
                    act.wait_ge(s_z_stored[u % 2], at(turn, s_z_stored[u % 2], 16 * (u // 2)))
                act.activation(zz[rows, u % 2, :], zps[0:DH, :], ACT.Copy).then_inc(s_z_copied, 1)

            def step(turn, k, last_turn):
                if k >= 0:
                    probs_high(turn, k)
                projections = step_projections(k, last_turn)
                before = 0 if k % 2 else QT - 1
                if head(k + 2, last_turn) and before:
                    exps(turn, k + 2, range(before))
                for which, u in projections[:1]:
                    high(turn, which, u, last_turn)
                between = 2 if k % 2 else QT
                if head(k + 2, last_turn):
                    exps(turn, k + 2, range(before, between))
                for which, u in projections[1:]:
                    high(turn, which, u, last_turn)
                if head(k + 2, last_turn) and between < QT:
                    exps(turn, k + 2, range(between, QT))
                if k >= 0:
                    z_copy(turn, k)

            schedule(act, step)

        @block.vector
        def _(dve):
            for buf in (qh, ql):
                for k in range(2):
                    dve.memset(buf[DH:P, k, 0, :].bitcast(F32), 0.0).then_inc(s_zeros, 1)
                    dve.memset(buf[0:DH, k, 1, :].bitcast(F32), 0.0).then_inc(s_zeros, 1)
            def moments(b):
                dve.wait_ge(s_x_loaded[b], 16)
                for t in range(QT):
                    dve.bn_stats(stats[:, b % 2, t, :], xin[:, b, t, :]).then_inc(s_stats, 1)
                dve.wait_ge(s_stats, 4 * (b + 1))
                for t in range(QT):
                    dve.bn_aggr(mv[:, b % 2, t, :], stats[:, b % 2, t, :]).then_inc(s_moments, 1)
                dve.wait_ge(s_moments, 4 * (b + 1))
                dve.tensor_scalar(var_eps[:, b % 2], mv[:, b % 2, :, 1], EPS, None, ALU.add).then_inc(s_variance, 1)

            def normalise(b):
                dve.wait_ge(s_rstd, b + 1)
                for t in range(QT):
                    dve.tensor_scalar(xin[:, b, t, :], xin[:, b, t, :], mv[:, b % 2, t, 0:1], rstd[:, b % 2, t:t + 1],
                                      ALU.subtract, ALU.mult).then_inc(s_normalised, 1)

            def x_low(b):
                dve.wait_ge(s_x_high, b + 1)
                cols = slice(b * S, (b + 1) * S)
                dve.tensor_tensor(xl[:, :, cols], pps[:, :, :], xh[:, :, cols].bitcast(F32), ALU.subtract).then_inc(s_x_low, 1)

            moments(0)
            for b in range(B):
                if b + 1 < B:
                    moments(b + 1)
                normalise(b)
                if b:
                    x_low(b - 1)
            x_low(B - 1)
            dve.wait_ge(s_mask_loaded, 16)
            dve.tensor_reduce(tilemax[:], maskb[:].rearrange("p b (i k) -> p b i k", i=QT), AX.X, ALU.max).then_inc(s_future_step, 1)
            for i in range(QT - 2, -1, -1):
                dve.wait_ge(s_future_step, QT - 1 - i)
                dve.tensor_tensor(tilemax[:, :, i:i + 1], tilemax[:, :, i:i + 1], tilemax[:, :, i + 1:i + 2], ALU.max).then_inc(s_future_step, 1)
            dve.wait_ge(s_future_step, QT)
            dve.tensor_scalar(future[:], tilemax[:], IGNORE, W8, ALU.add, ALU.mult).then_inc(s_future_step, 1)
            dve.wait_ge(s_mask_tables, B)

            def low(turn, which, u, last_turn):
                n = unit(which, u)
                src = pps[:, n % 2, :]
                dve.wait_ge(s_proj_high, at(turn, s_proj_high, split(n, last_turn)))
                if which == K_:
                    dve.scalar_tensor_tensor(out=kl[:, u % 2, :], in0=src, scalar=bkq[:, K_:K_ + 1],
                                             in1=kh[:, u % 2, :].bitcast(F32), op0=ALU.add, op1=ALU.subtract).then_inc(s_proj_low, 1)
                elif which == Q_:
                    for s in range(2):
                        rows = slice(s * DH, (s + 1) * DH)
                        dve.scalar_tensor_tensor(out=ql[rows, u % 2, s, :], in0=src[rows, :], scalar=bkq[rows, Q_:Q_ + 1],
                                                 in1=qh[rows, u % 2, s, :].bitcast(F32), op0=ALU.add,
                                                 op1=ALU.subtract).then_inc(s_proj_low, 1)
                else:
                    dve.tensor_tensor(vv[:, u % 2, :, :, DH:2 * DH], src.rearrange("p (t s d) -> p t s d", t=QT, s=2),
                                      vv[:, u % 2, :, :, 0:DH].bitcast(F32), ALU.subtract).then_inc(s_proj_low, 1)

            def masked_max(turn, n):
                u = (n // 2) % B
                dve.wait_ge(s_probs_turned, at(turn, s_probs_turned, 3 * (n - NSB + 1)))
                for i in range(QT):
                    bank, col = SB_[i]
                    if i != 1:
                        wait_alone(dve, s_scores, at(turn, s_scores, 3 * n + max(i, 1)), passed)
                    dve.tensor_tensor_reduce(out=sc[:, n % NSB, S_OFF[i]:S_OFF[i] + S_W[i]],
                                             in0=sps[:, bank, col:col + S_W[i]],
                                             in1=madd[:, u, S_OFF[i]:S_OFF[i] + S_W[i]],
                                             scale=1.0, scalar=-3.0e38, op0=ALU.add, op1=ALU.max,
                                             accum_out=mx[:, n % NSB, i:i + 1]).then_inc(s_row_max, 1)

            def negate_max(turn, n):
                dve.wait_ge(s_row_max, at(turn, s_row_max, 4 * n + 4))
                dve.tensor_scalar(nm[:, n % NSB, :], mx[:, n % NSB, :], -SCALE, None, ALU.mult).then_inc(s_neg_max, 1)
                u = (n // 2) % B
                dve.wait_ge(s_lowest, at(turn, s_lowest, n))
                dve.tensor_tensor(lowest[:, u], lowest[:, u], mx[:, n % NSB, :], ALU.min).then_inc(s_lowest, 1)

            def reciprocal(turn, n):
                dve.wait_ge(s_exps, at(turn, s_exps, 4 * n + 4))
                dve.reciprocal(rc[:, n % NSB, :], rs[:, n % NSB, :]).then_inc(s_reciprocal, 1)

            def probs_low(turn, n, m):
                g = 3 * n + m
                dve.wait_ge(s_probs_high, at(turn, s_probs_high, g + 1))
                w, o = sum(T_W[j] for j in T_UNITS[m]), T_OFF[T_UNITS[m][0]]
                dve.tensor_tensor(pl[:, n % 2, o:o + w], tps[:, g % 2, 0:w], ph[:, n % 2, o:o + w].bitcast(F32),
                                  ALU.subtract).then_inc(s_probs_low, 1)

            def z_add(turn, n):
                u, s = n // 2, n % 2
                rows = slice(s * DH, (s + 1) * DH)
                dve.wait_ge(s_z_copied, at(turn, s_z_copied, n + 1))
                dve.tensor_tensor(zz[rows, u % 2, :], zps[DH:P, :], zz[rows, u % 2, :], ALU.add).then_inc(s_z_added, 1)

            def step(turn, k, last_turn):
                if k >= 0:
                    for part in range(3):
                        probs_low(turn, k, part)
                if head(k + 3, last_turn):
                    masked_max(turn, k + 3)
                projections = step_projections(k, last_turn)
                for which, u in projections[:1]:
                    low(turn, which, u, last_turn)
                if head(k + 3, last_turn):
                    negate_max(turn, k + 3)
                for which, u in projections[1:]:
                    low(turn, which, u, last_turn)
                if head(k + 2, last_turn):
                    reciprocal(turn, k + 2)
                if k >= 0:
                    z_add(turn, k)

            schedule(dve, step)


def attention_all_keys(nc, ap, zt, xh, xl, lowest, future):
    ctx = ExitStack()
    with ctx:
        def sb(name, shape, dt=F32):
            return ctx.enter_context(nc.sbuf_tensor(name, shape, dt))

        def sem(name):
            return ctx.enter_context(nc.semaphore(name))

        ident, ones = sb("ident_a", [P, P]), sb("ones_a", [P, P])
        seen, ignore = sb("seen_a", [P, P]), sb("ignore_a", [P, P])
        bias = sb("bias_a", [P, HP, 2])
        near = sb("near", [P, B, QT])
        nears = sb("nears", [P, 1])
        again = sb("again", [P, 1], I32)
        mask = sb("mask_a", [P, S])
        past, later = sb("past", [P, S]), sb("later", [P, S])
        w = sb("w_a", [P, 3, KT, P])
        c = sb("c_a", [P, KT, S])
        kqv = sb("kqv", [P, 3, S])
        v = sb("v_a", [P, QT, P])
        sc = sb("sc_a", [P, S])
        mx, nm, rs, rc = (sb(n, [P, 1]) for n in ("mx_a", "nm_a", "rs_a", "rc_a"))
        pt = sb("pt", [P, QT, P])
        zz = sb("zz_a", [P, S])
        pps = ctx.enter_context(nc.psum_tensor("pps_a", [P, 3, S], F32))
        vps = ctx.enter_context(nc.psum_tensor("vps_a", [P, QT, P], F32))
        sps = ctx.enter_context(nc.psum_tensor("sps_a", [P, S], F32))
        tps = ctx.enter_context(nc.psum_tensor("tps_a", [P, QT, P], F32))
        zps = ctx.enter_context(nc.psum_tensor("zps_a", [P, P], F32))
        nps = ctx.enter_context(nc.psum_tensor("nps_a", [P, 1], F32))

        a_consts, a_tables, a_near, a_count, a_again = (sem(n) for n in (
            "a_consts", "a_tables", "a_near", "a_count", "a_again"))
        a_loaded, a_projected, a_kqv_copied, a_v_turned, a_scores, a_vector_step, a_neg_max, a_exps, a_probs, a_probs_turned, a_probs_copied, a_values, a_z_stored = (sem(n) for n in (
            "a_loaded", "a_projected", "a_kqv_copied", "a_v_turned", "a_scores", "a_vector_step", "a_neg_max", "a_exps", "a_probs", "a_probs_turned", "a_probs_copied", "a_values", "a_z_stored"))
        UNITS = [(s, i) for s in range(2) for i in range(QT)]
        C = {a_loaded: 48, a_projected: 1, a_kqv_copied: 3, a_v_turned: 1, a_scores: 8, a_vector_step: 63, a_neg_max: 8, a_exps: 8, a_probs: 8, a_probs_turned: 8, a_probs_copied: 8,
             a_values: 8, a_z_stored: 16}

        block = ctx.enter_context(nc.Block())

        def loops(eng, turn):
            eng.wait_ge(a_again, 1)
            n = eng.value_load(again[0:1, 0:1], min_val=0, max_val=1)
            with eng.If(n > 0):
                with eng.Fori(0, HP) as hp:
                    with eng.Fori(0, B) as b:
                        turn(hp, b, lambda s, k: hp * (B * C[s]) + b * C[s] + (C[s] + k))

        @block.sync
        def _(sp):
            sp.dma_start(ident[:], ap["ident"]).then_inc(a_consts, 16)
            sp.dma_start(bias[:], ap["bkq"]).then_inc(a_consts, 16)

            def turn(hp, b, at):
                sp.wait_ge(a_z_stored, at(a_z_stored, 0))
                sp.dma_start(w[:], ap["wkqv"][hp]).then_inc(a_loaded, 16)
                sp.dma_start(mask[:], ap["mask"][b]).then_inc(a_loaded, 16)
                sp.dma_start(c[:], ap["ctx_t"].rearrange("p k (b n) -> b p k n", b=B)[b]).then_inc(a_loaded, 16)
                sp.wait_ge(a_values, at(a_values, 8))
                sp.wait_ge(a_vector_step, at(a_vector_step, C[a_vector_step]))
                sp.dma_start(zt.rearrange("h p (b n) -> h b p n", b=B)[hp, b], zz[:]).then_inc(a_z_stored, 16)
            loops(sp, turn)

        @block.gpsimd
        def _(pool):
            for s, n in C.items():
                pool.sem_inc(s, n)
            pool.memset(seen[:], 1.0).then_inc(a_tables, 1)
            pool.memset(ignore[:], 0.0).then_inc(a_tables, 1)
            pool.wait_ge(a_tables, 2)
            pool.affine_select(out=seen[:], in_=seen[:], compare_op=ALU.is_ge, fill=0.0, base=0,
                               pattern=[[-1, P]], channel_multiplier=1).then_inc(a_tables, 1)
            pool.affine_select(out=ignore[:], in_=ignore[:], compare_op=ALU.is_ge, fill=W8 * IGNORE, base=0,
                               pattern=[[-1, P]], channel_multiplier=1).then_inc(a_tables, 1)

        @block.tensor
        def _(pe):
            pe.wait_ge(a_near, 3)
            pe.matmul(nps[:], ones[:], nears[:], start=True, stop=True).then_inc(a_count, 1)
            pe.wait_ge(a_consts, 32)

            def turn(hp, b, at):
                pe.wait_ge(a_loaded, at(a_loaded, 48))
                for which, parts in ((0, (c,)), (1, (xh, xl)), (2, (c,))):
                    terms = [(kt, v_) for kt in range(KT) for v_ in parts]
                    for g, (kt, v_) in enumerate(terms):
                        rhs = v_[:, kt, :] if v_ is c else \
                            v_[:].bitcast(F32).rearrange("p k (b n) -> p k b n", b=B)[:, kt, b]
                        last = pe.matmul(pps[:, which, :], w[:, which, kt, :], rhs, start=(g == 0), stop=(g == len(terms) - 1))
                last.then_inc(a_projected, 1)
                pe.wait_ge(a_kqv_copied, at(a_kqv_copied, 3))
                for t in range(QT):
                    last = pe.transpose(vps[:, t, :], kqv[:, 2, t * P:(t + 1) * P], ident[:])
                last.then_inc(a_v_turned, 1)
                for g, (s, i) in enumerate(UNITS):
                    rows = slice(s * DH, (s + 1) * DH)
                    pe.wait_ge(a_values, at(a_values, g))
                    pe.matmul(sps[:], kqv[rows, 1, i * P:(i + 1) * P], kqv[rows, 0, :], start=True, stop=True).then_inc(a_scores, 1)
                    pe.wait_ge(a_probs, at(a_probs, g + 1))
                    for t in range(QT):
                        last = pe.transpose(tps[:, t, :], sc[:, t * P:(t + 1) * P], ident[:])
                    last.then_inc(a_probs_turned, 1)
                    pe.wait_ge(a_probs_copied, at(a_probs_copied, g + 1))
                    for t in range(QT):
                        last = pe.matmul(zps[:], v[:, t, :], pt[:, t, :], start=(t == 0), stop=(t == QT - 1))
                    last.then_inc(a_values, 1)
            loops(pe, turn)

        @block.scalar
        def _(act):
            def turn(hp, b, at):
                for g in range(len(UNITS)):
                    act.wait_ge(a_neg_max, at(a_neg_max, g + 1))
                    act.activation(sc[:], sc[:], ACT.Exp, bias=nm[:], scale=SCALE, accum_out=rs[:]).then_inc(a_exps, 1)
            loops(act, turn)

        @block.vector
        def _(dve):
            dve.memset(ones[:], 1.0).then_inc(a_near, 1)
            dve.scalar_tensor_tensor(out=near[:], in0=lowest[:], scalar=-W8 * FAR_BELOW, in1=future[:],
                                     op0=ALU.add, op1=ALU.is_lt).then_inc(a_near, 1)
            dve.wait_ge(a_near, 2)
            dve.tensor_reduce(nears[:], near[:].rearrange("p b i -> p (b i)"), AX.X, ALU.add).then_inc(a_near, 1)
            dve.wait_ge(a_count, 1)
            dve.tensor_scalar(nears[:], nps[:], 1.0, None, ALU.min).then_inc(a_near, 1)
            dve.wait_ge(a_near, 4)
            dve.tensor_copy(again[:], nears[:]).then_inc(a_again, 1)
            dve.wait_ge(a_tables, 4)
            dve.wait_ge(a_consts, 32)

            def turn(hp, b, at):
                done = [0]

                def link(ins):
                    done[0] += 1
                    ins.then_inc(a_vector_step, 1)
                    dve.wait_ge(a_vector_step, at(a_vector_step, done[0]))

                dve.wait_ge(a_loaded, at(a_loaded, 48))
                dve.wait_ge(a_z_stored, at(a_z_stored, 0))
                link(dve.tensor_scalar(past[:], mask[:], W8, None, ALU.mult))
                link(dve.tensor_scalar(later[:], mask[:], IGNORE, W8, ALU.add, ALU.mult))
                dve.wait_ge(a_projected, at(a_projected, 1))
                for which in (0, 1):
                    dve.tensor_scalar(kqv[:, which, :], pps[:, which, :], bias[:, bass.ds(hp, 1), which], None, ALU.add).then_inc(a_kqv_copied, 1)
                dve.tensor_copy(kqv[:, 2, :], pps[:, 2, :]).then_inc(a_kqv_copied, 1)
                dve.wait_ge(a_v_turned, at(a_v_turned, 1))
                link(dve.tensor_copy(v[:], vps[:]))
                for g, (s, i) in enumerate(UNITS):
                    diag = slice(i * P, (i + 1) * P)
                    dve.wait_ge(a_scores, at(a_scores, g + 1))
                    if i:
                        link(dve.tensor_tensor(sc[:, 0:i * P], sps[:, 0:i * P], past[:, 0:i * P], ALU.add))
                    link(dve.tensor_tensor(sc[:, diag], sps[:, diag], seen[:], ALU.mult))
                    link(dve.tensor_tensor(sc[:, diag], sc[:, diag], ignore[:], ALU.add))
                    link(dve.tensor_tensor(sc[:, diag], sc[:, diag], past[:, diag], ALU.add))
                    if i < QT - 1:
                        link(dve.tensor_copy(sc[:, (i + 1) * P:], later[:, (i + 1) * P:]))
                    link(dve.tensor_reduce(mx[:], sc[:], AX.X, ALU.max))
                    dve.tensor_scalar(nm[:], mx[:], -SCALE, None, ALU.mult).then_inc(a_neg_max, 1)
                    dve.wait_ge(a_exps, at(a_exps, g + 1))
                    link(dve.reciprocal(rc[:], rs[:]))
                    dve.tensor_scalar(sc[:], sc[:], rc[:], None, ALU.mult).then_inc(a_probs, 1)
                    dve.wait_ge(a_probs_turned, at(a_probs_turned, g + 1))
                    dve.tensor_copy(pt[:], tps[:]).then_inc(a_probs_copied, 1)
                    dve.wait_ge(a_values, at(a_values, g + 1))
                    link(dve.tensor_copy(zz[s * DH:(s + 1) * DH, diag], zps[s * DH:(s + 1) * DH, :]))
                assert done[0] == C[a_vector_step], done
            loops(dve, turn)


NB = NT + NE - 1
NA = NT + NB
NS = NT // 2


def feed_forward(nc, ap, zt, rows_in, rows_out, out):
    with ExitStack() as ctx:
        def sb(name, shape, dt=F32):
            return ctx.enter_context(nc.sbuf_tensor(name, shape, dt))

        keep = {
            "x2": sb("x2", [P, NT, D]),
            "h": sb("h", [P, NT, D]),
            "slot": sb("slot", [P, NT], U32),
            "prob": sb("prob", [P, NT]),
            "expert": sb("expert", [P, NA], I32),
            "six": sb("six", [P, NA - 5], I32),
            "ident": sb("ident2", [P, P]),
            "t1": sb("t1", [P, NE + 1, KT, F], F32R),
            "t2": sb("t2", [P, NE + 1, FT, D], F32R),
            "s1": sb("s1", [P, NE + 1, F]),
            "s2": sb("s2", [P, NE + 1, D]),
        }
        route(nc, ap, zt, rows_in, **keep)
        run_experts(nc, rows_in, rows_out, out, **keep)


def route(nc, ap, zt, rows_in, x2, h, slot, prob, expert, six, ident, t1, t2, s1, s2):
    ctx = ExitStack()
    with ctx:
        def sb(name, shape, dt=F32):
            return ctx.enter_context(nc.sbuf_tensor(name, shape, dt))

        def sem(name):
            return ctx.enter_context(nc.semaphore(name))

        wo = sb("wo", [P, HP, D])
        rows = sb("rows", [P, 3, D])
        wr = sb("wr", [P, KT, NE])
        bv = sb("bv", [P, HP])
        zs = sb("zs", [P, 2, HP, P])
        hx = sb("hx", [P, QT, D])
        hs = sb("hs", [P, KT, S])
        bvw = hs[:].rearrange("p k (g n) -> p (k g) n", n=P)
        ww = sb("ww", [P, 3, KT * F + FT * D])
        wa = sb("wa", [P, KT * F + FT * D])
        wsum = sb("wsum", [P, 3, F + D])
        stats = sb("stats2", [P, QT, 6])
        mv = sb("mv2", [P, QT, 2])
        ve = sb("ve2", [P, QT])
        rstd = sb("rstd2", [P, QT])
        neg_half = sb("neg_half2", [P, QT])
        numbers = sb("numbers", [P, NA])
        before = sb("before", [P, P])
        ones = sb("ones", [P, P])
        row0 = sb("row0", [P, P])
        small = sb("small", [P, 4, QT, NE])
        tiny = sb("tiny", [P, 5, QT])
        hot = sb("hot", [P, NT, NE])
        count = sb("count", [P, 2, NT, NE])
        filled = sb("filled", [P, NE, NT])
        ends = sb("ends", [P, 2, NE])
        first = sb("first", [P, NE])
        pos = sb("pos", [P, NT, NE])
        fslot = sb("fslot", [P, NT])
        ended = sb("ended", [P, NB, NE])
        ends_before = sb("ends_before", [P, NB])
        fexp = sb("fexp", [P, NA])
        two = sb("two", [P, NA - 1])
        rest = sb("rest", [P, NA - 5])
        zero = sb("zero", [P, D])
        NO = 3
        ops = ctx.enter_context(nc.psum_tensor("ops", [P, NO, 512], F32))
        hps = ctx.enter_context(nc.psum_tensor("hps", [P, 2, 512], F32))
        wps = ctx.enter_context(nc.psum_tensor("wps", [P, 2, 512], F32))
        last_ps = ctx.enter_context(nc.psum_tensor("last_ps", [P, 512], F32))
        rps = last_ps[:, 0:QT * NE].rearrange("p (t e) -> p t e", t=QT)
        cps = last_ps[:, 256:512].rearrange("p (a t e) -> p a t e", a=2, t=NT)

        r_consts, r_tables, r_x_first, r_bias_vec, r_bias_product, passed, r_zero_filled = (sem(n) for n in (
            "r_consts", "r_tables", "r_x_first", "r_bias_vec", "r_bias_product", "r_passed", "r_zero_filled"))
        r_ident_wr, r_x_rest = sem("r_ident_wr"), sem("r_x_rest")
        r_heads_loaded = [sem("r_heads_loaded0"), sem("r_heads_loaded1")]
        r_weights_loaded = [sem(f"r_weights_loaded{k}") for k in range(3)]
        r_sizes, r_size_parts, r_size_sums, r_scales, r_compared, r_ternary1, r_ternary2 = (sem(n) for n in (
            "r_sizes", "r_size_parts", "r_size_sums", "r_scales", "r_compared", "r_ternary1", "r_ternary2"))
        r_projected, r_residual, r_moments, r_softmax_step, r_variance, r_rstd, r_normalised, r_gamma_done, r_rows_ready, r_rows_turned, r_turned_copied, r_logits, r_less_max, r_exps = (sem(n) for n in (
            "r_projected", "r_residual", "r_moments", "r_softmax_step", "r_variance", "r_rstd", "r_normalised", "r_gamma_done", "r_rows_ready", "r_rows_turned", "r_turned_copied", "r_logits", "r_less_max", "r_exps"))
        r_choice, r_counted, r_place_step, r_rows_stored, r_rows_kept = sem("r_choice"), sem("r_counted"), sem("r_place_step"), sem("r_rows_stored"), sem("r_rows_kept")
        NNORM, NSOFT = 2 * QT, 8
        C = {r_heads_loaded[0]: 32, r_heads_loaded[1]: 32, r_projected: QT, r_residual: QT, r_moments: NNORM, r_softmax_step: NSOFT, r_variance: 1, r_rstd: 1, r_normalised: 1, r_gamma_done: 1,
             r_rows_ready: 1, r_rows_turned: 1, r_turned_copied: 1, r_rows_kept: 1, r_logits: 1, r_less_max: 1, r_exps: 1,
             r_sizes: 3, r_size_parts: 12, r_size_sums: 3, r_scales: 6, r_compared: 12, r_ternary1: 3, r_ternary2: 3}
        WK = 3
        TURNS = (NE + 1) // WK
        assert TURNS * WK == NE + 1 and TURNS == B - 1
        W1 = KT * F

        def at(turn, s, k):
            return turn * C[s] + (C[s] + k)

        def bank(t):
            return t % NO

        def turns(eng, turn):
            with eng.Fori(0, TURNS - 1) as b:
                turn(b, True)
            turn(TURNS - 1, False)

        block = ctx.enter_context(nc.Block())

        @block.sync
        def _(sp):
            for d, s in ((wo, "wo"), (bv, "bv"), (rows, "rows")):
                sp.dma_start(d[:], ap[s]).then_inc(r_consts, 16)

            def heads_out(b, tiles=range(QT)):
                zv = zt.rearrange("h p (b t q) -> b t p h q", b=B, q=P)
                for t in tiles:
                    sp.wait_ge(r_projected, at(b, r_projected, t - 1))
                    sp.dma_start(zs[:, t % 2], zv[b, t]).then_inc(r_heads_loaded[t % 2], 16)

            def turn(b, more):
                heads_out(b + 1)

            xv = ap["x"].rearrange("(t p) d -> p t d", p=P)
            heads_out(0, (0, 1))
            sp.dma_start(x2[:, 0:QT], xv[:, 0:QT]).then_inc(r_x_first, 16)
            for d, s in ((ident, "ident"), (wr, "wr")):
                sp.dma_start(d[:], ap[s]).then_inc(r_ident_wr, 16)
            heads_out(0, (2, 3))
            sp.dma_start(x2[:, QT:], xv[:, QT:]).then_inc(r_x_rest, 16)
            turns(sp, turn)
            sp.wait_ge(r_tables, 1)
            sp.dma_start(rows_in[NS * P:(NS + NB) * P].rearrange("(n p) d -> p n d", p=P),
                         zero[:].rearrange("p (o d) -> p o d", o=1).to_broadcast([P, NB, D])).then_inc(r_zero_filled, 16)
            sp.wait_ge(r_zero_filled, 16)

        @block.gpsimd
        def _(pool):
            for s, c in C.items():
                pool.sem_inc(s, c)
            pool.memset(zero[:], 0.0).then_inc(r_tables, 1)
            pool.memset(neg_half[:], -0.5).then_inc(r_tables, 1)
            pool.memset(ones[:], 1.0).then_inc(r_tables, 1)
            pool.memset(row0[:], 0.0).then_inc(r_tables, 1)
            pool.wait_ge(r_tables, 4)
            pool.memset(row0[0:1, :], 1.0).then_inc(r_tables, 1)
            pool.iota(numbers[:], pattern=[[1, NA]], base=0, channel_multiplier=0,
                      allow_small_or_imprecise_dtypes=True).then_inc(r_tables, 1)
            pool.affine_select(out=before[:], in_=ones[:], compare_op=ALU.is_gt, fill=0.0, base=0,
                               pattern=[[1, P]], channel_multiplier=-1).then_inc(r_tables, 1)
            pool.wait_ge(r_consts, 48)

            def power(b):
                pool.wait_ge(r_variance, at(b, r_variance, 1))
                pool.tensor_tensor(rstd[:], ve[:], neg_half[:], ALU.pow).then_inc(r_rstd, 1)

            def scale_shift(b):
                hb = h[:].rearrange("p (b t) d -> p b t d", b=B)[:, b]
                wait_alone(pool, r_normalised, at(b, r_normalised, 1), passed)
                pool.tensor_tensor(hb, hb, rows[:, 1:2, :].to_broadcast([P, QT, D]), ALU.mult).then_inc(r_gamma_done, 1)
                pool.wait_ge(r_rows_kept, at(b, r_rows_kept, 0))
                wait_alone(pool, r_gamma_done, at(b, r_gamma_done, 1), passed)
                pool.tensor_tensor(hx[:], hb, rows[:, 2:3, :].to_broadcast([P, QT, D]), ALU.add).then_inc(r_rows_ready, 1)

            def size_sums(b, k):
                a1 = wa[:, 0:W1].rearrange("p (t n) -> p t n", t=KT)
                a2 = wa[:, W1:].rearrange("p (t n) -> p t n", t=FT)
                pool.wait_ge(r_size_sums, at(b, r_size_sums, k - 2))
                wait_alone(pool, r_sizes, at(b, r_sizes, k + 1), passed)
                pool.tensor_tensor(wsum[:, k, 0:F], a1[:, 0], a1[:, 1], ALU.add).then_inc(r_size_parts, 1)
                pool.tensor_tensor(wsum[:, k, F:], a2[:, 0], a2[:, 1], ALU.add).then_inc(r_size_parts, 1)
                for j in range(2, FT):
                    wait_alone(pool, r_size_parts, at(b, r_size_parts, 4 * k + j), passed)
                    pool.tensor_tensor(wsum[:, k, F:], wsum[:, k, F:], a2[:, j], ALU.add).then_inc(r_size_parts, 1)

            def less(b, k):
                wait_alone(pool, r_compared, at(b, r_compared, 4 * k + 4), passed)
                e = bass.ds(b * WK + k, 1)
                pool.tensor_tensor(t2[:, e].rearrange("p o t n -> p (o t n)"), t2[:, e].bitcast(F32).rearrange("p o t n -> p (o t n)"),
                                   ww[:, k, W1:], ALU.subtract).then_inc(r_ternary2, 1)

            def load(b, k):
                wait_alone(pool, r_ternary1, at(b, r_ternary1, k - 2), passed)
                wait_alone(pool, r_ternary2, at(b, r_ternary2, k - 2), passed)
                pool.dma_start(ww[:, k], ap["w"][b * WK + k]).then_inc(r_weights_loaded[k], 16)

            def turn(b, more):
                size_sums(b, 2)
                for k in range(2):
                    less(b, k)
                    if more:
                        load(b + 1, k)
                if more:
                    size_sums(b + 1, 0)
                power(b + 1)
                scale_shift(b + 1)
                less(b, 2)
                if more:
                    load(b + 1, 2)
                    size_sums(b + 1, 1)

            for k in range(WK):
                pool.dma_start(ww[:, k], ap["w"][k]).then_inc(r_weights_loaded[k], 16)
            size_sums(0, 0)
            size_sums(0, 1)
            power(0)
            scale_shift(0)
            turns(pool, turn)

        @block.tensor
        def _(pe):
            pe.wait_ge(r_consts, 48)
            pe.wait_ge(r_bias_vec, 1)
            for g in range(HP):
                last = pe.matmul(wps[:, 1, 0:D], bvw[:, g, :], wo[:, g, :], start=(g == 0), stop=(g == HP - 1))
            last.then_inc(r_bias_product, 1)

            def project(b, tiles=range(QT)):
                for t in tiles:
                    pe.wait_ge(r_heads_loaded[t % 2], at(b, r_heads_loaded[t % 2], 16 * (t // 2 + 1)))
                    pe.wait_ge(r_residual, at(b, r_residual, max(t - NO + 1, 0)))
                    for g in range(HP):
                        pe.matmul(ops[:, bank(t), 0:D], zs[:, t % 2, g, :], wo[:, g, :], start=(g == 0), stop=False)
                    pe.wait_ge(r_bias_vec, 2)
                    last = pe.matmul(ops[:, bank(t), 0:D], row0[:], rows[:, 0, :], start=False, stop=True)
                    last.then_inc(r_projected, 1)

            def sizes(b, k):
                pe.wait_ge(r_scales, at(b, r_scales, 2 * k))
                pe.wait_ge(r_size_parts, at(b, r_size_parts, 4 * k + 4))
                pe.matmul(wps[:, 0, :], ones[:], wsum[:, k, 0:F], start=True, stop=True)
                pe.matmul(wps[:, 1, 0:D], ones[:], wsum[:, k, F:], start=True, stop=True).then_inc(r_size_sums, 1)

            def logits(b):
                pe.wait_ge(r_rows_ready, at(b, r_rows_ready, 1))
                pe.wait_ge(r_turned_copied, at(b, r_turned_copied, 0))
                for kt in range(KT):
                    for t in range(QT):
                        last = pe.transpose(hps[:, kt, t * P:(t + 1) * P], hx[:, t, kt * P:(kt + 1) * P], ident[:])
                last.then_inc(r_rows_turned, 1)
                pe.wait_ge(r_turned_copied, at(b, r_turned_copied, 1))
                pe.wait_ge(r_less_max, at(b, r_less_max, 0))
                for t in range(QT):
                    for kt in range(KT):
                        last = pe.matmul(rps[:, t, :], hs[:, kt, t * P:(t + 1) * P], wr[:, kt, :], start=(kt == 0), stop=(kt == 1))
                last.then_inc(r_logits, 1)

            def turn(b, more):
                sizes(b, 0)
                project(b + 1, (0,))
                sizes(b, 1)
                project(b + 1, (1, 2))
                sizes(b, 2)
                project(b + 1, (3,))
                logits(b)

            pe.wait_ge(r_tables, 5)
            project(0)
            pe.wait_ge(r_ident_wr, 32)
            turns(pe, turn)
            logits(B - 1)
            pe.wait_ge(r_choice, B)
            pe.wait_ge(r_tables, 7)
            pe.matmul(cps[:, 0], before[:], hot[:], start=True, stop=True)
            pe.matmul(cps[:, 1], ones[:], hot[:], start=True, stop=True).then_inc(r_counted, 1)

        @block.scalar
        def _(act):
            def sizes(b, k):
                act.wait_ge(r_weights_loaded[k], b * 16 + 16)
                act.wait_ge(r_size_parts, at(b, r_size_parts, 4 * k))
                act.activation(wa[:], ww[:, k], ACT.Abs).then_inc(r_sizes, 1)

            def router_in(b, loop_half=False):
                act.wait_ge(r_rows_turned, at(b, r_rows_turned, 1))
                act.wait_ge(r_logits, at(b, r_logits, 0))
                act.activation(hs[:], hps[:], ACT.Copy).then_inc(r_turned_copied, 1)
                act.activation(h[:].rearrange("p (b t) d -> p b t d", b=B)[:, b], hx[:], ACT.Copy).then_inc(r_rows_kept, 1)
                wait_alone(act, r_rows_kept, at(b, r_rows_kept, 1), passed)
                at_row = b * S if loop_half else (NB * P + b * S)
                act.dma_start(rows_in[bass.ds(at_row, S)].rearrange("(t p) d -> p t d", p=P),
                              h[:].rearrange("p (b t) d -> p b t d", b=B)[:, b]).then_inc(r_rows_stored, 16)

            def router_exp(b):
                act.wait_ge(r_less_max, at(b, r_less_max, 1))
                act.activation(small[:, 1], small[:, 0], ACT.Exp).then_inc(r_exps, 1)

            def turn(b, more):
                sizes(b, 2)
                if more:
                    sizes(b + 1, 0)
                router_in(b, more)
                router_exp(b)
                if more:
                    sizes(b + 1, 1)

            sizes(0, 0)
            sizes(0, 1)
            turns(act, turn)
            router_in(B - 1)
            router_exp(B - 1)
            act.wait_ge(r_rows_stored, 16 * B)

        @block.vector
        def _(dve):
            dve.wait_ge(r_consts, 48)
            dve.tensor_copy(bvw, bv[:].rearrange("p (h o) -> p h o", o=1).to_broadcast([P, HP, P])).then_inc(r_bias_vec, 1)
            dve.wait_ge(r_bias_product, 1)
            dve.tensor_tensor(rows[:, 0, :], rows[:, 0, :], wps[:, 1, 0:D], ALU.add).then_inc(r_bias_vec, 1)

            def tile(v, b, t):
                return v[:, bass.ds(b * QT + t, 1), :].rearrange("p o d -> p (o d)")

            def residual(b, t):
                dve.wait_ge(r_projected, at(b, r_projected, t + 1))
                dve.tensor_tensor(tile(x2, b, t), ops[:, bank(t), 0:D], tile(x2, b, t), ALU.add).then_inc(r_residual, 1)

            def norms(b):
                wait_alone(dve, r_residual, at(b, r_residual, QT), passed)
                for t in range(QT):
                    dve.bn_stats(stats[:, t, :], tile(x2, b, t)).then_inc(r_moments, 1)
                wait_alone(dve, r_moments, at(b, r_moments, QT), passed)
                for t in range(QT):
                    dve.bn_aggr(mv[:, t, :], stats[:, t, :]).then_inc(r_moments, 1)
                dve.wait_ge(r_moments, at(b, r_moments, 2 * QT))
                dve.tensor_scalar(ve[:], mv[:, :, 1], 1.0 + EPS, EPS * EPS, ALU.mult, ALU.add).then_inc(r_variance, 1)
                dve.wait_ge(r_rstd, at(b, r_rstd, 1))
                for t in range(QT):
                    last = dve.tensor_scalar(tile(h, b, t), tile(x2, b, t), mv[:, t, 0:1], rstd[:, t:t + 1], ALU.subtract, ALU.mult)
                last.then_inc(r_normalised, 1)

            def weights(b, k):
                e = bass.ds(b * WK + k, 1)
                sc1, sc2 = s1[:, e, :].rearrange("p o n -> p (o n)"), s2[:, e, :].rearrange("p o n -> p (o n)")
                dve.wait_ge(r_size_sums, at(b, r_size_sums, k + 1))
                dve.tensor_scalar(sc1, wps[:, 0, :], 1.0 / D, 1e-5, ALU.mult, ALU.max).then_inc(r_scales, 1)
                dve.tensor_scalar(sc2, wps[:, 1, 0:D], 1.0 / F, 1e-5, ALU.mult, ALU.max).then_inc(r_scales, 1)
                wait_alone(dve, r_scales, at(b, r_scales, 2 * k + 2), passed)
                for first, size, tiles, sc, dst in ((0, W1, KT, s1, t1), (W1, FT * D, FT, s2, t2)):
                    wv = ww[:, k, first:first + size].rearrange("p (t n) -> p t n", t=tiles)
                    scb = sc[:, e, :].to_broadcast([P, tiles, size // tiles])
                    dve.scalar_tensor_tensor(out=dst[:, e].rearrange("p o t n -> p (o t) n"), in0=wv, scalar=2.0, in1=scb,
                                             op0=ALU.mult, op1=ALU.is_gt).then_inc(r_compared, 1)
                    dve.scalar_tensor_tensor(out=wv, in0=wv, scalar=-2.0, in1=scb, op0=ALU.mult, op1=ALU.is_gt).then_inc(r_compared, 1)
                dve.wait_ge(r_compared, at(b, r_compared, 4 * k + 4))
                dve.tensor_tensor(t1[:, e].rearrange("p o t n -> p (o t n)"), t1[:, e].bitcast(F32).rearrange("p o t n -> p (o t n)"),
                                  ww[:, k, 0:W1], ALU.subtract).then_inc(r_ternary1, 1)

            def softmax(b):
                done = [0]

                def link(ins):
                    done[0] += 1
                    ins.then_inc(r_softmax_step, 1)
                    dve.wait_ge(r_softmax_step, at(b, r_softmax_step, done[0]))

                def wide(v):
                    return v.rearrange("p (t o) -> p t o", o=1).to_broadcast([P, QT, NE])

                m, e, below, cand = (small[:, n] for n in range(4))
                mx, em, es, ix, pr = (tiny[:, n] for n in range(5))
                iota = numbers[:, 0:NE].rearrange("p (o n) -> p o n", o=1).to_broadcast([P, QT, NE])
                dve.wait_ge(r_logits, at(b, r_logits, 1))
                link(dve.tensor_reduce(mx, rps, AX.X, ALU.max))
                dve.tensor_tensor(m, rps, wide(mx), ALU.subtract).then_inc(r_less_max, 1)
                dve.wait_ge(r_exps, at(b, r_exps, 1))
                link(dve.tensor_reduce(em, e, AX.X, ALU.max))
                link(dve.tensor_reduce(es, e, AX.X, ALU.add))
                link(dve.reciprocal(pr, es))
                link(dve.tensor_tensor(prob[:].rearrange("p (b t) -> p b t", b=B)[:, b], pr, em, ALU.mult))
                link(dve.tensor_tensor(below, e, wide(em), ALU.is_lt))
                link(dve.scalar_tensor_tensor(out=cand, in0=below, scalar=float(NE), in1=iota, op0=ALU.mult, op1=ALU.add))
                link(dve.tensor_reduce(ix, cand, AX.X, ALU.min))
                dve.tensor_tensor(hot[:].rearrange("p (b t) e -> p b t e", b=B)[:, b], iota, wide(ix), ALU.is_equal).then_inc(r_choice, 1)
                assert done[0] == C[r_softmax_step], done

            def turn(b, more):
                weights(b, 0)
                residual(b + 1, 0)
                weights(b, 1)
                residual(b + 1, 1)
                residual(b + 1, 2)
                weights(b, 2)
                residual(b + 1, 3)
                norms(b + 1)
                softmax(b)

            dve.wait_ge(r_x_first, 16)
            for t in range(QT):
                residual(0, t)
            norms(0)
            dve.wait_ge(r_x_rest, 16)
            turns(dve, turn)
            softmax(B - 1)

            dve.wait_ge(r_counted, 1)
            done = [0]

            def link(ins):
                done[0] += 1
                ins.then_inc(r_place_step, 1)
                dve.wait_ge(r_place_step, done[0])

            rank, total = cps[:, 0], cps[:, 1]
            link(dve.tensor_copy(count[:, 0], total))
            src, dst = 0, 1
            for k in (1, 2, 4, 8):
                link(dve.tensor_copy(count[:, dst, 0:k], count[:, src, 0:k]))
                link(dve.tensor_tensor(count[:, dst, k:], count[:, src, k:], count[:, src, 0:NT - k], ALU.add))
                src, dst = dst, src
            counts = count[:, src, NT - 1, :]
            link(dve.scalar_tensor_tensor(out=filled[:], in0=numbers[:, 0:NT].rearrange("p (o n) -> p o n", o=1).to_broadcast([P, NE, NT]),
                                          scalar=float(P), in1=counts.rearrange("p (n o) -> p n o", o=1).to_broadcast([P, NE, NT]),
                                          op0=ALU.mult, op1=ALU.is_lt))
            link(dve.tensor_reduce(first[:], filled[:], AX.X, ALU.add))
            link(dve.tensor_copy(ends[:, 0], first[:]))
            a, z = 0, 1
            for k in (1, 2, 4):
                link(dve.tensor_copy(ends[:, z, 0:k], ends[:, a, 0:k]))
                link(dve.tensor_tensor(ends[:, z, k:], ends[:, a, k:], ends[:, a, 0:NE - k], ALU.add))
                a, z = z, a
            end = ends[:, a].rearrange("p (o n) -> p o n", o=1)
            link(dve.tensor_tensor(first[:], ends[:, a], first[:], ALU.subtract))
            link(dve.tensor_tensor(pos[:], count[:, src], total, ALU.subtract))
            link(dve.tensor_tensor(pos[:], pos[:], rank, ALU.add))
            link(dve.scalar_tensor_tensor(out=pos[:], in0=first[:].rearrange("p (o n) -> p o n", o=1).to_broadcast([P, NT, NE]),
                                          scalar=float(P), in1=pos[:], op0=ALU.mult, op1=ALU.add))
            link(dve.tensor_tensor(pos[:], pos[:], hot[:], ALU.mult))
            link(dve.tensor_reduce(fslot[:], pos[:], AX.X, ALU.add))
            link(dve.tensor_scalar(slot[:], fslot[:], float(NS * P), None, ALU.add))
            link(dve.tensor_tensor(ended[:], numbers[:, 0:NB].rearrange("p (n o) -> p n o", o=1).to_broadcast([P, NB, NE]),
                                   end.to_broadcast([P, NB, NE]), ALU.is_ge))
            link(dve.tensor_reduce(ends_before[:], ended[:], AX.X, ALU.add))
            link(dve.tensor_scalar(fexp[:], numbers[:], 0.0, None, ALU.mult))
            link(dve.tensor_scalar(fexp[:, NS:NS + NB], ends_before[:], 1.0, float(NE), ALU.add, ALU.min))
            link(dve.tensor_copy(expert[:], fexp[:]))
            link(dve.scalar_tensor_tensor(out=two[:], in0=fexp[:, 1:], scalar=16.0, in1=fexp[:, 0:NA - 1], op0=ALU.mult, op1=ALU.add))
            link(dve.scalar_tensor_tensor(out=rest[:], in0=two[:, 4:], scalar=256.0, in1=two[:, 2:NA - 3], op0=ALU.mult, op1=ALU.add))
            link(dve.scalar_tensor_tensor(out=six[:], in0=rest[:], scalar=256.0, in1=two[:, 0:NA - 5], op0=ALU.mult, op1=ALU.add))


def run_experts(nc, rows_in, rows_out, out, x2, h, slot, prob, expert, six, ident, t1, t2, s1, s2):
    ctx = ExitStack()
    with ctx:
        def sb(name, shape, dt=F32):
            return ctx.enter_context(nc.sbuf_tensor(name, shape, dt))

        def ps(name):
            return ctx.enter_context(nc.psum_tensor(name, [P, 2, 512], F32))

        def sem(name):
            return ctx.enter_context(nc.semaphore(name))

        hb = sb("hb", [P, 2, D])
        hh, hl = sb("hh", [P, 2, KT, P], F32R), sb("hl", [P, 2, KT, P], F32R)
        zf = sb("zf", [P, 2, F])
        gf = sb("gf", [P, 2, F])
        gh, gl = sb("gh", [P, 2, FT, P], F32R), sb("gl", [P, 2, FT, P], F32R)
        yb = sb("yb", [P, 2, D])
        ysh = sb("ysh", [P, NT, D])
        yrt = sb("yrt", [P, NT, D])
        hps, fps, gps, yps = ps("hps3"), ps("fps"), ps("gps"), ps("yps")

        rows_loaded = [sem("rows_loaded0"), sem("rows_loaded1")]
        result_stored = [sem("result_stored0"), sem("result_stored1")]
        rows_turned, rows_high, rows_low, hidden_summed, hidden_scaled, silu_done, silu_turned, silu_high, silu_low, result_summed, result_scaled = (sem(n) for n in (
            "rows_turned", "rows_high", "rows_low", "hidden_summed", "hidden_scaled", "silu_done", "silu_turned", "silu_high", "silu_low", "result_summed", "result_scaled"))
        shared_fetched = [sem(f"shared_fetched{k}") for k in range(NS + 1)]
        routed_fetched, rows_scattered = [sem("routed_fetched0"), sem("routed_fetched1")], sem("rows_scattered")
        first_half_added, last_half_added, tile_done, out_stored = sem("first_half_added"), sem("last_half_added"), sem("tile_done"), sem("out_stored")
        LAST = [*range(NS, NT), *range(NS)]

        UN = 4
        LEAD = range(-4, NS - 3)
        BODY = (NA - 2 - LEAD.stop) // UN
        assert LEAD.stop + UN * BODY == NA - 2

        def after(eng, s, n):
            j, m = n
            if not isinstance(j, int) or UN * j + m >= 0:
                eng.wait_ge(s, j * UN + (m + 1))

        def after_dma(eng, s, n):
            j, m = n
            if not isinstance(j, int) or UN * j + m >= 0:
                eng.wait_ge(s[m % 2], j * (16 * UN // 2) + 16 * (m // 2 + 1))

        def there(n):
            j, m = n
            return not isinstance(j, int) or 0 <= UN * j + m < NA

        def number(n):
            return n[0] * UN + n[1]

        def schedule(eng, step, with_experts=False):
            def one(n):
                return eng.value_load(expert[0:1, bass.ds(number(n), 1)], min_val=0, max_val=NE)

            def at(m):
                return (lambda k: (0, m + k),) + ((one,) if with_experts else ())
            for m in LEAD:
                step(*at(m))
            with eng.Fori(0, BODY) as j:
                found = ()
                if with_experts:
                    w = eng.value_load(six[0:1, bass.ds(j * UN + LEAD.stop - 1, 1)], min_val=0, max_val=NE * 0x111111)
                    found = (lambda n: ((w >> 4 * (n[1] - LEAD.stop + 1)) & 15).with_bounds(min_val=0, max_val=NE),)
                for m in range(LEAD.stop, LEAD.stop + UN):
                    step(lambda k, m=m: (j, m + k), *found)
            for m in (NA - 2, NA - 1, NA):
                step(*at(m))

        block = ctx.enter_context(nc.Block())

        @block.sync
        def _(sp):
            sh = rows_out.rearrange("(t p) d -> p t d", p=P)

            def store(n):
                after(sp, result_scaled, n)
                sp.dma_start(rows_out.rearrange("(n p) d -> n p d", p=P)[number(n)], yb[:, n[1] % 2]).then_inc(result_stored[n[1] % 2], 16)

            def fetch_first_half():
                for n in (NS - 2, NS - 1):
                    sp.wait_ge(result_stored[n % 2], 16 * (n // 2 + 1))
                sp.dma_start(ysh[:, 0:NS], sh[:, 0:NS]).then_inc(shared_fetched[0], 16)

            def step(i):
                n = i(-2)
                if there(n):
                    store(n)
                n = i(4)
                if there(n):
                    if isinstance(n[0], int) and n[1] == NS:
                        sp.wait_ge(rows_scattered, 16 * NT)
                    after(sp, rows_turned, i(2))
                    sp.dma_start(hb[:, n[1] % 2], rows_in.rearrange("(n p) d -> n p d", p=P)[number(n)]).then_inc(rows_loaded[n[1] % 2], 16)

            for m in LEAD:
                step(lambda k, m=m: (0, m + k))
            with sp.Fori(0, BODY - 1) as j:
                for m in range(LEAD.stop, LEAD.stop + UN):
                    step(lambda k, m=m: (j, m + k))
            fetch_first_half()
            for m in range(LEAD.stop + UN * (BODY - 1), NA + 2):
                step(lambda k, m=m: (0, m + k))

            for t in range(NS, NT):
                n = NB + t
                sp.wait_ge(result_stored[n % 2], 16 * (n // 2 + 1))
                sp.dma_start(ysh[:, t], sh[:, n]).then_inc(shared_fetched[t - NS + 1], 16)
            for n in range(0, NT, 4):
                t = LAST[n]
                sp.wait_ge(tile_done, n + 4)
                sp.dma_start(out.rearrange("(t p) d -> p t d", p=P)[:, t:t + 4], x2[:, t:t + 4, :]).then_inc(out_stored, 16)
            sp.wait_ge(out_stored, 16 * NT // 4)

        @block.gpsimd
        def _(pool):
            for t in range(NT):
                pool.indirect_dma_start(rows_in, bass.IndirectOffsetOnAxis(ap=slot[:, t:t + 1], axis=0), h[:, t, :], None).then_inc(rows_scattered, 16)
            for n in (NS + NB - 2, NS + NB - 1):
                pool.wait_ge(result_stored[n % 2], 16 * (n // 2 + 1))
            for t in range(NT):
                pool.indirect_dma_start(yrt[:, t, :], None, rows_out[0:(NS + NB) * P], bass.IndirectOffsetOnAxis(ap=slot[:, t:t + 1], axis=0)).then_inc(routed_fetched[t // NS], 16)
            pool.wait_ge(shared_fetched[0], 16)
            pool.tensor_tensor(x2[:, 0:NS], x2[:, 0:NS], ysh[:, 0:NS], ALU.add).then_inc(first_half_added, 1)
        @block.tensor
        def _(pe):
            def step(i, block_expert):
                n = i(2)
                if there(n):
                    k = n[1] % 2
                    after_dma(pe, rows_loaded, n)
                    after(pe, rows_low, i(0))
                    for kt in range(KT):
                        last = pe.transpose(hps[:, k, kt * P:(kt + 1) * P], hb[:, k, kt * P:(kt + 1) * P], ident[:])
                    last.then_inc(rows_turned, 1)
                n = i(1)
                if there(n):
                    k = n[1] % 2
                    e = block_expert(n)
                    after(pe, rows_low, n)
                    after(pe, hidden_scaled, i(-1))
                    parts = [(v, kt) for kt in range(KT) for v in (hh, hl)]
                    for v, kt in parts:
                        last = pe.matmul(fps[:, k, :], v[:, k, kt, :], t1[:, bass.ds(e, 1), kt, :].rearrange("p o n -> p (o n)"),
                                         start=((v, kt) == parts[0]), stop=((v, kt) == parts[-1]))
                    last.then_inc(hidden_summed, 1)
                n = i(0)
                if there(n):
                    k = n[1] % 2
                    after(pe, silu_done, n)
                    after(pe, silu_low, i(-2))
                    for j in range(FT):
                        last = pe.transpose(gps[:, k, j * P:(j + 1) * P], gf[:, k, j * P:(j + 1) * P], ident[:])
                    last.then_inc(silu_turned, 1)
                n = i(-1)
                if there(n):
                    k = n[1] % 2
                    e = block_expert(n)
                    after(pe, silu_low, n)
                    after(pe, result_scaled, i(-3))
                    parts = [(v, j) for j in range(FT) for v in (gh, gl)]
                    for v, j in parts:
                        last = pe.matmul(yps[:, k, 0:D], v[:, k, j, :], t2[:, bass.ds(e, 1), j, :].rearrange("p o n -> p (o n)"),
                                         start=((v, j) == parts[0]), stop=((v, j) == parts[-1]))
                    last.then_inc(result_summed, 1)
            schedule(pe, step, True)

        @block.scalar
        def _(act):
            def step(i):
                n = i(2)
                if there(n):
                    k = n[1] % 2
                    after(act, rows_turned, n)
                    after(act, hidden_summed, i(0))
                    act.activation(hh[:, k].rearrange("p t n -> p (t n)"), hps[:, k, 0:D], ACT.Copy).then_inc(rows_high, 1)
                n = i(0)
                if there(n):
                    k = n[1] % 2
                    after(act, silu_turned, n)
                    after(act, result_summed, i(-2))
                    act.activation(gh[:, k].rearrange("p t n -> p (t n)"), gps[:, k, :], ACT.Copy).then_inc(silu_high, 1)
                n = i(1)
                if there(n):
                    k = n[1] % 2
                    after(act, hidden_scaled, n)
                    after(act, silu_turned, i(-1))
                    act.activation(gf[:, k], zf[:, k], ACT.Silu).then_inc(silu_done, 1)
            schedule(act, step)

        @block.vector
        def _(dve):
            def step(i, block_expert):
                n = i(2)
                if there(n):
                    k = n[1] % 2
                    after(dve, rows_high, n)
                    dve.tensor_tensor(hl[:, k].rearrange("p t n -> p (t n)"), hps[:, k, 0:D],
                                      hh[:, k].bitcast(F32).rearrange("p t n -> p (t n)"), ALU.subtract).then_inc(rows_low, 1)
                n = i(1)
                if there(n):
                    k = n[1] % 2
                    e = block_expert(n)
                    after(dve, hidden_summed, n)
                    after(dve, silu_done, i(-1))
                    dve.tensor_tensor(zf[:, k], fps[:, k, :], s1[:, bass.ds(e, 1), :].rearrange("p o n -> p (o n)"), ALU.mult).then_inc(hidden_scaled, 1)
                n = i(0)
                if there(n):
                    k = n[1] % 2
                    after(dve, silu_high, n)
                    dve.tensor_tensor(gl[:, k].rearrange("p t n -> p (t n)"), gps[:, k, :],
                                      gh[:, k].bitcast(F32).rearrange("p t n -> p (t n)"), ALU.subtract).then_inc(silu_low, 1)
                n = i(-1)
                if there(n):
                    k = n[1] % 2
                    e = block_expert(n)
                    after(dve, result_summed, n)
                    after_dma(dve, result_stored, i(-3))
                    dve.tensor_tensor(yb[:, k], yps[:, k, 0:D], s2[:, bass.ds(e, 1), :].rearrange("p o n -> p (o n)"), ALU.mult).then_inc(result_scaled, 1)
            schedule(dve, step, True)
            for t in range(NS, NT):
                dve.wait_ge(shared_fetched[t - NS + 1], 16)
                dve.tensor_tensor(x2[:, t, :], x2[:, t, :], ysh[:, t], ALU.add).then_inc(last_half_added, 1)
            for t in LAST:
                if t == NS:
                    dve.wait_ge(last_half_added, NS)
                    dve.wait_ge(routed_fetched[1], 16 * NS)
                if t == 0:
                    dve.wait_ge(first_half_added, 1)
                    dve.wait_ge(routed_fetched[0], 16 * NS)
                dve.scalar_tensor_tensor(out=x2[:, t, :], in0=yrt[:, t], scalar=prob[:, t:t + 1], in1=x2[:, t, :],
                                         op0=ALU.mult, op1=ALU.add).then_inc(tile_done, 1)


def kernel(**inputs):
    import numpy as _np
    import concourse.bacc as _bacc
    from concourse import mybir as _mybir
    from concourse.bass_utils import run_bass_kernel_spmd as _run

    a = {k: _np.asarray(v) for k, v in inputs.items()}
    c = _np.ascontiguousarray
    wkqv = _np.stack([a[f"L0_xattn_W_{n}"] for n in "KQV"])
    wkqv = wkqv.reshape(3, HP, 2, KT, P, DH).transpose(1, 4, 0, 3, 2, 5)
    bkq = _np.stack([a[f"L0_xattn_b_{n}"] for n in "KQ"]).reshape(2, HP, P).transpose(2, 1, 0)
    ffn = "L0_ffn_"
    w1 = _np.concatenate([a[ffn + "shared_w1"][None], a[ffn + "expert_w1"]]).reshape(NE + 1, F, KT, P).transpose(0, 3, 2, 1)
    w2 = _np.concatenate([a[ffn + "shared_w2"][None], a[ffn + "expert_w2"]]).reshape(NE + 1, D, FT, P).transpose(0, 3, 2, 1)
    arrays = {
        "x": c(a["x"].reshape(T, D)),
        "ctx_t": c(a["ctx_1024"].reshape(T, KT, P).transpose(2, 1, 0)),
        "mask": c(_np.broadcast_to(a["mask_Bx1x1xS2_ff0"].reshape(B, 1, S), (B, P, S))),
        "wkqv": c(wkqv.reshape(HP, P, 3, KT, P)),
        "bkq": c(bkq),
        "bv": c(a["L0_xattn_b_V"].reshape(HP, P).T),
        "ident": _np.eye(P, dtype=_np.float32),
        "wo": c(a["L0_xattn_W_O"].reshape(HP, P, D).transpose(1, 0, 2)),
        "rows": c(_np.broadcast_to(_np.stack([a["L0_xattn_b_O"], a[ffn + "ln_gamma"], a[ffn + "ln_beta"]]), (P, 3, D))),
        "w": c(_np.concatenate([w1.reshape(NE + 1, P, KT * F), w2.reshape(NE + 1, P, FT * D)], axis=2)),
        "wr": c(a[ffn + "router_w"].reshape(NE, KT, P).transpose(2, 1, 0)),
    }
    nc = _bacc.Bacc("TRN2", target_bir_lowering=False, num_devices=1)
    ap = {n: nc.dram_tensor(f"in_{n}", v.shape, _mybir.dt.from_np(v.dtype), kind="ExternalInput").ap() for n, v in arrays.items()}
    out = nc.dram_tensor("out", (T, D), _mybir.dt.float32, kind="ExternalOutput").ap()
    zt = nc.dram_tensor("zt", (HP, P, T), _mybir.dt.float32, kind="Internal").ap()
    attention(nc, ap, zt)
    rows_in, rows_out = (nc.dram_tensor(n, (NA * P, D), _mybir.dt.float32, kind="Internal").ap() for n in ("rows_in", "rows_out"))
    feed_forward(nc, ap, zt, rows_in, rows_out, out)
    r = _run(nc, [{f"in_{n}": v for n, v in arrays.items()}], core_ids=[0])
    return _np.asarray(r.results[0]["out"]).reshape(B, S, D)
```
